# Optimizing a Trainium2 kernel written in Bass

```python
import numpy as np
import jax
import jax.numpy as jnp

def _softmax(x, axis=-1):
    return jax.nn.softmax(x, axis=axis)

def _gelu(x):
    return jax.nn.gelu(x, approximate=True)

def _silu(x):
    return jax.nn.silu(x)

def _sigmoid(x):
    return jax.nn.sigmoid(x)

def _layernorm(x, axis=-1, eps=1e-05):
    m = jnp.mean(x, axis=axis, keepdims=True)
    v = jnp.var(x, axis=axis, keepdims=True)
    return (x - m) / jnp.sqrt(v + eps)

def _scatter_add(tgt, idx, src, axis=0):
    return tgt.at[idx].add(src)

def _segment_sum(src, seg, n):
    return jax.ops.segment_sum(src, seg, n)
kernel_name = 'mk_gnn_resnorm_d4_gnn_r64_6ae64e'

def setup_inputs(seed: int=0):
    np.random.seed(seed)
    _w = jnp.asarray

    def _rec_inputs():
        import jax
        import jax.numpy as jnp
        _gk = jax.random.key(seed)
        x = -0.0005121 + 1.001 * jax.random.normal(jax.random.fold_in(_gk, 1), (50000, 64), jnp.float32)
        src = jax.random.randint(jax.random.fold_in(_gk, 2), (25000,), 0, 50000, jnp.int32)
        dst = jax.random.randint(jax.random.fold_in(_gk, 3), (25000,), 0, 50000, jnp.int32)
        _o = jnp.argsort(dst, stable=True)
        src = src[_o]
        dst = dst[_o]
        edge_attr_2 = jax.random.uniform(jax.random.fold_in(_gk, 13), (25000, 2), jnp.float32, 0.0, 1)
        edge_attr_8 = -0.00019784 + 0.999804 * jax.random.normal(jax.random.fold_in(_gk, 14), (25000, 8), jnp.float32)
        edge_type_500 = jax.random.randint(jax.random.fold_in(_gk, 16), (25000,), 0, 500, jnp.int32)
        return (x, src, dst, edge_attr_2, edge_attr_8, edge_type_500)
    x, src, dst, edge_attr_2, edge_attr_8, edge_type_500 = _rec_inputs()

    def _L0_gnn_setup():
        import jax, jax.numpy as jnp
        import numpy as np
        K = 5

        def spline_conv(x, edge_index, pseudo, W, root, bias):
            N = x.shape[0]
            src, dst = (edge_index[0], edge_index[1])
            xk = jnp.einsum('ni,kio->nko', x, W)
            v = pseudo * (K - 1)
            bot = jnp.floor(v)
            frac = v - bot
            bot = bot.astype(jnp.int32)
            msg = jnp.zeros((src.shape[0], W.shape[2]), dtype=x.dtype)
            for s0 in (0, 1):
                for s1 in (0, 1):
                    b0 = frac[:, 0] if s0 else 1.0 - frac[:, 0]
                    b1 = frac[:, 1] if s1 else 1.0 - frac[:, 1]
                    basis = b0 * b1
                    idx = jnp.clip(bot[:, 0] + s0, 0, K - 1) + K * jnp.clip(bot[:, 1] + s1, 0, K - 1)
                    msg = msg + basis[:, None] * xk[src, idx]
            agg = jax.ops.segment_max(msg, dst, num_segments=N)
            agg = jnp.where(jnp.isfinite(agg), agg, jnp.zeros_like(agg))
            return agg + x @ root + bias
        key = jax.random.key(seed)
        ks = jax.random.split(key, 8)
        N, E, C = (50000, 25000, 64)
        Cin = C
        s = 1.0 / np.sqrt(25 * Cin)
        return {'x': jax.random.normal(ks[0], (N, C), dtype=jnp.float32), 'edge_index': jax.random.randint(ks[1], (2, E), 0, N, dtype=jnp.int32), 'edge_attr': jax.random.uniform(ks[2], (E, 2), dtype=jnp.float32), 'W1': jax.random.normal(ks[3], (25, C, C), dtype=jnp.float32) * s, 'root1': jax.random.normal(ks[4], (C, C), dtype=jnp.float32) / np.sqrt(C), 'bias1': jnp.zeros((C,), dtype=jnp.float32), 'W2': jax.random.normal(ks[5], (25, C, C), dtype=jnp.float32) * s, 'root2': jax.random.normal(ks[6], (C, C), dtype=jnp.float32) / np.sqrt(C), 'bias2': jnp.zeros((C,), dtype=jnp.float32)}
    _L0_gnn_all = _L0_gnn_setup()
    _L0_gnn_in = {k: v for k, v in _L0_gnn_all.items() if k in ('W1', 'root1', 'bias1', 'W2', 'root2', 'bias2')}
    del _L0_gnn_all

    def _L1_gnn_setup():
        import jax, jax.numpy as jnp
        import numpy as np
        N_ENT, N_REL, N_EDGE = (50000, 500, 500000)
        L_LAYERS, HEADS, DIM = (2, 2, 64)
        POW_ITER, ALPHA, LN_EPS = (3, 0.15, 1e-05)

        def _layernorm(x, g, b):
            mu = jnp.mean(x, axis=-1, keepdims=True)
            var = jnp.mean(jnp.square(x - mu), axis=-1, keepdims=True)
            return (x - mu) * jax.lax.rsqrt(var + LN_EPS) * g + b

        def _node_scores(h, W, att):
            t = jnp.tanh((h @ W).reshape(h.shape[0], HEADS, DIM))
            return jnp.einsum('mhd,hd->mh', t, att)

        def _segment_softmax(scores, seg, num_segments):
            m = jax.ops.segment_max(scores, seg, num_segments=num_segments)
            e = jnp.exp(scores - m[seg])
            z = jax.ops.segment_sum(e, seg, num_segments=num_segments)
            return e / z[seg]
        key = jax.random.key(seed)
        ks = jax.random.split(key, 13)
        s = 1.0 / np.sqrt(DIM)
        return {'entity_embed': jax.random.normal(ks[0], (N_ENT, DIM), jnp.float32) * 0.05, 'relation_embed': jax.random.normal(ks[1], (N_REL, DIM), jnp.float32) * 0.05, 'edge_index': jax.random.randint(ks[2], (2, N_EDGE), 0, N_ENT, jnp.int32), 'edge_type': jax.random.randint(ks[3], (N_EDGE,), 0, N_REL, jnp.int32), 'ln_gamma': jnp.ones((L_LAYERS, DIM), jnp.float32), 'ln_beta': jnp.zeros((L_LAYERS, DIM), jnp.float32), 'W_h': jax.random.normal(ks[4], (L_LAYERS, DIM, HEADS * DIM), jnp.float32) * s, 'W_t': jax.random.normal(ks[5], (L_LAYERS, DIM, HEADS * DIM), jnp.float32) * s, 'W_r': jax.random.normal(ks[6], (L_LAYERS, DIM, HEADS * DIM), jnp.float32) * s, 'att_h': jax.random.normal(ks[7], (L_LAYERS, HEADS, DIM), jnp.float32) * s, 'att_t': jax.random.normal(ks[8], (L_LAYERS, HEADS, DIM), jnp.float32) * s, 'att_r': jax.random.normal(ks[9], (L_LAYERS, HEADS, DIM), jnp.float32) * s, 'W_o': jax.random.normal(ks[10], (L_LAYERS, HEADS * DIM, DIM), jnp.float32) * s}
    _L1_gnn_all = _L1_gnn_setup()
    _L1_gnn_in = {k: v for k, v in _L1_gnn_all.items() if k in ('relation_embed', 'ln_gamma', 'ln_beta', 'W_h', 'W_t', 'W_r', 'att_h', 'att_t', 'att_r', 'W_o')}
    del _L1_gnn_all

    def _L2_gnn_setup():
        import jax, jax.numpy as jnp
        import numpy as np
        N_NODES = 100000
        N_EDGES = 15625
        D = 64
        N_LAYERS = 3
        key = jax.random.key(seed)
        k1, k2, k3, k4 = jax.random.split(key, 4)
        embedding = jax.random.normal(k1, (N_NODES, D), dtype=jnp.float32)
        src = jax.random.randint(k2, (N_EDGES,), 0, N_NODES)
        dst = jax.random.randint(k3, (N_EDGES,), 0, N_NODES)
        sqrt_degree = jax.random.uniform(k4, (N_NODES, 1), dtype=jnp.float32, minval=0.01, maxval=1.0)
        return {'embedding': embedding, 'sqrt_degree': sqrt_degree, 'src': src, 'dst': dst, 'n_layers': N_LAYERS}
    _L2_gnn_all = _L2_gnn_setup()
    _L2_gnn_in = {k: v for k, v in _L2_gnn_all.items() if k in ()}
    del _L2_gnn_all

    def _L3_gnn_setup():
        import jax, jax.numpy as jnp
        import numpy as np
        LN_EPS = 1e-06
        N, E, D_IN, D_EDGE, P, F = (50000, 12500, 64, 8, 64, 64)

        def layer_norm(x, scale, bias):
            mu = jnp.mean(x, axis=-1, keepdims=True)
            var = jnp.var(x, axis=-1, keepdims=True)
            return (x - mu) * jax.lax.rsqrt(var + LN_EPS) * scale + bias
        key = jax.random.key(seed)
        ks = jax.random.split(key, 10)
        he = lambda k, shape: jax.random.normal(k, shape, jnp.float32) * np.sqrt(2.0 / shape[0])
        din = 2 * P + D_EDGE
        inp = {'nodes': jax.random.normal(ks[0], (N, D_IN), jnp.float32), 'edges': jax.random.normal(ks[1], (E, D_EDGE), jnp.float32), 'senders': jax.random.randint(ks[2], (E,), 0, N), 'receivers': jax.random.randint(ks[3], (E,), 0, N), 'copy_arr': jnp.zeros((1,), jnp.float32), 'W_q': he(ks[4], (D_IN, P)), 'b_q': jnp.zeros((P,), jnp.float32), 'W1': he(ks[5], (din, F)), 'b1': jnp.zeros((F,), jnp.float32), 'g1': jnp.ones((F,), jnp.float32), 'be1': jnp.zeros((F,), jnp.float32), 'W2': he(ks[6], (F, F)), 'b2': jnp.zeros((F,), jnp.float32), 'g2': jnp.ones((F,), jnp.float32), 'be2': jnp.zeros((F,), jnp.float32), 'W3': he(ks[7], (F, 1)), 'b3': jnp.zeros((1,), jnp.float32), 'g3': jnp.ones((1,), jnp.float32), 'be3': jnp.zeros((1,), jnp.float32)}
        return inp
    _L3_gnn_all = _L3_gnn_setup()
    _L3_gnn_in = {k: v for k, v in _L3_gnn_all.items() if k in ('copy_arr', 'W_q', 'b_q', 'W1', 'b1', 'g1', 'be1', 'W2', 'b2', 'g2', 'be2', 'W3', 'b3', 'g3', 'be3')}
    del _L3_gnn_all
    return {'x': x, 'src': src, 'dst': dst, 'edge_attr_2': edge_attr_2, 'edge_attr_8': edge_attr_8, 'edge_type_500': edge_type_500, 'L0_gnn_W1': _L0_gnn_in['W1'], 'L0_gnn_root1': _L0_gnn_in['root1'], 'L0_gnn_bias1': _L0_gnn_in['bias1'], 'L0_gnn_W2': _L0_gnn_in['W2'], 'L0_gnn_root2': _L0_gnn_in['root2'], 'L0_gnn_bias2': _L0_gnn_in['bias2'], 'L1_gnn_relation_embed': _L1_gnn_in['relation_embed'], 'L1_gnn_ln_gamma': _L1_gnn_in['ln_gamma'], 'L1_gnn_ln_beta': _L1_gnn_in['ln_beta'], 'L1_gnn_W_h': _L1_gnn_in['W_h'], 'L1_gnn_W_t': _L1_gnn_in['W_t'], 'L1_gnn_W_r': _L1_gnn_in['W_r'], 'L1_gnn_att_h': _L1_gnn_in['att_h'], 'L1_gnn_att_t': _L1_gnn_in['att_t'], 'L1_gnn_att_r': _L1_gnn_in['att_r'], 'L1_gnn_W_o': _L1_gnn_in['W_o'], 'L3_gnn_copy_arr': _L3_gnn_in['copy_arr'], 'L3_gnn_W_q': _L3_gnn_in['W_q'], 'L3_gnn_b_q': _L3_gnn_in['b_q'], 'L3_gnn_W1': _L3_gnn_in['W1'], 'L3_gnn_b1': _L3_gnn_in['b1'], 'L3_gnn_g1': _L3_gnn_in['g1'], 'L3_gnn_be1': _L3_gnn_in['be1'], 'L3_gnn_W2': _L3_gnn_in['W2'], 'L3_gnn_b2': _L3_gnn_in['b2'], 'L3_gnn_g2': _L3_gnn_in['g2'], 'L3_gnn_be2': _L3_gnn_in['be2'], 'L3_gnn_W3': _L3_gnn_in['W3'], 'L3_gnn_b3': _L3_gnn_in['b3'], 'L3_gnn_g3': _L3_gnn_in['g3'], 'L3_gnn_be3': _L3_gnn_in['be3']}

def reference(x, src, dst, edge_attr_2, edge_attr_8, edge_type_500, L0_gnn_W1, L0_gnn_root1, L0_gnn_bias1, L0_gnn_W2, L0_gnn_root2, L0_gnn_bias2, L1_gnn_relation_embed, L1_gnn_ln_gamma, L1_gnn_ln_beta, L1_gnn_W_h, L1_gnn_W_t, L1_gnn_W_r, L1_gnn_att_h, L1_gnn_att_t, L1_gnn_att_r, L1_gnn_W_o, L3_gnn_copy_arr, L3_gnn_W_q, L3_gnn_b_q, L3_gnn_W1, L3_gnn_b1, L3_gnn_g1, L3_gnn_be1, L3_gnn_W2, L3_gnn_b2, L3_gnn_g2, L3_gnn_be2, L3_gnn_W3, L3_gnn_b3, L3_gnn_g3, L3_gnn_be3):
    import jax
    import jax.numpy as jnp

    def _L0_gnn_ref(x, edge_index, edge_attr, W1, root1, bias1, W2, root2, bias2):
        import jax, jax.numpy as jnp
        import numpy as np
        K = 5

        def spline_conv(x, edge_index, pseudo, W, root, bias):
            N = x.shape[0]
            src, dst = (edge_index[0], edge_index[1])
            xk = jnp.einsum('ni,kio->nko', x, W)
            v = pseudo * (K - 1)
            bot = jnp.floor(v)
            frac = v - bot
            bot = bot.astype(jnp.int32)
            msg = jnp.zeros((src.shape[0], W.shape[2]), dtype=x.dtype)
            for s0 in (0, 1):
                for s1 in (0, 1):
                    b0 = frac[:, 0] if s0 else 1.0 - frac[:, 0]
                    b1 = frac[:, 1] if s1 else 1.0 - frac[:, 1]
                    basis = b0 * b1
                    idx = jnp.clip(bot[:, 0] + s0, 0, K - 1) + K * jnp.clip(bot[:, 1] + s1, 0, K - 1)
                    msg = msg + basis[:, None] * xk[src, idx]
            agg = jax.ops.segment_max(msg, dst, num_segments=N)
            agg = jnp.where(jnp.isfinite(agg), agg, jnp.zeros_like(agg))
            return agg + x @ root + bias
        h = jax.nn.relu(spline_conv(x, edge_index, edge_attr, W1, root1, bias1))
        out = spline_conv(h, edge_index, edge_attr, W2, root2, bias2)
        return out

    def _L1_gnn_ref(entity_embed, relation_embed, edge_index, edge_type, ln_gamma, ln_beta, W_h, W_t, W_r, att_h, att_t, att_r, W_o):
        import jax, jax.numpy as jnp
        import numpy as np
        N_ENT, N_REL, N_EDGE = (50000, 500, 500000)
        L_LAYERS, HEADS, DIM = (2, 2, 64)
        POW_ITER, ALPHA, LN_EPS = (3, 0.15, 1e-05)

        def _layernorm(x, g, b):
            mu = jnp.mean(x, axis=-1, keepdims=True)
            var = jnp.mean(jnp.square(x - mu), axis=-1, keepdims=True)
            return (x - mu) * jax.lax.rsqrt(var + LN_EPS) * g + b

        def _node_scores(h, W, att):
            t = jnp.tanh((h @ W).reshape(h.shape[0], HEADS, DIM))
            return jnp.einsum('mhd,hd->mh', t, att)

        def _segment_softmax(scores, seg, num_segments):
            m = jax.ops.segment_max(scores, seg, num_segments=num_segments)
            e = jnp.exp(scores - m[seg])
            z = jax.ops.segment_sum(e, seg, num_segments=num_segments)
            return e / z[seg]
        src, dst = (edge_index[0], edge_index[1])
        n = entity_embed.shape[0]
        ent = entity_embed
        for l in range(L_LAYERS):
            x = ent
            h = _layernorm(x, ln_gamma[l], ln_beta[l])
            s_h = _node_scores(h, W_h[l], att_h[l])
            s_t = _node_scores(h, W_t[l], att_t[l])
            s_r = _node_scores(relation_embed, W_r[l], att_r[l])
            scores = jax.nn.leaky_relu(s_h[src] + s_t[dst] + s_r[edge_type])
            w = _segment_softmax(scores, src, n)
            A = (1.0 - ALPHA) * w
            Z = jnp.broadcast_to(h[:, None, :], (n, HEADS, DIM))
            aZ0 = ALPHA * h[:, None, :]
            for _ in range(POW_ITER):
                msg = A[:, :, None] * Z[dst]
                Z = jax.ops.segment_sum(msg, src, num_segments=n) + aZ0
            conv = Z.reshape(n, HEADS * DIM) @ W_o[l]
            ent = conv + x
        return ent

    def _L2_gnn_ref(embedding, sqrt_degree, src, dst, n_layers):
        import jax, jax.numpy as jnp
        import numpy as np
        N_NODES = 100000
        N_EDGES = 15625
        D = 64
        N_LAYERS = 3
        n_nodes = embedding.shape[0]
        h = embedding
        acc = embedding
        for _ in range(n_layers):
            msg = (h * sqrt_degree)[src]
            h = jax.ops.segment_sum(msg, dst, num_segments=n_nodes)
            h = h * sqrt_degree
            acc = acc + h
        return acc / jnp.asarray(n_layers + 1, dtype=embedding.dtype)

    def _L3_gnn_ref(nodes, edges, senders, receivers, copy_arr, W_q, b_q, W1, b1, g1, be1, W2, b2, g2, be2, W3, b3, g3, be3):
        import jax, jax.numpy as jnp
        import numpy as np
        LN_EPS = 1e-06
        N, E, D_IN, D_EDGE, P, F = (50000, 12500, 64, 8, 64, 64)

        def layer_norm(x, scale, bias):
            mu = jnp.mean(x, axis=-1, keepdims=True)
            var = jnp.var(x, axis=-1, keepdims=True)
            return (x - mu) * jax.lax.rsqrt(var + LN_EPS) * scale + bias
        n = nodes.shape[0]
        self_idx = jnp.arange(n)
        snd = jnp.concatenate([senders, self_idx])
        rcv = jnp.concatenate([receivers, self_idx])
        edg = jnp.concatenate([edges, jnp.zeros((n, edges.shape[-1]), edges.dtype)])
        q = nodes @ W_q + b_q
        sent = q[snd]
        recv = q[rcv]
        x = jnp.concatenate([sent, recv, edg], axis=-1)
        h = layer_norm(jax.nn.relu(x @ W1 + b1), g1, be1)
        h = layer_norm(jax.nn.relu(h @ W2 + b2), g2, be2)
        logits = layer_norm(jax.nn.relu(h @ W3 + b3), g3, be3)
        seg_max = jax.ops.segment_max(logits, rcv, num_segments=n)
        ex = jnp.exp(logits - jax.lax.stop_gradient(seg_max)[rcv])
        denom = jax.ops.segment_sum(ex, rcv, num_segments=n)
        att = ex / denom[rcv]
        out = jax.ops.segment_sum(sent * att, rcv, num_segments=n)
        return jax.nn.leaky_relu(out)
    edge_index = jnp.stack([src, dst])
    deg = jnp.maximum(jax.ops.segment_sum(jnp.ones(dst.shape, jnp.float32), dst, num_segments=50000), 1.0)
    deg_isqrt = deg ** (-0.5)
    x = _layernorm(x + _L0_gnn_ref(x, edge_index, edge_attr_2, L0_gnn_W1, L0_gnn_root1, L0_gnn_bias1, L0_gnn_W2, L0_gnn_root2, L0_gnn_bias2), axis=-1)
    x = _layernorm(x + _L1_gnn_ref(x, L1_gnn_relation_embed, edge_index, edge_type_500, L1_gnn_ln_gamma, L1_gnn_ln_beta, L1_gnn_W_h, L1_gnn_W_t, L1_gnn_W_r, L1_gnn_att_h, L1_gnn_att_t, L1_gnn_att_r, L1_gnn_W_o), axis=-1)
    x = _layernorm(x + _L2_gnn_ref(x, deg_isqrt[:, None], src, dst, 3), axis=-1)
    x = _layernorm(x + _L3_gnn_ref(x, edge_attr_8, src, dst, L3_gnn_copy_arr, L3_gnn_W_q, L3_gnn_b_q, L3_gnn_W1, L3_gnn_b1, L3_gnn_g1, L3_gnn_be1, L3_gnn_W2, L3_gnn_b2, L3_gnn_g2, L3_gnn_be2, L3_gnn_W3, L3_gnn_b3, L3_gnn_g3, L3_gnn_be3), axis=-1)
    return x

_drawn_inputs = setup_inputs


def setup_inputs(seed=0):
    import zlib

    import numpy as np

    out = dict(_drawn_inputs(seed))
    spreads = {'L0_gnn_bias1': (0.0, 0.1),
     'L0_gnn_bias2': (0.0, 0.1),
     'L1_gnn_ln_gamma': (1.0, 0.2),
     'L1_gnn_ln_beta': (0.0, 0.1),
     'L3_gnn_b_q': (0.0, 0.1),
     'L3_gnn_b1': (0.0, 0.1),
     'L3_gnn_g1': (1.0, 0.2),
     'L3_gnn_be1': (0.0, 0.1),
     'L3_gnn_b2': (0.0, 0.1),
     'L3_gnn_g2': (1.0, 0.2),
     'L3_gnn_be2': (0.0, 0.1)}
    factors = {'L1_gnn_relation_embed': 8.0,
     'L1_gnn_W_h': 4.773,
     'L1_gnn_W_r': 8.0,
     'L1_gnn_att_h': 4.401,
     'L1_gnn_att_r': 8.0,
     'L1_gnn_W_t': 4.088,
     'L1_gnn_att_t': 4.366}
    for name, (base, spread) in spreads.items():
        noise = np.random.default_rng([zlib.crc32(name.encode()), seed]).standard_normal(out[name].shape)
        drawn = base * np.exp(spread * noise) if base else spread * noise
        out[name] = jnp.asarray(drawn.astype(out[name].dtype))
    for name, factor in factors.items():
        out[name] = (out[name] * factor).astype(out[name].dtype)
    return out
```

```python
from contextlib import ExitStack

import concourse.bass as bass
from concourse import mybir

F32 = mybir.dt.float32
BF16 = mybir.dt.bfloat16
I32 = mybir.dt.int32
ALU = mybir.AluOpType
ACT = mybir.ActivationFunctionType
AX = mybir.AxisListType
P = 128
D = 64
K = 5
KK = K * K
NEG = -1.5e38
PAD_KEY = 65535
ROW = D + 2
U = 8
G = 14


def ds(at, n):
    return bass.ds(at, n)


class Steps:

    def __init__(self, eng, sem, per=0, turn=0, base=0):
        self.eng, self.sem, self.start, self.n = eng, sem, turn * per + base, 0
        self.fixed = isinstance(self.start, int)

    def did(self, ins):
        ins.then_inc(self.sem, 1)
        self.n += 1
        return ins

    def wait(self):
        if not self.fixed or self.start + self.n > 0:
            self.eng.wait_ge(self.sem, self.start + self.n)

    def link(self, ins):
        self.did(ins)
        self.wait()


RETIRED = []


def retire(nc, sems, at=100):
    RETIRED.extend(sems)
    if len(RETIRED) >= at:
        nc.clear_and_free_semaphores(RETIRED)
        nc.all_engine_barrier()
        RETIRED.clear()


class Stage:

    def __init__(self, nc, name):
        self.nc, self.name, self.ctx, self.sems = nc, name, ExitStack(), []

    def __enter__(self):
        self.ctx.__enter__()
        return self

    def __exit__(self, *a):
        out = self.ctx.__exit__(*a)
        retire(self.nc, self.sems)
        return out

    def sb(self, name, shape, dt=F32):
        return self.ctx.enter_context(self.nc.sbuf_tensor(f"{self.name}_{name}", shape, dt))

    def ps(self, name, shape, dt=F32):
        return self.ctx.enter_context(self.nc.psum_tensor(f"{self.name}_{name}", shape, dt))

    def sem(self, name):
        self.sems.append(self.nc.alloc_semaphore(name=f"{self.name}_{name}"))
        return self.sems[-1]


def turns_from_zero(eng, n):
    yield 0
    if n > 1:
        with eng.Fori(1, n) as i:
            yield i


def hold(eng, sem, value, s_turn):
    eng.wait_ge(sem, value)
    eng.sem_inc(s_turn, 1)


def bcast(ap, axis, n):
    v = ap.unsqueeze(axis)
    shape = list(v.shape)
    shape[axis] = n
    return v.broadcast_to(shape)



def segment_tables(nc, name, key, valid_key, T, ident, tab):
    with Stage(nc, name) as s:
        ext = s.sb("ext", [P, T + 2])
        one = s.sb("one", [P, T])
        tmp = s.sb("tmp", [P, T])
        base = s.sb("base", [P, T])
        s_key, s_shift, s_dve, s_pos = s.sem("key"), s.sem("shift"), s.sem("dve"), s.sem("pos")
        block = s.ctx.enter_context(nc.Block())

        @block.gpsimd
        def _(pool):
            nc.gpsimd.iota(tab["pos1"][:, :], pattern=[[1, T]], base=1, channel_multiplier=T,
                           allow_small_or_imprecise_dtypes=True).then_inc(s_pos, 1)

        @block.sync
        def _(sp):
            sp.wait_ge(s_key, 1)
            sp.dma_start(ext[1:P, 0:1], ext[0:P - 1, T:T + 1]).then_inc(s_shift, 16)
            sp.dma_start(ext[0:P - 1, T + 1:T + 2], ext[1:P, 1:2]).then_inc(s_shift, 16)

        @block.vector
        def _(dve):
            st = Steps(dve, s_dve)
            st.did(nc.vector.memset(one[:, :], 1.0))
            st.link(nc.vector.memset(ext[:, :], -1.0))
            nc.vector.tensor_copy(ext[:, 1:T + 1], key).then_inc(s_key, 1)
            dve.wait_ge(s_shift, 32)
            dve.wait_ge(s_key, 1)
            mid = ext[:, 1:T + 1]
            st.did(nc.vector.tensor_tensor(tab["keep"][:, :], mid, ext[:, 0:T], ALU.is_equal))
            st.link(nc.vector.tensor_tensor(tab["keepback"][:, :], mid, ext[:, 2:T + 2], ALU.is_equal))
            st.did(nc.vector.tensor_scalar(tab["neg"][:, :], tab["keep"][:, :], -NEG, NEG, ALU.mult, ALU.add))
            st.did(nc.vector.tensor_scalar(tab["negback"][:, :], tab["keepback"][:, :], -NEG, NEG, ALU.mult, ALU.add))
            st.did(nc.vector.tensor_tensor_scan(tab["pre"][:, :], tab["keep"][:, :], one[:, :], 1.0,
                                                ALU.mult, ALU.mult))
            st.link(nc.vector.tensor_tensor_scan(tab["post"][:, T - 1::-1], tab["keepback"][:, T - 1::-1],
                                                 one[:, T - 1::-1], 1.0, ALU.mult, ALU.mult))
            st.did(nc.vector.tensor_scalar(tab["negpre"][:, :], tab["pre"][:, :], -NEG, NEG, ALU.mult, ALU.add))
            st.did(nc.vector.tensor_scalar(tab["negpost"][:, :], tab["post"][:, :], -NEG, NEG, ALU.mult, ALU.add))
            st.did(nc.vector.tensor_tensor_scan(tab["count"][:, :], tab["keep"][:, :], one[:, :], 0.0,
                                                ALU.mult, ALU.add))
            st.link(nc.vector.scalar_tensor_tensor(tmp[:, :], tab["keepback"][:, :], float(PAD_KEY), mid,
                                                   ALU.mult, ALU.add))
            st.link(nc.vector.tensor_copy(tab["endrow"][:, :], tmp[:, :]))
    carry = carry_over(nc, f"{name}_c", tab["count"][:, T - 1:T], tab["pre"][:, T - 1:T], ident, 1, "sum", tab["ccount"][:, :])
    with Stage(nc, f"{name}_f") as s:
        s_dve = s.sem("dve")
        tmp = s.sb("tmp", [P, T])
        block = s.ctx.enter_context(nc.Block())

        @block.vector
        def _(dve):
            st = Steps(dve, s_dve)
            st.link(nc.vector.tensor_scalar(tmp[:, :], tab["pre"][:, :], tab["ccount"][:, 0:1], None, ALU.mult))
            st.link(nc.vector.tensor_tensor(tab["count"][:, :], tab["count"][:, :], tmp[:, :], ALU.add))


def carry_over(nc, name, ends, whole, ident, W, kind, out, back=False):
    op = (ALU.mult, ALU.add) if kind == "sum" else (ALU.add, ALU.max)
    init = 0.0 if kind == "sum" else NEG
    with Stage(nc, name) as s:
        wide = s.sb("wide", [P, W])
        wholeT = s.sb("wholeT", [W, P])
        state = s.sb("state", [W, P + 1])
        psE = s.ps("psE", [W, P])
        psW = s.ps("psW", [W, P])
        psC = s.ps("psC", [P, W])
        s_wide, s_turn, s_dve, s_state, s_back = s.sem("wide"), s.sem("turn"), s.sem("dve"), s.sem("state"), s.sem("back")
        block = s.ctx.enter_context(nc.Block())

        @block.tensor
        def _(pe):
            nc.tensor.transpose(psE[:, :], ends, ident[:, :]).then_inc(s_turn, 1)
            pe.wait_ge(s_wide, 1)
            nc.tensor.transpose(psW[:, :], wide[:, :], ident[:, :]).then_inc(s_turn, 1)
            pe.wait_ge(s_state, 1)
            src = state[:, 1:P + 1] if back else state[:, 0:P]
            nc.tensor.transpose(psC[:, :], src, ident[0:W, 0:W]).then_inc(s_back, 1)

        @block.vector
        def _(dve):
            st = Steps(dve, s_dve)
            nc.vector.tensor_copy(wide[:, :], whole.broadcast_to([P, W])).then_inc(s_wide, 1)
            edge = P if back else 0
            st.did(nc.vector.memset(state[:, edge:edge + 1], init))
            dve.wait_ge(s_turn, 2)
            st.link(nc.vector.tensor_copy(wholeT[:, :], psW[:, :]))
            if back:
                nc.vector.tensor_tensor_scan(state[:, P - 1::-1], wholeT[:, P - 1::-1], psE[:, P - 1::-1],
                                             init, *op).then_inc(s_state, 1)
            else:
                nc.vector.tensor_tensor_scan(state[:, 1:P + 1], wholeT[:, :], psE[:, :], init, *op).then_inc(s_state, 1)
            dve.wait_ge(s_back, 1)
            st.link(nc.vector.tensor_copy(out, psC[:, :]))



def sort_pass(nc, name, load, digit, out_rows, T, ones, upper, n_pass):
    C = T // G
    R = 256
    with Stage(nc, name) as s:
        rows = s.sb("rows", [P, T, 4], I32)
        dig_i = s.sb("dig_i", [P, T], I32)
        dig = s.sb("dig", [P, T])
        digits = s.sb("digits", [P, R])
        hist = s.sb("hist", [P, R])
        total = s.sb("total", [P, R])
        onesr = s.sb("onesr", [P, R])
        cum = s.sb("cum", [P, R])
        hit = s.sb("hit", [P, R])
        place = s.sb("place", [P, 2, G])
        placei = s.sb("placei", [P, 2, G], I32)
        rslot = s.sb("rslot", [P, 2, G, 4], I32)
        psB = s.ps("psB", [P, R])
        psT = s.ps("psT", [P, R])
        s_in, s_iota, s_dve, s_hist, s_pre = s.sem("in"), s.sem("iota"), s.sem("dve"), s.sem("hist"), s.sem("pre")
        s_placed, s_turn = s.sem("placed"), s.sem("turn")
        s_sent = [s.sem("sent0"), s.sem("sent1")]
        block = s.ctx.enter_context(nc.Block())

        @block.sync
        def _(sp):
            load(sp, rows, s_in)

        @block.tensor
        def _(pe):
            pe.wait_ge(s_hist, 1)
            nc.tensor.matmul(psB[:, :], upper[:, :], hist[:, :], start=True, stop=True)
            nc.tensor.matmul(psT[:, :], ones[:, :], hist[:, :], start=True, stop=True).then_inc(s_pre, 1)

        @block.gpsimd
        def _(pool):
            nc.gpsimd.iota(digits[:, :], pattern=[[1, R]], base=0, channel_multiplier=0,
                           allow_small_or_imprecise_dtypes=True).then_inc(s_iota, 1)
            bound = pool.to_reg(P * T - 1)
            for i in turns_from_zero(pool, C // 2):
                for h in range(2):
                    pool.wait_ge(s_placed, i * 2 + (h + 1))
                    pool.sem_inc(s_turn, 1)
                    for g in range(G):
                        nc.gpsimd.indirect_dma_start(
                            out=out_rows[:, :], out_offset=bass.IndirectOffsetOnAxis(ap=placei[:, h, g:g + 1], axis=0),
                            in_=rslot[:, h, g, :], in_offset=None, bounds_check=bound,
                            oob_is_err=False).then_inc(s_sent[h], 16)
            for h in range(2):
                pool.wait_ge(s_sent[h], 16 * G * (C // 2))

        @block.vector
        def _(dve):
            st = Steps(dve, s_dve)
            st.did(nc.vector.memset(onesr[:, :], 1.0))
            st.link(nc.vector.memset(hist[:, :], 0.0))
            dve.wait_ge(s_in, n_pass)
            if digit == 0:
                st.link(nc.vector.tensor_scalar(dig_i[:, :], rows[:, :, 0], R - 1, None, ALU.bitwise_and))
            else:
                st.link(nc.vector.tensor_scalar(dig_i[:, :], rows[:, :, 0], 8, None, ALU.arith_shift_right))
            st.link(nc.vector.tensor_copy(dig[:, :], dig_i[:, :]))
            dve.wait_ge(s_iota, 1)
            n0 = st.n
            with dve.Fori(0, C) as c:
                sl = Steps(dve, s_dve, G, c, n0)
                for g in range(G):
                    sl.link(nc.vector.scalar_tensor_tensor(hist[:, :], digits[:, :], dig[:, ds(c * G + g, 1)],
                                                           hist[:, :], ALU.is_equal, ALU.add))
            n0 += G * C
            st = Steps(dve, s_dve, base=n0)
            st.eng.sem_inc(s_hist, 1)
            dve.wait_ge(s_pre, 1)
            st.link(nc.vector.tensor_copy(total[:, :], psT[:, :]))
            st.link(nc.vector.tensor_tensor_scan(cum[:, :], onesr[:, :], total[:, :], 0.0, ALU.mult, ALU.add))
            st.link(nc.vector.tensor_tensor(cum[:, :], cum[:, :], total[:, :], ALU.subtract))
            st.link(nc.vector.tensor_tensor(hist[:, :], cum[:, :], psB[:, :], ALU.add))
            n0 += st.n
            per = 2 * (3 * G + 2)

            def chunk(c, h, sl):
                for g in range(G):
                    t = c * G + g
                    sl.link(nc.vector.scalar_tensor_tensor(hit[:, :], digits[:, :], dig[:, ds(t, 1)], hist[:, :],
                                                           ALU.is_equal, ALU.mult))
                    sl.link(nc.vector.tensor_reduce(place[:, h, g:g + 1], hit[:, :], AX.X, ALU.add))
                    sl.link(nc.vector.scalar_tensor_tensor(hist[:, :], digits[:, :], dig[:, ds(t, 1)], hist[:, :],
                                                           ALU.is_equal, ALU.add))
                sl.link(nc.vector.tensor_copy(placei[:, h, :], place[:, h, :]))
                sl.link(nc.vector.tensor_copy(rslot[:, h, :, :], rows[:, ds(c * G, G), :]))
                dve.sem_inc(s_placed, 1)

            for i in turns_from_zero(dve, C // 2):
                sl = Steps(dve, s_dve, per, i, n0)
                for h in range(2):
                    dve.wait_ge(s_sent[h], i * (16 * G))
                    chunk(i * 2 + h, h, sl)


def setup(nc, A, N, E, T, tabD, ident, upper, ones, rows0):
    full = E // T
    rest = E - full * T
    with Stage(nc, "setup") as s:
        onef = s.sb("onef", [P, P])
        key_src = s.sb("key_src", [P, T], I32)
        etype = s.sb("etype", [P, T], I32)
        loads = 16 * 4 * (2 if rest else 1)
        s_one, s_c, s_mem, s_in, s_dve = s.sem("one"), s.sem("c"), s.sem("mem"), s.sem("in"), s.sem("dve")
        block = s.ctx.enter_context(nc.Block())

        @block.vector
        def _(dve):
            st = Steps(dve, s_dve)
            nc.vector.memset(onef[:, :], 1.0).then_inc(s_one, 1)
            st.did(nc.vector.memset(ones[:, :], 1.0))
            for tile, pad in ((tabD["keyi"], PAD_KEY), (tabD["src"], 0), (key_src, PAD_KEY), (etype, 0)):
                nc.vector.memset(tile[:, :], pad).then_inc(s_mem, 1)
            dve.wait_ge(s_in, loads)
            nc.vector.memset(rows0[:, :, 3], 0).then_inc(s_dve, 1)
            for f, tile in enumerate((key_src, tabD["keyi"], etype)):
                nc.vector.tensor_copy(rows0[:, :, f], tile[:, :]).then_inc(s_dve, 1)

        @block.gpsimd
        def _(pool):
            pool.wait_ge(s_one, 1)
            nc.gpsimd.affine_select(out=ident[:, :], in_=onef[:, :], compare_op=ALU.is_equal, fill=0.0, base=0,
                                    pattern=[[-1, P]], channel_multiplier=1).then_inc(s_c, 1)
            nc.gpsimd.affine_select(out=upper[:, :], in_=onef[:, :], compare_op=ALU.is_gt, fill=0.0, base=0,
                                    pattern=[[1, P]], channel_multiplier=-1).then_inc(s_c, 1)

        @block.sync
        def _(sp):
            sp.wait_ge(s_mem, 4)
            for tile, name in ((tabD["keyi"], "dst"), (tabD["src"], "src"), (key_src, "src"),
                               (etype, "edge_type_500")):
                v = A[name]
                sp.dma_start(tile[0:full, :], v[0:full * T].rearrange("(p t) -> p t", t=T)).then_inc(s_in, 16)
                if rest:
                    sp.dma_start(tile[full:full + 1, 0:rest],
                                 v[full * T:E].rearrange("(p t) -> p t", p=1)).then_inc(s_in, 16)



def basis_tables(nc, A, E, T, basisT, ident):
    full, rest = E // T, E - E // T * T
    C = T // G
    with Stage(nc, "basis") as s:
        attr = s.sb("attr", [P, T, 2])
        lowi = s.sb("lowi", [P, T, 2], I32)
        low = s.sb("low", [P, T, 2])
        frac = s.sb("frac", [P, T, 2])
        knot = s.sb("knot", [P, T, 2])
        tmp = s.sb("tmp", [P, T, 2])
        hat = s.sb("hat", [P, 2, T, K])
        prod = s.sb("prod", [P, 2, G, KK])
        parts = s.sb("parts", [P, 2, G, 3 * KK], BF16)
        identb = s.sb("identb", [P, P], BF16)
        psT = [s.ps(f"psT{h}", [3 * KK, G // 2, P], BF16) for h in range(2)]
        s_mem, s_in, s_dve, s_id = s.sem("mem"), s.sem("in"), s.sem("dve"), s.sem("id")
        s_split, s_turned, s_copied = s.sem("split"), s.sem("turned"), s.sem("copied")
        block = s.ctx.enter_context(nc.Block())

        @block.sync
        def _(sp):
            sp.wait_ge(s_mem, 1)
            v = A["edge_attr_2"]
            sp.dma_start(attr[0:full, :, :], v[0:full * T, :].rearrange("(p t) f -> p t f", t=T)).then_inc(s_in, 16)
            if rest:
                sp.dma_start(attr[full:full + 1, 0:rest, :],
                             v[full * T:E, :].rearrange("(p t) f -> p t f", p=1)).then_inc(s_in, 16)

        @block.vector
        def _(dve):
            st = Steps(dve, s_dve)
            nc.vector.memset(attr[:, :, :], 0.0).then_inc(s_mem, 1)
            nc.vector.memset(basisT[:, T * P:], 0.0).then_inc(s_mem, 1)
            nc.vector.tensor_copy(identb[:, :], ident[:, :]).then_inc(s_id, 1)
            dve.wait_ge(s_in, 32 if rest else 16)
            st.link(nc.vector.tensor_scalar(attr[:, :, :], attr[:, :, :], float(K - 1), None, ALU.mult))
            st.link(nc.vector.tensor_copy(lowi[:, :, :], attr[:, :, :]))
            st.link(nc.vector.tensor_copy(low[:, :, :], lowi[:, :, :]))
            st.link(nc.vector.tensor_tensor(tmp[:, :, :], low[:, :, :], attr[:, :, :], ALU.is_gt))
            st.link(nc.vector.tensor_tensor(low[:, :, :], low[:, :, :], tmp[:, :, :], ALU.subtract))
            st.link(nc.vector.tensor_tensor(frac[:, :, :], attr[:, :, :], low[:, :, :], ALU.subtract))
            for upper in range(2):
                st.link(nc.vector.tensor_scalar(knot[:, :, :], low[:, :, :], float(upper), 0.0, ALU.add, ALU.max))
                st.did(nc.vector.tensor_scalar(knot[:, :, :], knot[:, :, :], float(K - 1), None, ALU.min))
                if not upper:
                    st.link(nc.vector.tensor_scalar(tmp[:, :, :], frac[:, :, :], -1.0, 1.0, ALU.mult, ALU.add))
                st.wait()
                part = frac if upper else tmp
                for d in range(2):
                    for a in range(K):
                        if upper:
                            st.link(nc.vector.scalar_tensor_tensor(low[:, :, d], knot[:, :, d], float(a),
                                                                   part[:, :, d], ALU.is_equal, ALU.mult))
                            st.link(nc.vector.tensor_tensor(hat[:, d, :, a], hat[:, d, :, a], low[:, :, d], ALU.add))
                        else:
                            st.did(nc.vector.scalar_tensor_tensor(hat[:, d, :, a], knot[:, :, d], float(a),
                                                                  part[:, :, d], ALU.is_equal, ALU.mult))
                st.wait()
            n0 = st.n
            for i in turns_from_zero(dve, C // 2):
                sl = Steps(dve, s_dve, 2 * (K + 4), i, n0)
                for h in range(2):
                    c = i * 2 + h
                    for b in range(K):
                        sl.did(nc.vector.tensor_tensor(
                            prod[:, h, :, K * b:K * b + K], hat[:, 0, ds(c * G, G), :],
                            hat[:, 1, ds(c * G, G), b:b + 1].broadcast_to([P, G, K]), ALU.mult))
                    sl.wait()
                    dve.wait_ge(s_turned, i * 4 + 2 * h)
                    sl.link(nc.vector.tensor_copy(parts[:, h, :, 0:KK], prod[:, h, :, :]))
                    sl.link(nc.vector.tensor_tensor(prod[:, h, :, :], prod[:, h, :, :], parts[:, h, :, 0:KK], ALU.subtract))
                    sl.link(nc.vector.tensor_copy(parts[:, h, :, KK:2 * KK], prod[:, h, :, :]))
                    sl.link(nc.vector.tensor_tensor(parts[:, h, :, 2 * KK:3 * KK], prod[:, h, :, :],
                                                    parts[:, h, :, KK:2 * KK], ALU.subtract))
                    dve.sem_inc(s_split, 1)

        @block.tensor
        def _(pe):
            pe.wait_ge(s_id, 1)
            pe.sem_inc(s_turned, 2)
            for i in turns_from_zero(pe, C // 2):
                for h in range(2):
                    pe.wait_ge(s_split, i * 2 + (h + 1))
                    for u in range(2):
                        pe.wait_ge(s_copied, i * 4 + (2 * h + u))
                        for g in range(G // 2):
                            ins = nc.tensor.transpose(psT[u][:, g, :], parts[:, h, u * (G // 2) + g, :], identb[:, :])
                        ins.then_inc(s_turned, 1)

        @block.scalar
        def _(act):
            act.sem_inc(s_copied, 1)
            for i in turns_from_zero(act, C // 2):
                for h in range(2):
                    for u in range(2):
                        act.wait_ge(s_turned, i * 4 + (2 * h + u + 3))
                        nc.scalar.activation(basisT[:, ds(((i * 2 + h) * 2 + u) * (G // 2) * P, (G // 2) * P)],
                                             psT[u][:, :, :].rearrange("k g p -> k (g p)"), ACT.Copy).then_inc(s_copied, 1)


def gather_chunks(nc, pool, C, s_turn, jobs, free, n=G):
    bounds = [pool.to_reg(last) for _, last, *_ in jobs]
    for i in turns_from_zero(pool, C // 2):
        for h in range(2):
            for sem, per in free:
                pool.wait_ge(sem, i * (2 * per) + (h + 1) * per)
                pool.sem_inc(s_turn, 1)
            for (table, _, idx, islot, rslot, s_rows, s_idx), bound in zip(jobs, bounds):
                nc.gpsimd.tensor_copy(islot[:, h, :], idx[:, ds((i * 2 + h) * n, n)]).then_inc(s_idx, 1)
                pool.wait_ge(s_idx, i * 2 + (h + 1))
                pool.sem_inc(s_turn, 1)
                for g in range(n):
                    nc.gpsimd.indirect_dma_start(
                        out=rslot[:, h, g, 0:table.shape[1]], out_offset=None, in_=table[:, :],
                        in_offset=bass.IndirectOffsetOnAxis(ap=islot[:, h, g:g + 1], axis=0),
                        bounds_check=bound, oob_is_err=False).then_inc(s_rows[h], 16)


def scatter_chunks(nc, pool, C, s_turn, s_ready, table, last, islot, rslot, s_sent):
    bound = pool.to_reg(last)
    for i in turns_from_zero(pool, C // 2):
        for h in range(2):
            pool.wait_ge(s_ready, i * 2 + (h + 1))
            pool.sem_inc(s_turn, 1)
            for g in range(G):
                nc.gpsimd.indirect_dma_start(
                    out=table[:, :], out_offset=bass.IndirectOffsetOnAxis(ap=islot[:, h, g:g + 1], axis=0),
                    in_=rslot[:, h, g, :], in_offset=None, bounds_check=bound,
                    oob_is_err=False).then_inc(s_sent[h], 16)
    for h in range(2):
        pool.wait_ge(s_sent[h], 16 * G * (C // 2))


def spline_messages(nc, name, W, table, width, N, T, tab, basisT, ident, agg, ptr):
    C = T // G
    UN = [range(0, 4), range(4, 8), range(8, 12), range(12, 13)]
    with Stage(nc, name) as s:
        islot = s.sb("islot", [P, 2, G], I32)
        rows = s.sb("rows", [P, 2, G, width])
        rowsT = s.sb("rowsT", [P, 2, G, P])
        scaled = s.sb("scaled", [P, 2, 13, P])
        knots = s.sb("knots", [3 * KK, 26, D], BF16)
        knots0 = s.sb("knots0", [3 * KK, 26, D], BF16)
        Wr = s.sb("Wr", [P, 13, D])
        psX = [s.ps(f"psX{h}", [D, 4, P]) for h in range(2)]
        psB = [s.ps(f"psB{q}", [P, 4, P]) for q in range(4)]
        psM = [s.ps(f"psM{h}", [P, 512]) for h in range(2)]
        s_w, s_sel, s_turn, s_idx = s.sem("w"), s.sem("sel"), s.sem("turn"), s.sem("idx")
        s_rows = [s.sem("rows0"), s.sem("rows1")]
        s_xt, s_xcopied, s_basis, s_scaled = s.sem("xt"), s.sem("xcopied"), s.sem("basis"), s.sem("scaled")
        s_main, s_max, s_dve = s.sem("main"), s.sem("max"), s.sem("dve")
        s_kept, s_pturn = s.sem("kept"), s.sem("pturn")
        block = s.ctx.enter_context(nc.Block())

        @block.sync
        def _(sp):
            sp.dma_start(Wr[:, 0:12, :], W[0:24, :, :].rearrange("(c k) i o -> (k i) c o", k=2)).then_inc(s_w, 16)
            sp.dma_start(Wr[0:D, 12, :], W[24, :, :]).then_inc(s_w, 16)

        @block.gpsimd
        def _(pool):
            nc.gpsimd.memset(knots[:, :, :], 0.0).then_inc(s_sel, 1)
            for part in range(3):
                pool.wait_ge(s_sel, part + 1)
                nc.gpsimd.affine_select(out=knots[:, :, :], in_=knots[:, :, :], compare_op=ALU.not_equal, fill=1.0,
                                        base=-KK * part, pattern=[[-1, KK + 1], [0, D]], channel_multiplier=1).then_inc(s_sel, 1)
            gather_chunks(nc, pool, C, s_turn, [(table, N - 1, tab["src"], islot, rows, s_rows, s_idx)],
                          [(s_xt, 4), (s_kept, 1)])

        @block.tensor
        def _(pe):
            pe.wait_ge(s_sel, 4)
            pe.wait_ge(s_w, 32)
            pe.sem_inc(s_xt, 8)

            def spread(m, q):
                for n, c in enumerate(UN[q]):
                    w = P if c < 12 else D
                    ins = nc.tensor.matmul(psB[q][0:w, n, :], knots[:, 2 * c:2 * c + w // D, :],
                                           basisT[:, ds(m * P, P)], start=True, stop=True)
                ins.then_inc(s_basis, 1)

            for q in range(4):
                spread(0, q)
            for i in turns_from_zero(pe, C // 2):
                for h in range(2):
                    j = i * 2 + h
                    pe.wait_ge(s_rows[h], i * (16 * G) + 16 * G)
                    for q in range(4):
                        hold(pe, s_xcopied, j * 8 + 2 * q, s_pturn)
                        for n, t in enumerate(range(4 * q, min(4 * q + 4, G))):
                            ins = nc.tensor.transpose(psX[q % 2][:, n, :], rows[:, h, t, 0:D], ident[:, :])
                        ins.then_inc(s_xt, 1)
                    for t in range(G):
                        m = j * G + t
                        pe.wait_ge(s_max, m + 1)
                        for q in range(4):
                            pe.wait_ge(s_scaled, m * 4 + (q + 1 + 8 * G))
                            for c in UN[q]:
                                k = P if c < 12 else D
                                ins = nc.tensor.matmul(psM[t % 2][:, 0:D], scaled[0:k, t % 2, c, :], Wr[0:k, c, :],
                                                       start=(c == 0), stop=(c == 12))
                            if q == 3:
                                ins.then_inc(s_main, 1)
                            spread(m + 1, q)

        @block.scalar
        def _(act):
            act.sem_inc(s_xcopied, 2)
            for i in turns_from_zero(act, C // 2):
                for h in range(2):
                    j = i * 2 + h
                    act.wait_ge(s_scaled, j * (4 * G) + 4 * G)
                    for q in range(4):
                        n = min(4, G - 4 * q)
                        act.wait_ge(s_xt, j * 4 + (q + 9))
                        for half in (0, D):
                            nc.scalar.activation(rowsT[half:half + D, h, 4 * q:4 * q + n, :], psX[q % 2][:, 0:n, :],
                                                 ACT.Copy).then_inc(s_xcopied, 1)

        @block.vector
        def _(dve):
            nc.vector.memset(agg[:, 0, :], NEG).then_inc(s_dve, 1)
            dve.wait_ge(s_dve, 1)
            dve.sem_inc(s_max, 2)
            dve.sem_inc(s_scaled, 8 * G)
            dve.sem_inc(s_kept, 2)

            def running_max(m, par):
                dve.wait_ge(s_main, m + 1)
                dve.wait_ge(s_max, m + 2)
                nc.vector.scalar_tensor_tensor(agg[:, ds(m + 1, 1), :].rearrange("p a d -> p (a d)"),
                                               agg[:, ds(m, 1), :].rearrange("p a d -> p (a d)"),
                                               tab["neg"][:, ds(m, 1)], psM[par][:, 0:D], ALU.add,
                                               ALU.max).then_inc(s_max, 1)

            for i in turns_from_zero(dve, C // 2):
                for h in range(2):
                    j = i * 2 + h
                    dve.wait_ge(s_rows[h], i * (16 * G) + 16 * G)
                    if ptr is not None:
                        nc.vector.tensor_copy(ptr[:, ds(j * G, G)], rows[:, h, :, D]).then_inc(s_kept, 1)
                    else:
                        dve.sem_inc(s_kept, 1)
                    for t in range(G):
                        m = j * G + t
                        if t % 4 == 0:
                            dve.wait_ge(s_xcopied, j * 8 + (2 * (t // 4) + 4))
                        for q in range(4):
                            c0, c1 = UN[q][0], UN[q][-1] + 1
                            k = P if c0 < 12 else D
                            dve.wait_ge(s_basis, m * 4 + (q + 1))
                            nc.vector.tensor_tensor(scaled[0:k, t % 2, c0:c1, :], psB[q][0:k, 0:c1 - c0, :],
                                                    bcast(rowsT[0:k, h, t, :], 1, c1 - c0), ALU.mult).then_inc(s_scaled, 1)
                        if t:
                            running_max(m - 1, (t - 1) % 2)
                    running_max(j * G + (G - 1), (G - 1) % 2)


def scatter_ends(nc, name, T, tab, carry, agg, kind, table, N, cols=True):
    C = T // G
    with Stage(nc, name) as s:
        islot = s.sb("islot", [P, 2, G], I32)
        rslot = s.sb("rslot", [P, 2, G, ROW])
        s_turn, s_dve, s_ready = s.sem("turn"), s.sem("dve"), s.sem("ready")
        s_sent = [s.sem("sent0"), s.sem("sent1")]
        block = s.ctx.enter_context(nc.Block())

        @block.gpsimd
        def _(pool):
            scatter_chunks(nc, pool, C, s_turn, s_ready, table, N - 1, islot, rslot, s_sent)

        @block.vector
        def _(dve):
            pre, ops = (tab["negpre"], (ALU.add, ALU.max)) if kind == "max" else (tab["pre"], (ALU.mult, ALU.add))
            for i in turns_from_zero(dve, C // 2):
                for h in range(2):
                    sl = Steps(dve, s_dve, G + 3, i * 2 + h)
                    dve.wait_ge(s_sent[h], i * (16 * G))
                    for g in range(G):
                        t = (i * 2 + h) * G + g
                        sl.did(nc.vector.scalar_tensor_tensor(
                            rslot[:, h, g, 0:D], carry[:, :], pre[:, ds(t, 1)],
                            agg[:, ds(t + 1, 1), :].rearrange("p a d -> p (a d)"), *ops))
                    at = ds((i * 2 + h) * G, G)
                    sl.did(nc.vector.tensor_copy(rslot[:, h, :, D], tab["pos1"][:, at]))
                    sl.did(nc.vector.tensor_copy(rslot[:, h, :, D + 1], tab["count"][:, at]))
                    sl.did(nc.vector.tensor_copy(islot[:, h, :], tab["endrow"][:, at]))
                    sl.wait()
                    dve.sem_inc(s_ready, 1)


def zero_fill(nc, name, tensors):
    with Stage(nc, name) as s:
        z = s.sb("z", [P, 8 * ROW])
        s_z, s_out = s.sem("z"), s.sem("out")
        block = s.ctx.enter_context(nc.Block())

        @block.vector
        def _(dve):
            nc.vector.memset(z[:, :], 0.0).then_inc(s_z, 1)

        @block.sync
        def _(sp):
            sp.wait_ge(s_z, 1)
            n = 0
            for t in tensors:
                rows, w = t.shape
                per = U * w
                if rows % (P * U) == 0:
                    v = t.rearrange("(c p u) w -> c p (u w)", p=P, u=U)
                    chunks = rows // (P * U)
                    with sp.Fori(0, chunks) as c:
                        sp.dma_start(v[ds(c, 1)].rearrange("a p w -> (a p) w"), z[:, 0:per]).then_inc(s_out, 16)
                    n += chunks
                else:
                    sp.dma_start(t, z[0:rows, 0:w]).then_inc(s_out, 16)
                    n += 1
            sp.wait_ge(s_out, 16 * n)




def node_chunks(eng, NC):
    for i in turns_from_zero(eng, (NC - 1) // 2):
        for h in range(2):
            yield i * 2 + h, h, i, False
    yield NC - 1, 0, (NC - 1) // 2, True


def chunk_rows(table, c, last, N):
    v = table.rearrange("(p u) w -> p (u w)", u=U)
    n = (N // U - c * P) if last else P
    return v[ds(c * P, n), :], n


def node_mask(NC, N, last):
    return N // U - (NC - 1) * P if last else P


class Norm:

    def __init__(self, s, name, n, eps_tile):
        self.xc = s.sb(f"{name}_xc", [P, n, D])
        self.sq = s.sb(f"{name}_sq", [P, n, D])
        self.sum = s.sb(f"{name}_sum", [P, n])
        self.mean = s.sb(f"{name}_mean", [P, n])
        self.var = s.sb(f"{name}_var", [P, n])
        self.std = s.sb(f"{name}_std", [P, n])
        self.rstd = s.sb(f"{name}_rstd", [P, n])
        self.n, self.eps = n, eps_tile

    def centre(self, nc, st, x, s_var):
        st.link(nc.vector.tensor_reduce(self.sum[:, :], x, AX.X, ALU.add))
        st.link(nc.vector.tensor_scalar(self.mean[:, :], self.sum[:, :], 1.0 / D, None, ALU.mult))
        st.link(nc.vector.tensor_tensor(self.xc[:, :, :], x, bcast(self.mean[:, :], 2, D), ALU.subtract))
        st.link(nc.vector.tensor_tensor(self.sq[:, :, :], self.xc[:, :, :], self.xc[:, :, :], ALU.mult))
        nc.vector.tensor_reduce(self.var[:, :], self.sq[:, :, :], AX.X, ALU.add).then_inc(s_var, 1)

    def root(self, nc, s_std):
        nc.scalar.activation(self.std[:, :], self.var[:, :], ACT.Sqrt, bias=self.eps[:, :], scale=1.0 / D).then_inc(s_std, 1)

    def finish(self, nc, st, out):
        st.link(nc.vector.reciprocal(self.rstd[:, :], self.std[:, :]))
        st.link(nc.vector.tensor_tensor(out, self.xc[:, :, :], bcast(self.rstd[:, :], 2, D), ALU.mult))


def spread_rows(eng, tile, vec, sem):
    eng.dma_start(tile, vec.partition_broadcast(P)).then_inc(sem, 16)


def node_stage(nc, name, N, NC, ident, loads, stores, consts, product, acts, body, per):
    turned, weights, bias, early = product or (None, [], None, True)
    with Stage(nc, name) as s:
        tiles = {k: s.sb(k, [P, 2, U, w]) for k, (_, w) in {**loads, **stores}.items()}
        vec = {k: s.sb(k, [P, D]) for k in consts}
        eps = s.sb("eps", [P, 1])
        norm = Norm(s, "norm", U, eps)
        norms = len(acts)
        tmp = s.sb("tmp", [P, U, D])
        small_in = s.sb("small_in", [P, U])
        small_out = s.sb("small_out", [P, U])
        s_dve, s_const, s_mem, s_var, s_std = (s.sem(k) for k in ("dve", "const", "mem", "var", "std"))
        s_in = [s.sem("in0"), s.sem("in1")]
        s_out = [s.sem("out0"), s.sem("out1")]
        s_done, s_src, s_xt, s_xc, s_mm, s_turn, s_pturn = (s.sem(k) for k in (
            "done", "src", "xt", "xc", "mm", "turn", "pturn"))
        nw = len(weights)
        if product:
            xT = s.sb("xT", [D + 1, 2, U * P])
            wb = s.sb("wb", [D + 1, nw, D])
            psX = [s.ps(f"psX{k}", [D, 4 * P]) for k in range(2)]
            psO = [s.ps(f"psO{h}", [P, U, D]) for h in range(2)]
        block = s.ctx.enter_context(nc.Block())
        n_const = len(consts) + nw + (1 if bias is not None else 0)

        @block.sync
        def _(sp):
            for k, v in consts.items():
                spread_rows(sp, vec[k][:, :], v, s_const)
            if product:
                for n, w in enumerate(weights):
                    sp.dma_start(wb[0:D, n, :], w).then_inc(s_const, 16)
                if bias is not None:
                    sp.wait_ge(s_mem, 3)
                    sp.dma_start(wb[D:D + 1, 0, :], bias.rearrange("(a n) -> a n", a=1)).then_inc(s_const, 16)
            sp.wait_ge(s_mem, 3)
            for c, h, i, last in node_chunks(sp, NC):
                sp.wait_ge(s_done, c + 1)
                if product and early:
                    sp.wait_ge(s_mm, c + 1)
                for k, (table, w) in loads.items():
                    src, n = chunk_rows(table, c, last and table.shape[0] == N, N)
                    sp.dma_start(tiles[k][0:n, h].rearrange("p u d -> p (u d)"), src).then_inc(s_in[h], 16)

        @block.vector
        def _(dve):
            st = Steps(dve, s_dve)
            nc.vector.memset(eps[:, :], 1e-5).then_inc(s_mem, 1)
            if product:
                nc.vector.memset(xT[D:D + 1, :, :], 1.0).then_inc(s_mem, 1)
                nc.vector.memset(wb[D:D + 1, :, :], 0.0).then_inc(s_mem, 1)
            else:
                dve.sem_inc(s_mem, 2)
            dve.sem_inc(s_done, 2)
            if n_const:
                dve.wait_ge(s_const, 16 * n_const)

            for c, h, i, last in node_chunks(dve, NC):
                st = Steps(dve, s_dve, per, c)
                dve.wait_ge(s_in[h], i * (16 * len(loads)) + 16 * len(loads))
                dve.wait_ge(s_out[h], i * (16 * len(stores)))
                k = [0]

                def layer_norm(x, out):
                    norm.centre(nc, st, x, s_var)
                    dve.wait_ge(s_std, c * norms + (k[0] + 1))
                    k[0] += 1
                    norm.finish(nc, st, out)

                def product_ready():
                    dve.wait_ge(s_mm, c + 3)
                    return psO[h][:, :, :]

                def exp(x):
                    x.then_inc(s_var, 1)
                    dve.wait_ge(s_std, c * norms + (k[0] + 1))
                    k[0] += 1

                T = {n: (lambda v: (v[:, h, :, :]))(v) for n, v in tiles.items()}
                body(st, T, vec, c, tmp[:, :, :], layer_norm, product_ready,
                     lambda: dve.sem_inc(s_src, 1), *([small_in, small_out, exp] if "exp" in acts else []))
                assert st.n == per and k[0] == norms, (st.n, k[0])
                st.wait()
                dve.sem_inc(s_done, 1)

        @block.tensor
        def _(pe):
            if not product:
                return
            pe.sem_inc(s_mm, 2)
            pe.wait_ge(s_const, 16 * n_const)
            pe.wait_ge(s_mem, 3)
            for c, h, i, last in node_chunks(pe, NC):
                if early:
                    pe.wait_ge(s_in[h], i * (16 * len(loads)) + 16 * len(loads))
                else:
                    pe.wait_ge(s_src, c + 1)
                for q in range(2):
                    hold(pe, s_xc, c * 2 + (q + 1), s_pturn)
                    for g in range(4):
                        ins = nc.tensor.transpose(psX[q][:, g * P:(g + 1) * P], tiles[turned][:, h, q * 4 + g, 0:D], ident[:, :])
                    ins.then_inc(s_xt, 1)
                hold(pe, s_done, c + 1, s_pturn)
                for g in range(U):
                    if g % 4 == 0:
                        hold(pe, s_xc, c * 2 + (g // 4 + 3), s_pturn)
                    for n in range(nw):
                        ins = nc.tensor.matmul(psO[h][:, g, :], xT[:, h, g * P:(g + 1) * P], wb[:, n, :],
                                               start=(n == 0), stop=(n == nw - 1))
                ins.then_inc(s_mm, 1)

        @block.scalar
        def _(act):
            act.sem_inc(s_xc, 2)

            def copies(c, h):
                act.wait_ge(s_mm, c + 1)
                for q in range(2):
                    act.wait_ge(s_xt, c * 2 + (q + 1))
                    nc.scalar.activation(xT[0:D, h, q * 4 * P:(q + 1) * 4 * P], psX[q][:, :], ACT.Copy).then_inc(s_xc, 1)

            def roots(c):
                for k in range(norms):
                    act.wait_ge(s_var, c * norms + (k + 1))
                    if acts[k] == "root":
                        norm.root(nc, s_std)
                    else:
                        nc.scalar.activation(small_out[:, :], small_in[:, :], ACT.Exp).then_inc(s_std, 1)

            act.wait_ge(s_mem, 3)
            for c, h, i, last in node_chunks(act, NC):
                if product and early:
                    copies(c, h)
                roots(c)
                if product and not early:
                    copies(c, h)

        @block.gpsimd
        def _(pool):
            for c, h, i, last in node_chunks(pool, NC):
                pool.wait_ge(s_done, c + 3)
                pool.sem_inc(s_turn, 1)
                for k, (table, w) in stores.items():
                    dst, n = chunk_rows(table, c, last and table.shape[0] == N, N)
                    pool.dma_start(dst, tiles[k][0:n, h].rearrange("p u d -> p (u d)")).then_inc(s_out[h], 16)
            pool.wait_ge(s_out[0], 16 * len(stores) * ((NC + 1) // 2))
            pool.wait_ge(s_out[1], 16 * len(stores) * (NC // 2))


def node_hidden(nc, name, A, SD, H, N, NC, ident, countN):
    with Stage(nc, name) as s:
        x = s.sb("x", [P, 2, U, D])
        agg = s.sb("agg", [P, 2, U, ROW])
        xT = s.sb("xT", [D + 1, 2, U * P])
        tot = s.sb("tot", [P, 2, U, D])
        hrow = s.sb("hrow", [P, 2, U, ROW])
        wb = s.sb("wb", [D + 1, D])
        psX = [s.ps(f"psX{k}", [D, 4 * P]) for k in range(2)]
        psO = [s.ps(f"psO{h}", [P, U, D]) for h in range(2)]
        s_w, s_one, s_xt, s_xc, s_mm, s_tot, s_cols, s_relu = (s.sem(k) for k in (
            "w", "one", "xt", "xc", "mm", "tot", "cols", "relu"))
        s_in = [s.sem("in0"), s.sem("in1")]
        s_out = [s.sem("out0"), s.sem("out1")]
        s_turn, s_pturn = s.sem("turn"), s.sem("pturn")
        block = s.ctx.enter_context(nc.Block())

        @block.sync
        def _(sp):
            sp.dma_start(wb[0:D, :], A["L0_gnn_root1"]).then_inc(s_w, 16)
            sp.dma_start(wb[D:D + 1, :], A["L0_gnn_bias1"].rearrange("(a n) -> a n", a=1)).then_inc(s_w, 16)
            for c, h, i, last in node_chunks(sp, NC):
                sp.wait_ge(s_mm, c + 1)
                sp.wait_ge(s_cols, c * 2 + 2)
                src, n = chunk_rows(A["x"], c, last, N)
                sp.dma_start(x[0:n, h].rearrange("p u d -> p (u d)"), src).then_inc(s_in[h], 16)
                src, _ = chunk_rows(SD, c, False, N)
                sp.dma_start(agg[:, h].rearrange("p u d -> p (u d)"), src).then_inc(s_in[h], 16)

        @block.tensor
        def _(pe):
            pe.sem_inc(s_mm, 2)
            pe.wait_ge(s_w, 32)
            pe.wait_ge(s_one, 1)
            for c, h, i, last in node_chunks(pe, NC):
                pe.wait_ge(s_in[h], i * 32 + 32)
                for q in range(2):
                    hold(pe, s_xc, c * 2 + (q + 1), s_pturn)
                    for g in range(4):
                        ins = nc.tensor.transpose(psX[q][:, g * P:(g + 1) * P], x[:, h, q * 4 + g, :], ident[:, :])
                    ins.then_inc(s_xt, 1)
                pe.wait_ge(s_tot, c + 1)
                for g in range(U):
                    if g % 4 == 0:
                        hold(pe, s_xc, c * 2 + (g // 4 + 3), s_pturn)
                    ins = nc.tensor.matmul(psO[h][:, g, :], xT[:, h, g * P:(g + 1) * P], wb[:, :], start=True, stop=True)
                ins.then_inc(s_mm, 1)

        @block.scalar
        def _(act):
            act.sem_inc(s_xc, 2)
            for c, h, i, last in node_chunks(act, NC):
                act.wait_ge(s_mm, c + 1)
                for q in range(2):
                    act.wait_ge(s_xt, c * 2 + (q + 1))
                    nc.scalar.activation(xT[0:D, h, q * 4 * P:(q + 1) * 4 * P], psX[q][:, :], ACT.Copy).then_inc(s_xc, 1)
                act.wait_ge(s_tot, c + 3)
                act.wait_ge(s_out[h], i * 16)
                nc.scalar.activation(hrow[:, h, :, 0:D], tot[:, h, :, :], ACT.Relu).then_inc(s_relu, 1)

        @block.vector
        def _(dve):
            nc.vector.memset(x[:, :, :, :], 0.0).then_inc(s_one, 1)
            dve.wait_ge(s_one, 1)
            nc.vector.memset(xT[D:D + 1, :, :], 1.0).then_inc(s_one, 1)
            dve.wait_ge(s_one, 2)
            dve.sem_inc(s_tot, 2)
            dve.sem_inc(s_cols, 4)
            for c, h, i, last in node_chunks(dve, NC):
                dve.wait_ge(s_mm, c + 3)
                dve.wait_ge(s_relu, c)
                nc.vector.tensor_tensor(tot[:, h, :, :], psO[h][:, :, :], agg[:, h, :, 0:D], ALU.add).then_inc(s_tot, 1)
                dve.wait_ge(s_out[h], i * 16)
                nc.vector.tensor_copy(hrow[:, h, :, D:ROW], agg[:, h, :, D:ROW]).then_inc(s_cols, 1)
                nc.vector.tensor_copy(countN[:, ds(c * U, U)], agg[:, h, :, D + 1]).then_inc(s_cols, 1)

        @block.gpsimd
        def _(pool):
            for c, h, i, last in node_chunks(pool, NC):
                pool.wait_ge(s_relu, c + 1)
                pool.sem_inc(s_turn, 1)
                pool.wait_ge(s_cols, c * 2 + 6)
                pool.sem_inc(s_turn, 1)
                dst, n = chunk_rows(H, c, False, N)
                pool.dma_start(dst, hrow[:, h].rearrange("p u d -> p (u d)")).then_inc(s_out[h], 16)
            pool.wait_ge(s_out[0], 16 * ((NC + 1) // 2))
            pool.wait_ge(s_out[1], 16 * (NC // 2))




def relation_scores(nc, A, ones, table):
    R = A["L1_gnn_relation_embed"].shape[0]
    NT = -(-R // P)
    with Stage(nc, "rel") as s:
        emb = s.sb("emb", [P, NT, D])
        ident = s.sb("ident", [P, P])
        embT = s.sb("embT", [D, NT * P])
        w = s.sb("w", [D, 2, P])
        att = s.sb("att", [P, 2, P])
        th = s.sb("th", [P, NT, 2, P])
        prod = s.sb("prod", [P, NT, 2, P])
        res = s.sb("res", [P, NT, 4])
        psX = s.ps("psX", [D, NT * P])
        psS = [s.ps(f"psS{k}", [P, 2, 2, P]) for k in range(NT // 2)]
        s_mem, s_id, s_in, s_xt, s_xc, s_mm, s_th, s_dve, s_res, s_out = (s.sem(k) for k in (
            "mem", "id", "in", "xt", "xc", "mm", "th", "dve", "res", "out"))
        block = s.ctx.enter_context(nc.Block())
        full, rest = R // P, R % P

        @block.sync
        def _(sp):
            sp.wait_ge(s_mem, 1)
            e = A["L1_gnn_relation_embed"]
            for n in range(NT):
                m = min(P, R - n * P)
                sp.dma_start(emb[0:m, n, :], e[n * P:n * P + m, :]).then_inc(s_in, 16)
            for l in range(2):
                sp.dma_start(w[:, l, :], A["L1_gnn_W_r"][l]).then_inc(s_in, 16)
                spread_rows(sp, att[:, l, :], A["L1_gnn_att_r"][l].rearrange("h d -> (h d)"), s_in)
            sp.wait_ge(s_res, 1)
            for n in range(NT):
                m = min(P, R - n * P)
                sp.dma_start(table[n * P:n * P + m, :], res[0:m, n, :]).then_inc(s_out, 16)
            sp.wait_ge(s_out, 16 * NT)

        @block.gpsimd
        def _(pool):
            nc.gpsimd.affine_select(out=ident[:, :], in_=ones[:, :], compare_op=ALU.is_equal, fill=0.0, base=0,
                                    pattern=[[-1, P]], channel_multiplier=1).then_inc(s_id, 1)

        @block.tensor
        def _(pe):
            pe.wait_ge(s_id, 1)
            pe.wait_ge(s_in, 16 * (NT + 4))
            for n in range(NT):
                nc.tensor.transpose(psX[:, n * P:(n + 1) * P], emb[:, n, :], ident[:, :]).then_inc(s_xt, 1)
            pe.wait_ge(s_xc, 1)
            for n in range(NT):
                for l in range(2):
                    nc.tensor.matmul(psS[n // 2][:, n % 2, l, :], embT[:, n * P:(n + 1) * P], w[:, l, :],
                                     start=True, stop=True).then_inc(s_mm, 1)

        @block.scalar
        def _(act):
            act.wait_ge(s_xt, NT)
            nc.scalar.activation(embT[:, :], psX[:, :], ACT.Copy).then_inc(s_xc, 1)
            act.wait_ge(s_mm, 2 * NT)
            for k in range(NT // 2):
                nc.scalar.activation(th[:, 2 * k:2 * k + 2, :, :], psS[k][:, :, :, :], ACT.Tanh).then_inc(s_th, 1)

        @block.vector
        def _(dve):
            st = Steps(dve, s_dve)
            nc.vector.memset(emb[:, :, :], 0.0).then_inc(s_mem, 1)
            dve.wait_ge(s_in, 16 * (NT + 4))
            dve.wait_ge(s_th, NT // 2)
            st.link(nc.vector.tensor_tensor(prod[:, :, :, :], th[:, :, :, :], bcast(att[:, :, :], 1, NT), ALU.mult))
            nc.vector.tensor_reduce(res[:, :, :], prod[:, :, :, :].rearrange("p n l (h d) -> p n (l h) d", h=2),
                                    AX.X, ALU.add).then_inc(s_res, 1)


def sorted_edges(nc, sorted2, T, N, keyS, srcS, dstS, typS):
    with Stage(nc, "byS") as s:
        rows = s.sb("rows", [P, T, 4], I32)
        s_in, s_dve = s.sem("in"), s.sem("dve")
        block = s.ctx.enter_context(nc.Block())

        @block.sync
        def _(sp):
            sp.dma_start(rows[:, :, :], sorted2.rearrange("(p t) f -> p t f", t=T)).then_inc(s_in, 16)

        @block.vector
        def _(dve):
            dve.wait_ge(s_in, 16)
            st = Steps(dve, s_dve)
            st.did(nc.vector.tensor_copy(keyS, rows[:, :, 0]))
            st.did(nc.vector.tensor_copy(typS, rows[:, :, 2]))
            st.did(nc.vector.tensor_scalar(srcS, rows[:, :, 0], float(N - 1), None, ALU.min))
            st.did(nc.vector.tensor_scalar(dstS, rows[:, :, 1], float(N - 1), None, ALU.min))
            st.wait()


def scatter_places(nc, T, N, tab, table, ptrN, NC):
    C = T // G
    with Stage(nc, "places") as s:
        islot = s.sb("islot", [P, 2, G], I32)
        rslot = s.sb("rslot", [P, 2, G, 1])
        s_turn, s_dve, s_ready, s_in = s.sem("turn"), s.sem("dve"), s.sem("ready"), s.sem("in")
        s_sent = [s.sem("sent0"), s.sem("sent1")]
        block = s.ctx.enter_context(nc.Block())

        @block.gpsimd
        def _(pool):
            scatter_chunks(nc, pool, C, s_turn, s_ready, table, N - 1, islot, rslot, s_sent)
            pool.dma_start(ptrN.rearrange("p (c u) -> p c u", u=U),
                           table.rearrange("(c p u) w -> p c (u w)", p=P, u=U)).then_inc(s_in, 16)
            pool.wait_ge(s_in, 16)

        @block.vector
        def _(dve):
            for i in turns_from_zero(dve, C // 2):
                for h in range(2):
                    sl = Steps(dve, s_dve, 2, i * 2 + h)
                    dve.wait_ge(s_sent[h], i * (16 * G))
                    at = ds((i * 2 + h) * G, G)
                    sl.did(nc.vector.tensor_copy(rslot[:, h, :, 0], tab["pos1"][:, at]))
                    sl.link(nc.vector.tensor_copy(islot[:, h, :], tab["endrow"][:, at]))
                    dve.sem_inc(s_ready, 1)


def gather_whole(nc, name, T, table, last, idx, out, w):
    C = T // G
    with Stage(nc, name) as s:
        islot = s.sb("islot", [P, 2, G], I32)
        rows = s.sb("rows", [P, 2, G, w])
        s_turn, s_idx, s_kept = s.sem("turn"), s.sem("idx"), s.sem("kept")
        s_rows = [s.sem("rows0"), s.sem("rows1")]
        block = s.ctx.enter_context(nc.Block())

        @block.gpsimd
        def _(pool):
            gather_chunks(nc, pool, C, s_turn, [(table, last, idx, islot, rows, s_rows, s_idx)], [(s_kept, 1)])

        @block.vector
        def _(dve):
            dve.sem_inc(s_kept, 2)
            for i in turns_from_zero(dve, C // 2):
                for h in range(2):
                    dve.wait_ge(s_rows[h], i * (16 * G) + 16 * G)
                    nc.vector.tensor_copy(out[:, ds((i * 2 + h) * G, G), :], rows[:, h, :, :]).then_inc(s_kept, 1)


def attention_scores(nc, name, A, layer, T, N, HH, srcS, dstS, ident, srel, score, hdst, ptrS):
    C = T // G
    UNITS = G // 2
    with Stage(nc, name) as s:
        islot0 = s.sb("islot0", [P, 2, G], I32)
        islot1 = s.sb("islot1", [P, 2, G], I32)
        rs = s.sb("rs", [P, 2, G, ROW])
        rd = s.sb("rd", [P, 2, G, ROW])
        xT = s.sb("xT", [D, 2, 4 * P])
        w = s.sb("w", [D, 2, P])
        att = s.sb("att", [P, 2, P])
        th = s.sb("th", [P, 2, 2, 2 * P])
        prod = s.sb("prod", [P, 2, 2 * P])
        s4 = s.sb("s4", [P, G, 4])
        s2 = s.sb("s2", [P, G, 2])
        psX = [s.ps(f"psX{k}", [D, 4, P]) for k in range(2)]
        psS = [s.ps(f"psS{k}", [P, 2, 2, P]) for k in range(2)]
        s_w, s_turn, s_pturn, s_idx0, s_idx1, s_kept, s_xt, s_xc, s_mm, s_th, s_prod, s_dve = (s.sem(k) for k in (
            "w", "turn", "pturn", "idx0", "idx1", "kept", "xt", "xc", "mm", "th", "prod", "dve"))
        s_rs = [s.sem("rs0"), s.sem("rs1")]
        s_rd = [s.sem("rd0"), s.sem("rd1")]
        block = s.ctx.enter_context(nc.Block())

        @block.sync
        def _(sp):
            for n, k in enumerate(("h", "t")):
                sp.dma_start(w[:, n, :], A[f"L1_gnn_W_{k}"][layer]).then_inc(s_w, 16)
                spread_rows(sp, att[:, n, :], A[f"L1_gnn_att_{k}"][layer].rearrange("h d -> (h d)"), s_w)

        @block.gpsimd
        def _(pool):
            gather_chunks(nc, pool, C, s_turn, [(HH, N - 1, srcS, islot0, rs, s_rs, s_idx0),
                                                (HH, N - 1, dstS, islot1, rd, s_rd, s_idx1)],
                          [(s_xt, UNITS), (s_kept, 2)])

        @block.tensor
        def _(pe):
            pe.wait_ge(s_w, 64)
            pe.sem_inc(s_xt, 2 * UNITS)
            pe.sem_inc(s_mm, 2)
            for i in turns_from_zero(pe, C // 2):
                def products(v):
                    k = i * (2 * UNITS) + v
                    hold(pe, s_xc, k + 3, s_pturn)
                    hold(pe, s_th, k + 1, s_pturn)
                    for g in range(2):
                        for n in range(2):
                            at = (g * 2 + n) * P
                            ins = nc.tensor.matmul(psS[v % 2][:, g, n, :], xT[:, v % 2, at:at + P], w[:, n, :],
                                                   start=True, stop=True)
                    ins.then_inc(s_mm, 1)

                for v in range(2 * UNITS):
                    h, u = divmod(v, UNITS)
                    if u == 0:
                        hold(pe, s_rs[h], i * (16 * G) + 16 * G, s_pturn)
                        hold(pe, s_rd[h], i * (16 * G) + 16 * G, s_pturn)
                    hold(pe, s_xc, i * (2 * UNITS) + (v + 1), s_pturn)
                    for g in range(2):
                        for n, rows in enumerate((rs, rd)):
                            ins = nc.tensor.transpose(psX[v % 2][:, g * 2 + n, :], rows[:, h, 2 * u + g, 0:D], ident[:, :])
                    ins.then_inc(s_xt, 1)
                    if v:
                        products(v - 1)
                products(2 * UNITS - 1)

        @block.scalar
        def _(act):
            act.sem_inc(s_xc, 2)
            act.sem_inc(s_th, 2)
            for i in turns_from_zero(act, C // 2):
                for v in range(2 * UNITS):
                    k = i * (2 * UNITS) + v
                    act.wait_ge(s_xt, k + (2 * UNITS + 1))
                    act.wait_ge(s_mm, k + 1)
                    nc.scalar.activation(xT[:, v % 2, :], psX[v % 2][:, :, :].rearrange("k n p -> k (n p)"),
                                         ACT.Copy).then_inc(s_xc, 1)
                    act.wait_ge(s_mm, k + 3)
                    act.wait_ge(s_prod, k + 1)
                    nc.scalar.activation(th[:, v % 2, :, :], psS[v % 2][:, :, :, :].rearrange("p g n d -> p g (n d)"),
                                         ACT.Tanh).then_inc(s_th, 1)

        @block.vector
        def _(dve):
            dve.wait_ge(s_w, 64)
            dve.sem_inc(s_kept, 4)
            dve.sem_inc(s_prod, 2)
            for i in turns_from_zero(dve, C // 2):
                for h in range(2):
                    sl = Steps(dve, s_dve, UNITS + 3, i * 2 + h)
                    at = ds((i * 2 + h) * G, G)
                    dve.wait_ge(s_rd[h], i * (16 * G) + 16 * G)
                    nc.vector.tensor_copy(hdst[:, at, :], rd[:, h, :, 0:D]).then_inc(s_kept, 1)
                    nc.vector.tensor_copy(ptrS[:, at], rd[:, h, :, D]).then_inc(s_kept, 1)
                    for u in range(UNITS):
                        v = h * UNITS + u
                        k = i * (2 * UNITS) + v
                        dve.wait_ge(s_th, k + 3)
                        sl.wait()
                        nc.vector.tensor_tensor(prod[:, :, :], th[:, v % 2, :, :],
                                                bcast(att[:, :, :].rearrange("p n d -> p (n d)"), 1, 2),
                                                ALU.mult).then_inc(s_prod, 1)
                        dve.wait_ge(s_prod, k + 3)
                        sl.did(nc.vector.tensor_reduce(
                            s4[:, 2 * u:2 * u + 2, :], prod[:, :, :].rearrange("p g (q d) -> p g q d", d=D), AX.X, ALU.add))
                    sl.wait()
                    sl.link(nc.vector.tensor_tensor(s2[:, :, :], s4[:, :, 0:2], s4[:, :, 2:4], ALU.add))
                    sl.link(nc.vector.tensor_tensor(s2[:, :, :], s2[:, :, :], srel[:, at, 2 * layer:2 * layer + 2], ALU.add))
                    sl.link(nc.vector.scalar_tensor_tensor(score[:, at, :], s2[:, :, :], 0.01, s2[:, :, :],
                                                           ALU.mult, ALU.max))


def segment_softmax(nc, name, T, tab, ident, score, weight, rz, factor, W=2, floor=None):
    with Stage(nc, name) as s:
        top = s.sb("top", [P, T, W])
        end = s.sb("end", [P, W])
        carry = s.sb("carry", [P, W])
        tmp = s.sb("tmp", [P, T, W])

        def vector_block(tag, program):
            with Stage(nc, f"{name}_{tag}") as q:
                s_dve = q.sem("dve")
                block = q.ctx.enter_context(nc.Block())

                @block.vector
                def _(dve):
                    program(dve, Steps(dve, s_dve))

        def forward_max(dve, st):
            for w in range(W):
                st.did(nc.vector.tensor_tensor_scan(top[:, :, w], tab["neg"][:, :], score[:, :, w], NEG, ALU.add, ALU.max))
            st.wait()
            st.link(nc.vector.tensor_copy(end[:, :], top[:, T - 1, :]))

        def backward_max(dve, st):
            for w in range(W):
                st.did(nc.vector.tensor_scalar(tmp[:, :, w], tab["negpre"][:, :], carry[:, w:w + 1], None, ALU.add))
            st.wait()
            st.link(nc.vector.tensor_tensor(tmp[:, :, :], tmp[:, :, :], top[:, :, :], ALU.max))
            for w in range(W):
                st.did(nc.vector.tensor_tensor_scan(top[:, T - 1::-1, w], tab["negback"][:, T - 1::-1],
                                                    tmp[:, T - 1::-1, w], NEG, ALU.add, ALU.max))
            st.wait()
            st.link(nc.vector.tensor_copy(end[:, :], top[:, 0, :]))

        def less_max(dve, st):
            for w in range(W):
                st.did(nc.vector.tensor_scalar(tmp[:, :, w], tab["negpost"][:, :], carry[:, w:w + 1], None, ALU.add))
            st.wait()
            st.link(nc.vector.tensor_tensor(top[:, :, :], tmp[:, :, :], top[:, :, :], ALU.max))
            if floor is not None:
                st.link(nc.vector.tensor_tensor(top[:, :, :], top[:, :, :], floor, ALU.max))
                st.link(nc.vector.tensor_copy(floor, top[:, :, :]))
            st.link(nc.vector.tensor_tensor(tmp[:, :, :], score[:, :, :], top[:, :, :], ALU.subtract))

        def sums(dve, st):
            for w in range(W):
                st.did(nc.vector.tensor_tensor_scan(top[:, :, w], tab["keep"][:, :], weight[:, :, w], 0.0, ALU.mult, ALU.add))
            st.wait()
            st.link(nc.vector.tensor_copy(end[:, :], top[:, T - 1, :]))

        def inverse(dve, st):
            for w in range(W):
                st.did(nc.vector.tensor_scalar(tmp[:, :, w], tab["pre"][:, :], carry[:, w:w + 1], None, ALU.mult))
            st.wait()
            st.link(nc.vector.tensor_tensor(top[:, :, :], tmp[:, :, :], top[:, :, :], ALU.add))
            if factor is None:
                st.link(nc.vector.tensor_copy(rz[:, :, :], top[:, :, :]))
                return
            st.link(nc.vector.tensor_scalar(top[:, :, :], top[:, :, :], 1e-30, None, ALU.max))
            st.link(nc.vector.reciprocal(top[:, :, :], top[:, :, :]))
            st.link(nc.vector.tensor_scalar(rz[:, :, :], top[:, :, :], factor, None, ALU.mult))

        vector_block("fmax", forward_max)
        carry_over(nc, f"{name}_cf", end[:, :], tab["negpre"][:, T - 1:T], ident, W, "max", carry[:, :])
        vector_block("bmax", backward_max)
        carry_over(nc, f"{name}_cb", end[:, :], tab["negpost"][:, 0:1], ident, W, "max", carry[:, :], back=True)
        vector_block("less", less_max)
        with Stage(nc, f"{name}_exp") as q:
            s_e = q.sem("e")
            block = q.ctx.enter_context(nc.Block())

            @block.scalar
            def _(act):
                nc.scalar.activation(weight[:, :, :], tmp[:, :, :], ACT.Exp).then_inc(s_e, 1)
                act.wait_ge(s_e, 1)
        vector_block("sums", sums)
        carry_over(nc, f"{name}_cs", end[:, :], tab["pre"][:, T - 1:T], ident, W, "sum", carry[:, :])
        vector_block("inv", inverse)


def attention_step(nc, name, T, tab, first, EG, ptrS, hdst, weight, state):
    C = T // G
    with Stage(nc, name) as s:
        islot = s.sb("islot", [P, 2, G], I32)
        rows = s.sb("rows", [P, 2, G, 2 * D])
        s_turn, s_idx, s_used, s_dve = s.sem("turn"), s.sem("idx"), s.sem("used"), s.sem("dve")
        s_rows = [s.sem("rows0"), s.sem("rows1")]
        block = s.ctx.enter_context(nc.Block())

        if not first:
            @block.gpsimd
            def _(pool):
                gather_chunks(nc, pool, C, s_turn, [(EG, P * T, ptrS, islot, rows, s_rows, s_idx)], [(s_used, 1)])

        @block.vector
        def _(dve):
            nc.vector.memset(state[:, 0, :], 0.0).then_inc(s_used, 1)
            dve.wait_ge(s_used, 1)
            dve.sem_inc(s_used, 1)
            for i in turns_from_zero(dve, C // 2):
                for h in range(2):
                    sl = Steps(dve, s_dve, (2 if first else 4) + G, i * 2 + h)
                    j = i * 2 + h
                    at = ds(j * G, G)
                    if not first:
                        dve.wait_ge(s_rows[h], i * (16 * G) + 16 * G)
                    r = rows[:, h, :, :].rearrange("p g (h d) -> p g h d", h=2)
                    for hd in range(2):
                        if not first:
                            sl.did(nc.vector.scalar_tensor_tensor(r[:, :, hd, :], hdst[:, at, :], 0.15, r[:, :, hd, :],
                                                                  ALU.mult, ALU.add))
                    if not first:
                        sl.wait()
                    for hd in range(2):
                        z = hdst[:, at, :] if first else r[:, :, hd, :]
                        sl.did(nc.vector.tensor_tensor(r[:, :, hd, :], z, bcast(weight[:, at, hd], 2, D), ALU.mult))
                    sl.wait()
                    for g in range(G):
                        t = j * G + g
                        ins = nc.vector.scalar_tensor_tensor(
                            state[:, ds(t + 1, 1), :].rearrange("p a d -> p (a d)"),
                            state[:, ds(t, 1), :].rearrange("p a d -> p (a d)"),
                            tab["keep"][:, ds(t, 1)], rows[:, h, g, :], ALU.mult, ALU.add)
                        sl.link(ins)
                    dve.sem_inc(s_used, 1)


def attention_share(nc, name, T, tab, carry, state, rz, EG):
    C = T // G
    with Stage(nc, name) as s:
        rslot = s.sb("rslot", [P, 2, G, 2 * D])
        zero = s.sb("zero", [1, 2 * D])
        s_dve, s_ready, s_z, s_zo = s.sem("dve"), s.sem("ready"), s.sem("z"), s.sem("zo")
        s_out = [s.sem("out0"), s.sem("out1")]
        block = s.ctx.enter_context(nc.Block())
        v = EG[1:P * T + 1, :].rearrange("(p t) d -> p t d", t=T)

        @block.sync
        def _(sp):
            sp.wait_ge(s_z, 1)
            sp.dma_start(EG[0:1, :], zero[:, :]).then_inc(s_zo, 16)
            for i in turns_from_zero(sp, C // 2):
                for h in range(2):
                    sp.wait_ge(s_ready, i * 2 + (h + 1))
                    sp.dma_start(v[:, ds((i * 2 + h) * G, G), :], rslot[:, h, :, :]).then_inc(s_out[h], 16)
            for h in range(2):
                sp.wait_ge(s_out[h], 16 * (C // 2))
            sp.wait_ge(s_zo, 16)

        @block.vector
        def _(dve):
            nc.vector.memset(zero[:, :], 0.0).then_inc(s_z, 1)
            for i in turns_from_zero(dve, C // 2):
                for h in range(2):
                    sl = Steps(dve, s_dve, G + 2, i * 2 + h)
                    dve.wait_ge(s_out[h], i * 16)
                    finish_sums(nc, sl, i * 2 + h, tab, carry, state, rslot[:, h, :, :])
                    for hd in range(2):
                        r = rslot[:, h, :, hd * D:(hd + 1) * D]
                        sl.did(nc.vector.tensor_tensor(r, r, bcast(rz[:, ds((i * 2 + h) * G, G), hd], 2, D), ALU.mult))
                    sl.wait()
                    dve.sem_inc(s_ready, 1)


def finish_sums(nc, sl, j, tab, carry, state, out, n=G):
    for g in range(n):
        t = j * n + g
        sl.did(nc.vector.scalar_tensor_tensor(out[:, g, :], carry[:, :], tab["pre"][:, ds(t, 1)],
                                              state[:, ds(t + 1, 1), :].rearrange("p a d -> p (a d)"),
                                              ALU.mult, ALU.add))
    sl.wait()


def attention_output(nc, name, A, layer, T, N, tab, carry, state, rz, ident, byS):
    C = T // G
    HG = G // 2
    with Stage(nc, name) as s:
        share = s.sb("share", [P, 2, HG, 2 * D])
        shareT = s.sb("shareT", [P, 2, HG, P])
        rslot = s.sb("rslot", [P, 2, G, D])
        islot = s.sb("islot", [P, 2, G], I32)
        wo = s.sb("wo", [P, D])
        psX = [s.ps(f"psX{k}", [P, 4, P]) for k in range(4)]
        psO = [s.ps(f"psO{k}", [P, HG, D]) for k in range(2)]
        s_w, s_dve, s_share, s_xt, s_xc, s_mm, s_res, s_turn, s_pturn, s_ready = (s.sem(k) for k in (
            "w", "dve", "share", "xt", "xc", "mm", "res", "turn", "pturn", "ready"))
        s_sent = [s.sem("sent0"), s.sem("sent1")]
        block = s.ctx.enter_context(nc.Block())
        CUT = ((0, 4), (4, HG))

        @block.sync
        def _(sp):
            sp.dma_start(wo[:, :], A["L1_gnn_W_o"][layer]).then_inc(s_w, 16)

        @block.gpsimd
        def _(pool):
            scatter_chunks(nc, pool, C, s_turn, s_ready, byS, N - 1, islot, rslot, s_sent)

        @block.tensor
        def _(pe):
            pe.wait_ge(s_w, 16)
            pe.sem_inc(s_xt, 4)
            for i in turns_from_zero(pe, C // 2):
                for h in range(2):
                    j = i * 2 + h
                    for u in range(2):
                        k = j * 2 + u
                        hold(pe, s_share, k + 1, s_pturn)
                        for b, (t0, t1) in enumerate(CUT):
                            hold(pe, s_xc, k * 2 + (b + 1), s_pturn)
                            for t in range(t0, t1):
                                ins = nc.tensor.transpose(psX[2 * u + b][:, t - t0, :], share[:, u, t, :], ident[:, :])
                            ins.then_inc(s_xt, 1)
                        hold(pe, s_xc, k * 2 + 6, s_pturn)
                        hold(pe, s_res, k + 1, s_pturn)
                        for t in range(HG):
                            ins = nc.tensor.matmul(psO[u][:, t, :], shareT[:, u, t, :], wo[:, :], start=True, stop=True)
                        ins.then_inc(s_mm, 1)

        @block.scalar
        def _(act):
            act.sem_inc(s_xc, 4)
            for i in turns_from_zero(act, C // 2):
                for h in range(2):
                    for u in range(2):
                        k = (i * 2 + h) * 2 + u
                        act.wait_ge(s_res, k + 1)
                        for b, (t0, t1) in enumerate(CUT):
                            act.wait_ge(s_xt, k * 2 + (b + 5))
                            nc.scalar.activation(shareT[:, u, t0:t1, :], psX[2 * u + b][:, 0:t1 - t0, :], ACT.Copy).then_inc(s_xc, 1)

        @block.vector
        def _(dve):
            dve.sem_inc(s_res, 2)
            for i in turns_from_zero(dve, C // 2):
                for h in range(2):
                    j = i * 2 + h
                    sl = Steps(dve, s_dve, G + 5, j)
                    for u in range(2):
                        k = j * 2 + u
                        dve.wait_ge(s_xt, k * 2 + 2)
                        finish_sums(nc, sl, k, tab, carry, state, share[:, u, :, :], HG)
                        for hd in range(2):
                            r = share[:, u, :, hd * D:(hd + 1) * D]
                            sl.did(nc.vector.tensor_tensor(r, r, bcast(rz[:, ds(k * HG, HG), hd], 2, D), ALU.mult))
                        sl.wait()
                        dve.sem_inc(s_share, 1)
                    dve.wait_ge(s_sent[h], i * (16 * G))
                    sl.did(nc.vector.tensor_copy(islot[:, h, :], tab["endrow"][:, ds(j * G, G)]))
                    for u in range(2):
                        k = j * 2 + u
                        dve.wait_ge(s_mm, k + 1)
                        nc.vector.tensor_copy(rslot[:, h, u * HG:(u + 1) * HG, :], psO[u][:, :, :]).then_inc(s_res, 1)
                    dve.wait_ge(s_res, j * 2 + 4)
                    sl.wait()
                    dve.sem_inc(s_ready, 1)




def degree_factors(nc, T, NC, countD, countN, rdegD, dD, dN):
    with Stage(nc, "deg") as s:
        mN = s.sb("mN", [P, NC * U])
        s_dve, s_root = s.sem("dve"), s.sem("root")
        block = s.ctx.enter_context(nc.Block())

        @block.vector
        def _(dve):
            st = Steps(dve, s_dve)
            st.link(nc.vector.tensor_scalar(mN[:, :], countN[:, :], 1.0, None, ALU.max))
            st.link(nc.vector.reciprocal(rdegD[:, :], countD[:, :]))
            st.link(nc.vector.reciprocal(mN[:, :], mN[:, :]))

        @block.scalar
        def _(act):
            act.wait_ge(s_dve, 3)
            nc.scalar.activation(dD[:, :], rdegD[:, :], ACT.Sqrt).then_inc(s_root, 1)
            nc.scalar.activation(dN[:, :], mN[:, :], ACT.Sqrt).then_inc(s_root, 1)
            act.wait_ge(s_root, 2)


def running_sums(nc, name, T, tab, table, last, idx, state, weight=None, rows_in=None):
    C = T // G
    with Stage(nc, name) as s:
        islot = s.sb("islot", [P, 2, G], I32)
        rows = s.sb("rows", [P, 2, G, D])
        s_turn, s_idx, s_used, s_dve = s.sem("turn"), s.sem("idx"), s.sem("used"), s.sem("dve")
        s_rows = [s.sem("rows0"), s.sem("rows1")]
        block = s.ctx.enter_context(nc.Block())

        if table is not None:
            @block.gpsimd
            def _(pool):
                gather_chunks(nc, pool, C, s_turn, [(table, last, idx, islot, rows, s_rows, s_idx)], [(s_used, 1)])

        @block.vector
        def _(dve):
            nc.vector.memset(state[:, 0, :], 0.0).then_inc(s_used, 1)
            dve.wait_ge(s_used, 1)
            dve.sem_inc(s_used, 1)
            for i in turns_from_zero(dve, C // 2):
                for h in range(2):
                    j = i * 2 + h
                    sl = Steps(dve, s_dve, G + (1 if weight is not None else 0), j)
                    if table is not None:
                        dve.wait_ge(s_rows[h], i * (16 * G) + 16 * G)
                    if weight is not None:
                        at = ds(j * G, G)
                        sl.link(nc.vector.tensor_tensor(rows[:, h, :, :], rows_in[:, at, :],
                                                        bcast(weight[:, at], 2, D), ALU.mult))
                    for g in range(G):
                        t = j * G + g
                        sl.link(nc.vector.scalar_tensor_tensor(
                            state[:, ds(t + 1, 1), :].rearrange("p a d -> p (a d)"),
                            state[:, ds(t, 1), :].rearrange("p a d -> p (a d)"),
                            tab["keep"][:, ds(t, 1)], rows[:, h, g, :], ALU.mult, ALU.add))
                    dve.sem_inc(s_used, 1)


def degree_share(nc, name, T, tab, carry, state, rdegD, dD, acc, first, EG, byD, N):
    C = T // G
    with Stage(nc, name) as s:
        width = ROW if byD is not None else D
        rslot = s.sb("rslot", [P, 2, G, width])
        tmp = s.sb("tmp", [P, G, D])
        islot = s.sb("islot", [P, 2, G], I32)
        zero = s.sb("zero", [1, D])
        s_dve, s_ready, s_z, s_zo, s_turn = s.sem("dve"), s.sem("ready"), s.sem("z"), s.sem("zo"), s.sem("turn")
        s_out = [s.sem("out0"), s.sem("out1")]
        block = s.ctx.enter_context(nc.Block())

        if byD is None:
            @block.sync
            def _(sp):
                v = EG[1:P * T + 1, :].rearrange("(p t) d -> p t d", t=T)
                sp.wait_ge(s_z, 1)
                sp.dma_start(EG[0:1, :], zero[:, :]).then_inc(s_zo, 16)
                for i in turns_from_zero(sp, C // 2):
                    for h in range(2):
                        sp.wait_ge(s_ready, i * 2 + (h + 1))
                        sp.dma_start(v[:, ds((i * 2 + h) * G, G), :], rslot[:, h, :, :]).then_inc(s_out[h], 16)
                for h in range(2):
                    sp.wait_ge(s_out[h], 16 * (C // 2))
                sp.wait_ge(s_zo, 16)
        else:
            @block.gpsimd
            def _(pool):
                scatter_chunks(nc, pool, C, s_turn, s_ready, byD, N - 1, islot, rslot, s_out)

        @block.vector
        def _(dve):
            nc.vector.memset(zero[:, :], 0.0).then_inc(s_z, 1)
            step = 16 if byD is None else 16 * G
            for i in turns_from_zero(dve, C // 2):
                for h in range(2):
                    j = i * 2 + h
                    at = ds(j * G, G)
                    sl = Steps(dve, s_dve, G + (1 if first else 2) + (1 if byD is None else 3), j)
                    dve.wait_ge(s_out[h], i * step)
                    r = rslot[:, h, :, 0:D]
                    finish_sums(nc, sl, j, tab, carry, state, r)
                    if first:
                        sl.link(nc.vector.tensor_tensor(acc[:, at, :], r, bcast(dD[:, at], 2, D), ALU.mult))
                    else:
                        sl.link(nc.vector.tensor_tensor(tmp[:, :, :], r, bcast(dD[:, at], 2, D), ALU.mult))
                        into = acc[:, at, :] if byD is None else r
                        sl.link(nc.vector.tensor_tensor(into, acc[:, at, :], tmp[:, :, :], ALU.add))
                    if byD is None:
                        sl.link(nc.vector.tensor_tensor(r, r, bcast(rdegD[:, at], 2, D), ALU.mult))
                    else:
                        sl.did(nc.vector.tensor_copy(rslot[:, h, :, D], tab["pos1"][:, at]))
                        sl.did(nc.vector.tensor_copy(rslot[:, h, :, D + 1], tab["count"][:, at]))
                        sl.link(nc.vector.tensor_copy(islot[:, h, :], tab["endrow"][:, at]))
                    dve.sem_inc(s_ready, 1)



EW = D + 2 + 8 + 1


def turns(eng, NU):
    yield 0, 0, None, 0
    pairs = (NU - 1) // 2
    for i in turns_from_zero(eng, pairs):
        for h in (1, 0):
            k = i * 2 + (2 - h)
            yield k, h, k - 1, 1 - h
    if (NU - 1) % 2:
        yield NU - 1, (NU - 1) % 2, NU - 2, (NU - 2) % 2
    yield None, 0, NU - 1, (NU - 1) % 2


def edge_network(nc, name, A, n, NU, N, NC, T, ident, logits, nodes=None, edges=None):
    with Stage(nc, name) as s:
        W1a = s.sb("W1a", [D + 1, D])
        W1b = s.sb("W1b", [EW if edges else D, D])
        W2 = s.sb("W2", [D + 1, D])
        W2b = s.sb("W2b", [D + 1, D])
        g1 = s.sb("g1", [D, 1])
        be1 = s.sb("be1", [D, 1])
        b2 = s.sb("b2", [1, D])
        b2r = s.sb("b2r", [1, D])
        g2 = s.sb("g2", [P, D])
        be2 = s.sb("be2", [P, D])
        w3 = s.sb("w3", [P, D])
        gw = s.sb("gw", [P, D])
        bw = s.sb("bw", [P, D])
        b3 = s.sb("b3", [P, 1])
        c3 = s.sb("c3", [P, 1])
        eps = s.sb("eps", [P, 1])
        norm1 = Norm(s, "norm1", n, eps)
        norm2 = Norm(s, "norm2", n, eps)
        r1 = s.sb("r1", [P, n, D])
        r2 = s.sb("r2", [P, n, D])
        h1 = s.sb("h1", [P, 2, n, D])
        dot = s.sb("dot", [P, n])
        aT = s.sb("aT", [D + 1, 2, n * P])
        hT = s.sb("hT", [D + 1, 2, n * P])
        BANKS = ((0, 4), (4, n))
        psA = [s.ps(f"psA{k}", [D, 4 * P]) for k in range(2)]
        psH = [s.ps(f"psH{k}", [D, 4 * P]) for k in range(2)]
        ps1 = s.ps("ps1", [P, 8, D])
        ps2 = s.ps("ps2", [P, 8, D])
        if edges:
            rowsQ, src, dst, attr, qs, own = edges
            ra = s.sb("ra", [P, 2, n, ROW])
            rb = s.sb("rb", [P, 2, n, EW])
            bT = s.sb("bT", [EW, 2, n * P])
            islot0 = s.sb("islot0", [P, 2, n], I32)
            islot1 = s.sb("islot1", [P, 2, n], I32)
            psB = [s.ps(f"psB{k}", [EW, 4 * P]) for k in range(2)]
        else:
            ra = s.sb("ra", [P, 2, n, D])
        (s_w, s_mem, s_w2, s_b2, s_dve, s_turn, s_pturn, s_idx0, s_idx1, s_kept, s_at, s_bt, s_ht, s_ac, s_hc,
         s_m1, s_m2, s_r1, s_r2, s_c1, s_c2, s_h1, s_v1, s_v2, s_d1, s_d2, s_log) = (s.sem(k) for k in (
             "w", "mem", "w2", "b2", "dve", "turn", "pturn", "idx0", "idx1", "kept", "at", "bt", "ht", "ac", "hc",
             "m1", "m2", "r1", "r2", "c1", "c2", "h1", "v1", "v2", "d1", "d2", "log"))
        s_ra = [s.sem("ra0"), s.sem("ra1")]
        s_rb = [s.sem("rb0"), s.sem("rb1")]
        block = s.ctx.enter_context(nc.Block())
        got = 16 * n if edges else 16
        n_w = 12 if edges else 11
        copies = 4 if edges else 2
        row = lambda v: v.rearrange("(a n) -> a n", a=1)

        @block.sync
        def _(sp):
            sp.wait_ge(s_mem, 2)
            w = A["L3_gnn_W1"]
            sp.dma_start(W1a[0:D, :], w[0:D, :]).then_inc(s_w, 16)
            sp.dma_start(W1b[0:D, :], w[D:2 * D, :]).then_inc(s_w, 16)
            if edges:
                sp.dma_start(W1b[D + 2:EW - 1, :], w[2 * D:2 * D + 8, :]).then_inc(s_w, 16)
                sp.dma_start(W1b[EW - 1:EW, :], row(A["L3_gnn_b1"])).then_inc(s_w, 16)
            else:
                sp.dma_start(W1a[D:D + 1, :], row(A["L3_gnn_b1"])).then_inc(s_w, 16)
            sp.dma_start(W2[0:D, :], A["L3_gnn_W2"]).then_inc(s_w, 16)
            sp.dma_start(b2[:, :], row(A["L3_gnn_b2"])).then_inc(s_w, 16)
            sp.dma_start(g1[:, :], A["L3_gnn_g1"].rearrange("(n a) -> n a", a=1)).then_inc(s_w, 16)
            sp.dma_start(be1[:, :], A["L3_gnn_be1"].rearrange("(n a) -> n a", a=1)).then_inc(s_w, 16)
            spread_rows(sp, g2[:, :], A["L3_gnn_g2"], s_w)
            spread_rows(sp, be2[:, :], A["L3_gnn_be2"], s_w)
            spread_rows(sp, w3[:, :], A["L3_gnn_W3"].rearrange("n a -> (n a)"), s_w)
            spread_rows(sp, b3[:, :], A["L3_gnn_b3"], s_w)
            if not edges:
                for c, h, i, last in node_chunks(sp, NC):
                    sp.wait_ge(s_at, c * 2 + 2)
                    v, _ = chunk_rows(nodes, c, False, N)
                    sp.dma_start(ra[:, h].rearrange("p u d -> p (u d)"), v).then_inc(s_ra[h], 16)

        if edges:
            @block.gpsimd
            def _(pool):
                gather_chunks(nc, pool, NU, s_turn, [(rowsQ, N - 1, src, islot0, ra, s_ra, s_idx0),
                                                     (rowsQ, N - 1, dst, islot1, rb, s_rb, s_idx1)],
                              [(s_at, 2), (s_bt, 2), (s_kept, 2)], n)

        def rows_value(k, h):
            return (k - h) * (got // 2) + got

        @block.tensor
        def _(pe):
            pe.wait_ge(s_w, 16 * n_w)
            pe.wait_ge(s_mem, 5)
            nc.tensor.matmul(ps2[0:1, 0, :], be1[:, :], W2[0:D, :], start=True, stop=True).then_inc(s_b2, 1)
            pe.wait_ge(s_w2, 1)
            pe.sem_inc(s_at, 4)
            pe.sem_inc(s_bt, 4)
            for k, h, m, g in turns(pe, NU):
                if k is not None:
                    hold(pe, s_ra[h], rows_value(k, h), s_pturn)
                    if edges:
                        hold(pe, s_rb[h], rows_value(k, h), s_pturn)
                        hold(pe, s_kept, k * 2 + 6, s_pturn)
                    for b, (t0, t1) in enumerate(BANKS):
                        hold(pe, s_ac, k * copies + (b + 1), s_pturn)
                        for t in range(t0, t1):
                            ins = nc.tensor.transpose(psA[b][:, (t - t0) * P:(t - t0 + 1) * P], ra[:, h, t, 0:D], ident[:, :])
                        ins.then_inc(s_at, 1)
                    if edges:
                        for b, (t0, t1) in enumerate(BANKS):
                            hold(pe, s_ac, k * copies + (b + 3), s_pturn)
                            for t in range(t0, t1):
                                ins = nc.tensor.transpose(psB[b][:, (t - t0) * P:(t - t0 + 1) * P], rb[:, h, t, :], ident[:, :])
                            ins.then_inc(s_bt, 1)
                    hold(pe, s_ac, k * copies + 2 * copies, s_pturn)
                    hold(pe, s_r1, k + 1, s_pturn)
                    for t in range(n):
                        at = slice(t * P, (t + 1) * P)
                        if edges:
                            nc.tensor.matmul(ps1[:, t, :], aT[0:D, h, at], W1a[0:D, :], start=True, stop=False)
                            ins = nc.tensor.matmul(ps1[:, t, :], bT[:, h, at], W1b[:, :], start=False, stop=True)
                        else:
                            nc.tensor.matmul(ps1[:, t, :], aT[:, h, at], W1a[:, :], start=True, stop=False)
                            ins = nc.tensor.matmul(ps1[:, t, :], aT[0:D, h, at], W1b[:, :], start=False, stop=True)
                    ins.then_inc(s_m1, 1)
                if m is not None:
                    hold(pe, s_h1, m + 1, s_pturn)
                    for b, (t0, t1) in enumerate(BANKS):
                        hold(pe, s_hc, m * 2 + (b + 1), s_pturn)
                        for t in range(t0, t1):
                            ins = nc.tensor.transpose(psH[b][:, (t - t0) * P:(t - t0 + 1) * P], h1[:, g, t, :], ident[:, :])
                        ins.then_inc(s_ht, 1)
                    hold(pe, s_hc, m * 2 + 4, s_pturn)
                    hold(pe, s_r2, m + 1, s_pturn)
                    for t in range(n):
                        ins = nc.tensor.matmul(ps2[:, t, :], hT[:, g, t * P:(t + 1) * P], W2b[:, :], start=True, stop=True)
                    ins.then_inc(s_m2, 1)

        @block.scalar
        def _(act):
            act.wait_ge(s_mem, 5)
            act.sem_inc(s_ac, copies)
            act.sem_inc(s_hc, 2)
            act.sem_inc(s_r1, 1)
            act.sem_inc(s_r2, 1)
            for k, h, m, g in turns(act, NU):
                if k is not None:
                    if not isinstance(k, int) or k > 1:
                        act.wait_ge(s_m1, k - 1)
                    for b, (t0, t1) in enumerate(BANKS):
                        act.wait_ge(s_at, k * 2 + (b + 5))
                        nc.scalar.activation(aT[0:D, h, t0 * P:t1 * P], psA[b][:, 0:(t1 - t0) * P], ACT.Copy).then_inc(s_ac, 1)
                    if edges:
                        for b, (t0, t1) in enumerate(BANKS):
                            act.wait_ge(s_bt, k * 2 + (b + 5))
                            nc.scalar.activation(bT[:, h, t0 * P:t1 * P], psB[b][:, 0:(t1 - t0) * P], ACT.Copy).then_inc(s_ac, 1)
                    act.wait_ge(s_m1, k + 1)
                    act.wait_ge(s_c1, k)
                    nc.scalar.activation(r1[:, :, :], ps1[:, 0:n, :], ACT.Relu).then_inc(s_r1, 1)
                if m is not None:
                    for b, (t0, t1) in enumerate(BANKS):
                        act.wait_ge(s_ht, m * 2 + (b + 1))
                        nc.scalar.activation(hT[0:D, g, t0 * P:t1 * P], psH[b][:, 0:(t1 - t0) * P], ACT.Copy).then_inc(s_hc, 1)
                    act.wait_ge(s_m2, m + 1)
                    act.wait_ge(s_c2, m)
                    nc.scalar.activation(r2[:, :, :], ps2[:, 0:n, :], ACT.Relu).then_inc(s_r2, 1)
                if k is not None:
                    act.wait_ge(s_v1, k + 1)
                    norm1.root(nc, s_d1)
                if m is not None:
                    act.wait_ge(s_v2, m + 1)
                    norm2.root(nc, s_d2)

        @block.vector
        def _(dve):
            st = Steps(dve, s_dve)
            nc.vector.memset(W1b[:, :], 0.0).then_inc(s_mem, 1)
            nc.vector.memset(W1a[:, :], 0.0).then_inc(s_mem, 1)
            nc.vector.memset(eps[:, :], 1e-6).then_inc(s_mem, 1)
            nc.vector.memset(aT[D:D + 1, :, :], 1.0).then_inc(s_mem, 1)
            nc.vector.memset(hT[D:D + 1, :, :], 1.0).then_inc(s_mem, 1)
            dve.sem_inc(s_kept, 4)
            if edges:
                nc.vector.memset(rb[:, :, :, EW - 1], 1.0).then_inc(s_log, 1)
                dve.wait_ge(s_log, 1)
            dve.wait_ge(s_w, 16 * n_w)
            st.did(nc.vector.tensor_scalar(W2b[0:D, :], W2[0:D, :], g1[:, 0:1], None, ALU.mult))
            st.did(nc.vector.tensor_tensor(gw[:, :], g2[:, :], w3[:, :], ALU.mult))
            st.link(nc.vector.tensor_tensor(bw[:, :], be2[:, :], w3[:, :], ALU.mult))
            st.link(nc.vector.tensor_reduce(c3[:, :], bw[:, :], AX.X, ALU.add))
            st.link(nc.vector.tensor_tensor(c3[:, :], c3[:, :], b3[:, :], ALU.add))
            dve.wait_ge(s_b2, 1)
            st.link(nc.vector.tensor_tensor(b2r[:, :], b2[:, :], ps2[0:1, 0, :], ALU.add))
            st.link(nc.vector.tensor_copy(W2b[D:D + 1, :], b2r[:, :]))
            dve.sem_inc(s_w2, 1)
            n0 = st.n

            def keep(k, h):
                if not edges:
                    return
                at = ds(k * n, n)
                dve.wait_ge(s_ra[h], rows_value(k, h))
                dve.wait_ge(s_rb[h], rows_value(k, h))
                nc.vector.tensor_copy(qs[:, at, :], ra[:, h, :, 0:D]).then_inc(s_kept, 1)
                nc.vector.tensor_copy(own[:, at], rb[:, h, :, D]).then_inc(s_log, 1)
                dve.wait_ge(s_log, k + 2)
                nc.vector.tensor_copy(rb[:, h, :, D + 2:EW - 1], attr[:, at, :]).then_inc(s_kept, 1)

            keep(0, 0)
            A_N, B_N = 5, 7
            for k, h, m, g in turns(dve, NU):
                if k is not None and m is not None:
                    sl = Steps(dve, s_dve, A_N + B_N, m, n0 + A_N)
                elif k is not None:
                    sl = Steps(dve, s_dve, 0, 0, n0)
                else:
                    sl = Steps(dve, s_dve, A_N + B_N, m, n0 + A_N)
                if k is not None:
                    if not (isinstance(k, int) and k == 0):
                        keep(k, h)
                    dve.wait_ge(s_r1, k + 2)
                    sl.link(nc.vector.tensor_reduce(norm1.sum[:, :], r1[:, :, :], AX.X, ALU.add))
                    sl.link(nc.vector.tensor_scalar(norm1.mean[:, :], norm1.sum[:, :], 1.0 / D, None, ALU.mult))
                    nc.vector.tensor_tensor(norm1.xc[:, :, :], r1[:, :, :], bcast(norm1.mean[:, :], 2, D), ALU.subtract).then_inc(s_c1, 1)
                    dve.wait_ge(s_c1, k + 1)
                    sl.link(nc.vector.tensor_tensor(norm1.sq[:, :, :], norm1.xc[:, :, :], norm1.xc[:, :, :], ALU.mult))
                    sl.did(nc.vector.tensor_reduce(norm1.var[:, :], norm1.sq[:, :, :], AX.X, ALU.add))
                    sl.wait()
                    dve.sem_inc(s_v1, 1)
                if m is not None:
                    dve.wait_ge(s_r2, m + 2)
                    sl.link(nc.vector.tensor_reduce(norm2.sum[:, :], r2[:, :, :], AX.X, ALU.add))
                    sl.link(nc.vector.tensor_scalar(norm2.mean[:, :], norm2.sum[:, :], 1.0 / D, None, ALU.mult))
                    nc.vector.tensor_tensor(norm2.xc[:, :, :], r2[:, :, :], bcast(norm2.mean[:, :], 2, D), ALU.subtract).then_inc(s_c2, 1)
                    dve.wait_ge(s_c2, m + 1)
                    sl.link(nc.vector.tensor_tensor(norm2.sq[:, :, :], norm2.xc[:, :, :], norm2.xc[:, :, :], ALU.mult))
                    nc.vector.tensor_reduce(norm2.var[:, :], norm2.sq[:, :, :], AX.X, ALU.add).then_inc(s_v2, 1)
                if k is not None:
                    dve.wait_ge(s_d1, k + 1)
                    sl.link(nc.vector.reciprocal(norm1.rstd[:, :], norm1.std[:, :]))
                    if not isinstance(k, int) or k > 1:
                        dve.wait_ge(s_ht, k * 2 - 2)
                    nc.vector.tensor_tensor(h1[:, h, :, :], norm1.xc[:, :, :], bcast(norm1.rstd[:, :], 2, D), ALU.mult).then_inc(s_h1, 1)
                if m is not None:
                    dve.wait_ge(s_v2, m + 1)
                    sl.link(nc.vector.tensor_tensor(norm2.sq[:, :, :], norm2.xc[:, :, :], bcast(gw[:, :], 1, n), ALU.mult))
                    sl.did(nc.vector.tensor_reduce(dot[:, :], norm2.sq[:, :, :], AX.X, ALU.add))
                    dve.wait_ge(s_d2, m + 1)
                    sl.link(nc.vector.reciprocal(norm2.rstd[:, :], norm2.std[:, :]))
                    sl.link(nc.vector.tensor_tensor(dot[:, :], dot[:, :], norm2.rstd[:, :], ALU.mult))
                    nc.vector.tensor_scalar(logits[:, ds(m * n, n)], dot[:, :], c3[:, 0:1], 0.0, ALU.add, ALU.max).then_inc(s_turn, 1)


def last_norm(nc, name, A, logits):
    n = logits.shape[1]
    with Stage(nc, name) as s:
        g3 = s.sb("g3", [P, 1])
        be3 = s.sb("be3", [P, 1])
        mean = s.sb("mean", [P, n])
        xc = s.sb("xc", [P, n])
        var = s.sb("var", [P, n])
        eps = s.sb("eps", [P, 1])
        s_w, s_dve, s_std = s.sem("w"), s.sem("dve"), s.sem("std")
        block = s.ctx.enter_context(nc.Block())

        @block.sync
        def _(sp):
            spread_rows(sp, g3[:, :], A["L3_gnn_g3"], s_w)
            spread_rows(sp, be3[:, :], A["L3_gnn_be3"], s_w)

        @block.scalar
        def _(act):
            act.wait_ge(s_dve, 4)
            nc.scalar.activation(var[:, :], var[:, :], ACT.Sqrt, bias=eps[:, :], scale=1.0).then_inc(s_std, 1)

        @block.vector
        def _(dve):
            st = Steps(dve, s_dve)
            st.did(nc.vector.memset(eps[:, :], 1e-6))
            st.link(nc.vector.tensor_scalar(mean[:, :], logits, 1.0, None, ALU.mult))
            st.link(nc.vector.tensor_tensor(xc[:, :], logits, mean[:, :], ALU.subtract))
            st.link(nc.vector.tensor_tensor(var[:, :], xc[:, :], xc[:, :], ALU.mult))
            dve.wait_ge(s_std, 1)
            dve.wait_ge(s_w, 32)
            st.link(nc.vector.reciprocal(var[:, :], var[:, :]))
            st.link(nc.vector.tensor_tensor(xc[:, :], xc[:, :], var[:, :], ALU.mult))
            st.link(nc.vector.tensor_scalar(logits, xc[:, :], g3[:, 0:1], be3[:, 0:1], ALU.mult, ALU.add))


def q_rows(nc, N, NC, q0, lN, Q):
    with Stage(nc, "qrows") as s:
        row = s.sb("row", [P, 2, U, ROW])
        q = s.sb("q", [P, 2, U, D])
        s_copied, s_turn = s.sem("copied"), s.sem("turn")
        s_in = [s.sem("in0"), s.sem("in1")]
        s_out = [s.sem("out0"), s.sem("out1")]
        block = s.ctx.enter_context(nc.Block())

        @block.sync
        def _(sp):
            for c, h, i, last in node_chunks(sp, NC):
                sp.wait_ge(s_copied, c * 3 + 3)
                v, _ = chunk_rows(q0, c, False, N)
                sp.dma_start(q[:, h].rearrange("p u d -> p (u d)"), v).then_inc(s_in[h], 16)

        @block.vector
        def _(dve):
            dve.sem_inc(s_copied, 6)
            for c, h, i, last in node_chunks(dve, NC):
                dve.wait_ge(s_in[h], i * 16 + 16)
                dve.wait_ge(s_out[h], i * 16)
                nc.vector.tensor_copy(row[:, h, :, 0:D], q[:, h, :, :]).then_inc(s_copied, 1)
                nc.vector.tensor_copy(row[:, h, :, D], lN[:, ds(c * U, U)]).then_inc(s_copied, 1)
                nc.vector.tensor_copy(row[:, h, :, D + 1], lN[:, ds(c * U, U)]).then_inc(s_copied, 1)

        @block.gpsimd
        def _(pool):
            for c, h, i, last in node_chunks(pool, NC):
                pool.wait_ge(s_copied, c * 3 + 9)
                pool.sem_inc(s_turn, 1)
                v, _ = chunk_rows(Q, c, False, N)
                pool.dma_start(v, row[:, h].rearrange("p u d -> p (u d)")).then_inc(s_out[h], 16)
            pool.wait_ge(s_out[0], 16 * ((NC + 1) // 2))
            pool.wait_ge(s_out[1], 16 * (NC // 2))


def scatter_attention(nc, T, N, tab, carry, state, zsum, top, byD):
    C = T // G
    with Stage(nc, "scatt") as s:
        rslot = s.sb("rslot", [P, 2, G, ROW])
        islot = s.sb("islot", [P, 2, G], I32)
        s_dve, s_ready, s_turn = s.sem("dve"), s.sem("ready"), s.sem("turn")
        s_out = [s.sem("out0"), s.sem("out1")]
        block = s.ctx.enter_context(nc.Block())

        @block.gpsimd
        def _(pool):
            scatter_chunks(nc, pool, C, s_turn, s_ready, byD, N - 1, islot, rslot, s_out)

        @block.vector
        def _(dve):
            for i in turns_from_zero(dve, C // 2):
                for h in range(2):
                    j = i * 2 + h
                    at = ds(j * G, G)
                    sl = Steps(dve, s_dve, G + 3, j)
                    dve.wait_ge(s_out[h], i * (16 * G))
                    finish_sums(nc, sl, j, tab, carry, state, rslot[:, h, :, 0:D])
                    sl.did(nc.vector.tensor_copy(rslot[:, h, :, D], zsum[:, at]))
                    sl.did(nc.vector.tensor_copy(rslot[:, h, :, D + 1], top[:, at]))
                    sl.link(nc.vector.tensor_copy(islot[:, h, :], tab["endrow"][:, at]))
                    dve.sem_inc(s_ready, 1)


def load_attributes(nc, A, E, T, attr):
    full, rest = E // T, E - E // T * T
    with Stage(nc, "attr") as s:
        s_mem, s_in = s.sem("mem"), s.sem("in")
        block = s.ctx.enter_context(nc.Block())

        @block.vector
        def _(dve):
            nc.vector.memset(attr[:, :, :], 0.0).then_inc(s_mem, 1)

        @block.sync
        def _(sp):
            sp.wait_ge(s_mem, 1)
            v = A["edge_attr_8"]
            sp.dma_start(attr[0:full, :, :], v[0:full * T, :].rearrange("(p t) f -> p t f", t=T)).then_inc(s_in, 16)
            if rest:
                sp.dma_start(attr[full:full + 1, 0:rest, :],
                             v[full * T:E, :].rearrange("(p t) f -> p t f", p=1)).then_inc(s_in, 16)
            sp.wait_ge(s_in, 32 if rest else 16)


TAB = ("keep", "keepback", "neg", "negback", "pre", "post", "negpre", "negpost", "count", "pos1")


def tables(nc, ctx, name, T):
    tab = {k: ctx.enter_context(nc.sbuf_tensor(f"{name}_{k}", [P, T], F32)) for k in TAB}
    for k in ("keyi", "src", "endrow"):
        tab[k] = ctx.enter_context(nc.sbuf_tensor(f"{name}_{k}", [P, T], I32))
    tab["ccount"] = ctx.enter_context(nc.sbuf_tensor(f"{name}_ccount", [P, 1], F32))
    return tab


def build(nc, A, out, N, E, T, upto=99):
    RETIRED.clear()
    NC = -(-N // (P * U))
    NP = NC * P * U
    dram = lambda name, shape, dt=F32: nc.dram_tensor(name, shape, dt).ap()
    sorted1 = dram("sorted1", (P * T, 4), I32)
    sorted2 = dram("sorted2", (P * T, 4), I32)
    byD = dram("byD", (NP, ROW))
    H = dram("H", (NP, ROW))
    with ExitStack() as ctx:
        sb = lambda name, shape, dt=F32: ctx.enter_context(nc.sbuf_tensor(name, shape, dt))
        ident = sb("ident", [P, P])
        upper = sb("upper", [P, P])
        ones = sb("ones", [P, P])
        rows0 = sb("rows0", [P, T, 4], I32)
        countN = sb("countN", [P, NC * U])
        tabD = tables(nc, ctx, "tabD", T)
        ptrD = sb("ptrD", [P, T], I32)
        setup(nc, A, N, E, T, tabD, ident, upper, ones, rows0)
        zero_fill(nc, "zero", [byD])
        segment_tables(nc, "segD", tabD["keyi"][:, :], None, T, ident, tabD)
        sort_pass(nc, "sort0", lambda sp, rows, sem: sp.dma_start(rows[:, :, :], rows0[:, :, :]).then_inc(sem, 16), 0, sorted1, T, ones, upper, 16)
        sort_pass(nc, "sort1", lambda sp, rows, sem: sp.dma_start(rows[:, :, :], sorted1.rearrange("(p t) f -> p t f", t=T)).then_inc(sem, 16), 1, sorted2, T, ones, upper, 16)
        if upto < 1: return
        with ExitStack() as c0:
            basisT = c0.enter_context(nc.sbuf_tensor("basisT", [3 * KK, (T + 1) * P], BF16))
            agg = c0.enter_context(nc.sbuf_tensor("aggmax", [P, T + 1, D], F32))
            carry = c0.enter_context(nc.sbuf_tensor("carry", [P, D], F32))
            basis_tables(nc, A, E, T, basisT, ident)
            if upto < 2: return
            for layer in range(2):
                table, width = ((A["x"], D), (H, ROW))[layer]
                spline_messages(nc, f"spline{layer}", A[f"L0_gnn_W{layer + 1}"], table, width, N, T, tabD,
                                basisT, ident, agg, ptrD if layer else None)
                carry_over(nc, f"scarry{layer}", agg[:, T, :], tabD["negpre"][:, T - 1:T], ident, D, "max", carry[:, :])
                scatter_ends(nc, f"sends{layer}", T, tabD, carry, agg, "max", byD, N)
                if layer == 0:
                    node_hidden(nc, "hidden", A, byD, H, N, NC, ident, countN)
                if upto < 3: return
        x1 = dram("x1", (NP, D))
        HH = dram("HH", (NP, ROW))
        ent = dram("ent", (NP, D))
        HH1 = dram("HH1", (NP, ROW))
        x2 = dram("x2", (NP, D))
        x2d = dram("x2d", (NP, D))
        byS = dram("byS", (NP, D))
        places = dram("places", (NP, 1))
        relations = dram("relations", (A["L1_gnn_relation_embed"].shape[0], 4))
        EG = dram("EG", (P * T + 1, 2 * D))
        zero_fill(nc, "zeroS", [byS, places])
        tabS = tables(nc, ctx, "tabS", T)
        dstS = sb("dstS", [P, T], I32)
        typS = sb("typS", [P, T], I32)
        ptrS = sb("ptrS", [P, T], I32)
        ptrN = sb("ptrN", [P, NC * U])
        srel = sb("srel", [P, T, 4])
        sorted_edges(nc, sorted2, T, N, tabS["keyi"][:, :], tabS["src"][:, :], dstS[:, :], typS[:, :])
        segment_tables(nc, "segS", tabS["keyi"][:, :], None, T, ident, tabS)
        scatter_places(nc, T, N, tabS, places, ptrN[:, :], NC)
        relation_scores(nc, A, ones, relations)
        gather_whole(nc, "srel", T, relations, relations.shape[0] - 1, typS, srel, 4)

        def hidden_rows(st, t, v, c, out):
            st.link(nc.vector.tensor_tensor(out[:, :, 0:D], out[:, :, 0:D], bcast(v["g"][:, :], 1, U), ALU.mult))
            st.link(nc.vector.tensor_tensor(out[:, :, 0:D], out[:, :, 0:D], bcast(v["b"][:, :], 1, U), ALU.add))
            st.did(nc.vector.tensor_copy(out[:, :, D], ptrN[:, ds(c * U, U)]))
            st.did(nc.vector.tensor_copy(out[:, :, D + 1], ptrN[:, ds(c * U, U)]))

        def first_body(st, t, v, c, tmp, layer_norm, product, src_ready):
            st.link(nc.vector.tensor_tensor(tmp, product(), t["agg"][:, :, 0:D], ALU.add))
            st.link(nc.vector.tensor_tensor(tmp, tmp, t["x"], ALU.add))
            layer_norm(tmp, t["x1"])
            layer_norm(t["x1"], t["hh"][:, :, 0:D])
            hidden_rows(st, t, v, c, t["hh"])

        node_stage(nc, "nfirst", N, NC, ident, {"x": (A["x"], D), "agg": (byD, ROW), "h": (H, ROW)},
                   {"x1": (x1, D), "hh": (HH, ROW)},
                   {"g": A["L1_gnn_ln_gamma"][0], "b": A["L1_gnn_ln_beta"][0]},
                   ("h", [A["L0_gnn_root2"]], A["L0_gnn_bias2"], True), ["root", "root"], first_body, 18)
        if upto < 4: return
        for layer in range(2):
            table = (HH, HH1)[layer]
            with ExitStack() as c1:
                sb1 = lambda name, shape, dt=F32: c1.enter_context(nc.sbuf_tensor(f"{name}_{layer}", shape, dt))
                score = sb1("score", [P, T, 2])
                rz = sb1("rz", [P, T, 2])
                carry = sb1("carry1", [P, 2 * D])
                hdst = sb1("hdst", [P, T, D])
                attention_scores(nc, f"att{layer}", A, layer, T, N, table, tabS["src"], dstS, ident, srel, score, hdst, ptrS)
                segment_softmax(nc, f"soft{layer}", T, tabS, ident, score, score, rz, 0.85)
                with ExitStack() as c2:
                    state = c2.enter_context(nc.sbuf_tensor(f"state_{layer}", [P, T + 1, 2 * D], F32))
                    for step in range(3):
                        attention_step(nc, f"step{layer}{step}", T, tabS, step == 0, EG, ptrS, hdst, score, state)
                        carry_over(nc, f"stepc{layer}{step}", state[:, T, :], tabS["pre"][:, T - 1:T], ident, 2 * D, "sum", carry[:, :])
                        if step < 2:
                            attention_share(nc, f"share{layer}{step}", T, tabS, carry, state, rz, EG)
                        else:
                            attention_output(nc, f"wo{layer}", A, layer, T, N, tabS, carry, state, rz, ident, byS)
            if upto < 5: return

            def ent_body(st, t, v, c, tmp, layer_norm, product, src_ready):
                st.link(nc.vector.scalar_tensor_tensor(tmp, product(), 0.15, t["agg"], ALU.mult, ALU.add))
                st.link(nc.vector.tensor_tensor(t["ent"], tmp, t["x"], ALU.add))
                layer_norm(t["ent"], t["hh"][:, :, 0:D])
                hidden_rows(st, t, v, c, t["hh"])

            def last_body(st, t, v, c, tmp, layer_norm, product, src_ready):
                st.link(nc.vector.scalar_tensor_tensor(tmp, product(), 0.15, t["agg"], ALU.mult, ALU.add))
                st.link(nc.vector.tensor_tensor(tmp, tmp, t["x"], ALU.add))
                st.link(nc.vector.tensor_tensor(tmp, tmp, t["x1"], ALU.add))
                layer_norm(tmp, t["x2"])
                st.link(nc.vector.tensor_tensor(t["x2d"], t["x2"], bcast(dN[:, ds(c * U, U)], 2, D), ALU.mult))

            W_o = A["L1_gnn_W_o"][layer]
            halves = ("h", [W_o[0:D, :], W_o[D:2 * D, :]], None, True)
            if layer == 0:
                node_stage(nc, "nent", N, NC, ident, {"x": (x1, D), "agg": (byS, D), "h": (HH, ROW)},
                           {"ent": (ent, D), "hh": (HH1, ROW)},
                           {"g": A["L1_gnn_ln_gamma"][1], "b": A["L1_gnn_ln_beta"][1]},
                           halves, ["root"], ent_body, 12)
            else:
                dN = sb("dN", [P, NC * U])
                rdegD = sb("rdegD", [P, T])
                dD = sb("dD", [P, T])
                degree_factors(nc, T, NC, tabD["count"], countN, rdegD, dD, dN)
                node_stage(nc, "nlast", N, NC, ident,
                           {"x": (ent, D), "agg": (byS, D), "h": (HH1, ROW), "x1": (x1, D)},
                           {"x2": (x2, D), "x2d": (x2d, D)}, {}, halves, ["root"], last_body, 10)
        if upto < 6: return
        EG2 = dram("EG2", (P * T + 1, D))
        x3 = dram("x3", (NP, D))
        q0 = dram("q0", (NP, D))
        Q = dram("Q", (NP, ROW))
        with ExitStack() as c3:
            sb3 = lambda name, shape, dt=F32: c3.enter_context(nc.sbuf_tensor(name, shape, dt))
            state = sb3("stateD", [P, T + 1, D])
            acc = sb3("accD", [P, T, D])
            carry = sb3("carryD", [P, D])
            for step in range(3):
                if step == 0:
                    running_sums(nc, "deg0", T, tabD, x2d, N - 1, tabD["src"], state)
                else:
                    running_sums(nc, f"deg{step}", T, tabD, EG2, P * T, ptrD, state)
                carry_over(nc, f"degc{step}", state[:, T, :], tabD["pre"][:, T - 1:T], ident, D, "sum", carry[:, :])
                degree_share(nc, f"degs{step}", T, tabD, carry, state, rdegD, dD, acc, step == 0, EG2,
                             byD if step == 2 else None, N)

        def q_body(st, t, v, c, tmp, layer_norm, product, src_ready):
            st.link(nc.vector.tensor_tensor(tmp, t["x"], t["agg"][:, :, 0:D], ALU.add))
            st.link(nc.vector.scalar_tensor_tensor(tmp, tmp, 0.25, t["x"], ALU.mult, ALU.add))
            layer_norm(tmp, t["x3"])
            src_ready()
            st.link(nc.vector.tensor_copy(t["q"], product()))

        node_stage(nc, "nq", N, NC, ident, {"x": (x2, D), "agg": (byD, ROW)}, {"x3": (x3, D), "q": (q0, D)}, {},
                   ("x3", [A["L3_gnn_W_q"]], A["L3_gnn_b_q"], False), ["root"], q_body, 9)
        lN = sb("lN", [P, NC * U])
        edge_network(nc, "netn", A, U, NC, N, NC, T, ident, lN, nodes=q0)
        last_norm(nc, "lnn", A, lN[:, :])
        q_rows(nc, N, NC, q0, lN, Q)
        if upto < 7: return
        with ExitStack() as c4:
            sb4 = lambda name, shape, dt=F32: c4.enter_context(nc.sbuf_tensor(name, shape, dt))
            attr = sb4("attr8", [P, T, 8])
            qs = sb4("qs", [P, T, D])
            own = sb4("own", [P, T])
            lE = sb4("lE", [P, T])
            dstD = sb4("dstD", [P, T], I32)
            zsum = sb4("zsum", [P, T])
            carry = sb4("carryQ", [P, D])
            load_attributes(nc, A, E, T, attr)
            with Stage(nc, "dstD") as s:
                s_dve = s.sem("dve")
                block = s.ctx.enter_context(nc.Block())

                @block.vector
                def _(dve):
                    nc.vector.tensor_scalar(dstD[:, :], tabD["keyi"][:, :], float(N - 1), None, ALU.min).then_inc(s_dve, 1)
            edge_network(nc, "nete", A, G // 2, 2 * (T // G), N, NC, T, ident, lE,
                         edges=(Q, tabD["src"], dstD, attr, qs, own))
            last_norm(nc, "lne", A, lE[:, :])
            one = lambda x: x[:, :].rearrange("p (t a) -> p t a", a=1)
            segment_softmax(nc, "softQ", T, tabD, ident, one(lE), one(lE), one(zsum), None, 1, one(own))
            state = sb4("stateQ", [P, T + 1, D])
            running_sums(nc, "sumQ", T, tabD, None, None, None, state, lE, qs)
            carry_over(nc, "carQ", state[:, T, :], tabD["pre"][:, T - 1:T], ident, D, "sum", carry[:, :])
            scatter_attention(nc, T, N, tabD, carry, state, zsum, own, byD)
        if upto < 8: return

        def out_body(st, t, v, c, tmp, layer_norm, product, src_ready, small_in, small_out, exp):
            z, top = t["agg"][:, :, D], t["agg"][:, :, D + 1]
            own = lN[:, ds(c * U, U)]
            st.link(nc.vector.tensor_scalar(small_out[:, :], countN[:, ds(c * U, U)], 0.0, None, ALU.is_gt))
            st.link(nc.vector.tensor_tensor(small_in[:, :], own, top, ALU.subtract))
            exp(nc.vector.tensor_tensor(small_in[:, :], small_in[:, :], small_out[:, :], ALU.mult))
            st.link(nc.vector.tensor_tensor(small_in[:, :], small_out[:, :], z, ALU.add))
            st.link(nc.vector.reciprocal(small_in[:, :], small_in[:, :]))
            st.link(nc.vector.tensor_tensor(tmp, t["q"], bcast(small_out[:, :], 2, D), ALU.mult))
            st.link(nc.vector.tensor_tensor(tmp, tmp, t["agg"][:, :, 0:D], ALU.add))
            st.link(nc.vector.tensor_tensor(tmp, tmp, bcast(small_in[:, :], 2, D), ALU.mult))
            st.link(nc.vector.scalar_tensor_tensor(tmp, tmp, 0.01, tmp, ALU.mult, ALU.max))
            st.link(nc.vector.tensor_tensor(tmp, tmp, t["x3"], ALU.add))
            layer_norm(tmp, t["out"])

        node_stage(nc, "nout", N, NC, ident, {"x3": (x3, D), "q": (q0, D), "agg": (byD, ROW)}, {"out": (out, D)}, {},
                   None, ["exp", "root"], out_body, 15)


_OUTS = [((50000, 64), "float32")]


def kernel(**inputs):
    import numpy as np
    import concourse.bacc as bacc
    from concourse.bass_utils import run_bass_kernel_spmd

    nc = bacc.Bacc("TRN2", target_bir_lowering=False, num_devices=1)
    arrays, A = {}, {}
    for name, value in inputs.items():
        a = np.ascontiguousarray(value)
        arrays[f"in_{name}"] = a
        A[name] = nc.dram_tensor(f"in_{name}", a.shape, mybir.dt.from_np(a.dtype), kind="ExternalInput").ap()
    N, E = A["x"].shape[0], A["src"].shape[0]
    tiles = -(-E // P)
    T = -(-tiles // (2 * G)) * 2 * G
    out = nc.dram_tensor("out_0", (N, D), F32, kind="ExternalOutput").ap()
    build(nc, A, out, N, E, T)
    r = run_bass_kernel_spmd(nc, [arrays], core_ids=[0])
    return r.results[0]["out_0"]
```

```python
from contextlib import ExitStack

import concourse.bass as bass
from concourse import mybir

F32 = mybir.dt.float32
BF16 = mybir.dt.bfloat16
I32 = mybir.dt.int32
ALU = mybir.AluOpType
ACT = mybir.ActivationFunctionType
AX = mybir.AxisListType
P = 128
D = 64
K = 5
KK = K * K
NEG = -1.5e38
PAD_KEY = 65535
ROW = D + 2
U = 8
G = 14
SLOTS = 8
ACC = 4


def ds(at, n):
    return bass.ds(at, n)


class Steps:

    def __init__(self, eng, sem, per=0, turn=0, base=0):
        self.eng, self.sem, self.start, self.n = eng, sem, turn * per + base, 0
        self.fixed = isinstance(self.start, int)

    def did(self, ins):
        ins.then_inc(self.sem, 1)
        self.n += 1
        return ins

    def wait(self):
        if not self.fixed or self.start + self.n > 0:
            self.eng.wait_ge(self.sem, self.start + self.n)

    def link(self, ins):
        self.did(ins)
        self.wait()


RETIRED = []


def retire(nc, sems, at=100):
    RETIRED.extend(sems)
    if len(RETIRED) >= at:
        nc.clear_and_free_semaphores(RETIRED)
        nc.all_engine_barrier()
        RETIRED.clear()


class Stage:

    def __init__(self, nc, name):
        self.nc, self.name, self.ctx, self.sems = nc, name, ExitStack(), []

    def __enter__(self):
        self.ctx.__enter__()
        return self

    def __exit__(self, *a):
        out = self.ctx.__exit__(*a)
        retire(self.nc, self.sems)
        return out

    def sb(self, name, shape, dt=F32):
        return self.ctx.enter_context(self.nc.sbuf_tensor(f"{self.name}_{name}", shape, dt))

    def ps(self, name, shape, dt=F32):
        return self.ctx.enter_context(self.nc.psum_tensor(f"{self.name}_{name}", shape, dt))

    def sem(self, name):
        self.sems.append(self.nc.alloc_semaphore(name=f"{self.name}_{name}"))
        return self.sems[-1]


def turns_from_zero(eng, n):
    if n > 0:
        yield 0
    if n > 1:
        with eng.Fori(1, n) as i:
            yield i


def hold(eng, sem, value, s_turn):
    eng.wait_ge(sem, value)
    eng.sem_inc(s_turn, 1)


def bcast(ap, axis, n):
    v = ap.unsqueeze(axis)
    shape = list(v.shape)
    shape[axis] = n
    return v.broadcast_to(shape)



def segment_tables(nc, name, key, T, ident, tab):
    with Stage(nc, name) as s:
        ext = s.sb("ext", [P, T + 2])
        one = s.sb("one", [P, T])
        tmp = s.sb("tmp", [P, T])
        base = s.sb("base", [P, T])
        s_key, s_shift, s_dve, s_pos = s.sem("key"), s.sem("shift"), s.sem("dve"), s.sem("pos")
        block = s.ctx.enter_context(nc.Block())

        @block.gpsimd
        def _(pool):
            nc.gpsimd.iota(tab["pos1"][:, :], pattern=[[1, T]], base=1, channel_multiplier=T,
                           allow_small_or_imprecise_dtypes=True).then_inc(s_pos, 1)

        @block.sync
        def _(sp):
            sp.wait_ge(s_key, 1)
            sp.dma_start(ext[1:P, 0:1], ext[0:P - 1, T:T + 1]).then_inc(s_shift, 16)
            sp.dma_start(ext[0:P - 1, T + 1:T + 2], ext[1:P, 1:2]).then_inc(s_shift, 16)

        @block.vector
        def _(dve):
            st = Steps(dve, s_dve)
            st.did(nc.vector.memset(one[:, :], 1.0))
            st.link(nc.vector.memset(ext[:, :], -1.0))
            nc.vector.tensor_copy(ext[:, 1:T + 1], key).then_inc(s_key, 1)
            dve.wait_ge(s_shift, 32)
            dve.wait_ge(s_key, 1)
            mid = ext[:, 1:T + 1]
            st.did(nc.vector.tensor_tensor(tab["keep"][:, :], mid, ext[:, 0:T], ALU.is_equal))
            st.link(nc.vector.tensor_tensor(tab["keepback"][:, :], mid, ext[:, 2:T + 2], ALU.is_equal))
            st.did(nc.vector.tensor_scalar(tab["neg"][:, :], tab["keep"][:, :], -NEG, NEG, ALU.mult, ALU.add))
            st.did(nc.vector.tensor_scalar(tab["negback"][:, :], tab["keepback"][:, :], -NEG, NEG, ALU.mult, ALU.add))
            st.did(nc.vector.tensor_tensor_scan(tab["pre"][:, :], tab["keep"][:, :], one[:, :], 1.0,
                                                ALU.mult, ALU.mult))
            st.link(nc.vector.tensor_tensor_scan(tab["post"][:, T - 1::-1], tab["keepback"][:, T - 1::-1],
                                                 one[:, T - 1::-1], 1.0, ALU.mult, ALU.mult))
            st.did(nc.vector.tensor_scalar(tab["negpre"][:, :], tab["pre"][:, :], -NEG, NEG, ALU.mult, ALU.add))
            st.did(nc.vector.tensor_scalar(tab["negpost"][:, :], tab["post"][:, :], -NEG, NEG, ALU.mult, ALU.add))
            st.did(nc.vector.tensor_tensor_scan(tab["count"][:, :], tab["keep"][:, :], one[:, :], 0.0,
                                                ALU.mult, ALU.add))
            st.link(nc.vector.scalar_tensor_tensor(tmp[:, :], tab["keepback"][:, :], float(PAD_KEY), mid,
                                                   ALU.mult, ALU.add))
            st.link(nc.vector.tensor_copy(tab["endrow"][:, :], tmp[:, :]))
    carry_over(nc, f"{name}_c", tab["count"][:, T - 1:T], tab["pre"][:, T - 1:T], ident, 1, "sum", tab["ccount"][:, :])
    with Stage(nc, f"{name}_f") as s:
        s_dve = s.sem("dve")
        tmp = s.sb("tmp", [P, T])
        block = s.ctx.enter_context(nc.Block())

        @block.vector
        def _(dve):
            st = Steps(dve, s_dve)
            st.link(nc.vector.tensor_scalar(tmp[:, :], tab["pre"][:, :], tab["ccount"][:, 0:1], None, ALU.mult))
            st.link(nc.vector.tensor_tensor(tab["count"][:, :], tab["count"][:, :], tmp[:, :], ALU.add))


def carry_over(nc, name, ends, whole, ident, W, kind, out, back=False):
    op = (ALU.mult, ALU.add) if kind == "sum" else (ALU.add, ALU.max)
    init = 0.0 if kind == "sum" else NEG
    with Stage(nc, name) as s:
        wide = s.sb("wide", [P, W])
        wholeT = s.sb("wholeT", [W, P])
        state = s.sb("state", [W, P + 1])
        psE = s.ps("psE", [W, P])
        psW = s.ps("psW", [W, P])
        psC = s.ps("psC", [P, W])
        s_wide, s_turn, s_dve, s_state, s_back = s.sem("wide"), s.sem("turn"), s.sem("dve"), s.sem("state"), s.sem("back")
        block = s.ctx.enter_context(nc.Block())

        @block.tensor
        def _(pe):
            nc.tensor.transpose(psE[:, :], ends, ident[:, :]).then_inc(s_turn, 1)
            pe.wait_ge(s_wide, 1)
            nc.tensor.transpose(psW[:, :], wide[:, :], ident[:, :]).then_inc(s_turn, 1)
            pe.wait_ge(s_state, 1)
            src = state[:, 1:P + 1] if back else state[:, 0:P]
            nc.tensor.transpose(psC[:, :], src, ident[0:W, 0:W]).then_inc(s_back, 1)

        @block.vector
        def _(dve):
            st = Steps(dve, s_dve)
            nc.vector.tensor_copy(wide[:, :], whole.broadcast_to([P, W])).then_inc(s_wide, 1)
            edge = P if back else 0
            st.did(nc.vector.memset(state[:, edge:edge + 1], init))
            dve.wait_ge(s_turn, 2)
            st.link(nc.vector.tensor_copy(wholeT[:, :], psW[:, :]))
            if back:
                nc.vector.tensor_tensor_scan(state[:, P - 1::-1], wholeT[:, P - 1::-1], psE[:, P - 1::-1],
                                             init, *op).then_inc(s_state, 1)
            else:
                nc.vector.tensor_tensor_scan(state[:, 1:P + 1], wholeT[:, :], psE[:, :], init, *op).then_inc(s_state, 1)
            dve.wait_ge(s_back, 1)
            st.link(nc.vector.tensor_copy(out, psC[:, :]))



def zero_fill(sp, tensors, z, s_zeroed):
    n = 0
    for t in tensors:
        v = t.rearrange("(c p u) w -> c p (u w)", p=P, u=U)
        chunks, _, per = v.shape
        with sp.Fori(0, chunks) as c:
            sp.dma_start(v[ds(c, 1)].rearrange("a p w -> (a p) w"), z[:, 0:per]).then_inc(s_zeroed, 16)
        n += chunks
    return 16 * n


def sort_pass(nc, name, load, digit, out_rows, T, ones, upper, n_pass, zeroed=()):
    C = T // G
    R = 256
    with Stage(nc, name) as s:
        rows = s.sb("rows", [P, T, 4], I32)
        dig_i = s.sb("dig_i", [P, T], I32)
        dig = s.sb("dig", [P, T])
        digits = s.sb("digits", [P, R])
        hist = s.sb("hist", [P, R])
        total = s.sb("total", [P, R])
        onesr = s.sb("onesr", [P, R])
        cum = s.sb("cum", [P, R])
        hit = s.sb("hit", [P, 2, R])
        place = s.sb("place", [P, 2, G])
        placei = s.sb("placei", [P, 2, G], I32)
        rslot = s.sb("rslot", [P, 2, G, 4], I32)
        psB = s.ps("psB", [P, R])
        psT = s.ps("psT", [P, R])
        s_in, s_iota, s_dve, s_hist, s_pre = s.sem("in"), s.sem("iota"), s.sem("dve"), s.sem("hist"), s.sem("pre")
        s_placed, s_turn, s_z, s_zeroed = s.sem("placed"), s.sem("turn"), s.sem("z"), s.sem("zeroed")
        z = s.sb("z", [P, U * ROW]) if zeroed else None
        s_sent = [s.sem("sent0"), s.sem("sent1")]
        block = s.ctx.enter_context(nc.Block())

        @block.sync
        def _(sp):
            load(sp, rows, s_in)
            if zeroed:
                sp.wait_ge(s_z, 1)
                n = zero_fill(sp, zeroed, z, s_zeroed)
                sp.wait_ge(s_zeroed, n)

        @block.tensor
        def _(pe):
            pe.wait_ge(s_hist, 1)
            nc.tensor.matmul(psB[:, :], upper[:, :], hist[:, :], start=True, stop=True)
            nc.tensor.matmul(psT[:, :], ones[:, :], hist[:, :], start=True, stop=True).then_inc(s_pre, 1)

        @block.gpsimd
        def _(pool):
            nc.gpsimd.iota(digits[:, :], pattern=[[1, R]], base=0, channel_multiplier=0,
                           allow_small_or_imprecise_dtypes=True).then_inc(s_iota, 1)
            bound = pool.to_reg(P * T - 1)
            for i in turns_from_zero(pool, C // 2):
                for h in range(2):
                    pool.wait_ge(s_placed, i * 2 + (h + 1))
                    pool.sem_inc(s_turn, 1)
                    for g in range(G):
                        nc.gpsimd.indirect_dma_start(
                            out=out_rows[:, :], out_offset=bass.IndirectOffsetOnAxis(ap=placei[:, h, g:g + 1], axis=0),
                            in_=rslot[:, h, g, :], in_offset=None, bounds_check=bound,
                            oob_is_err=False).then_inc(s_sent[h], 16)
            for h in range(2):
                pool.wait_ge(s_sent[h], 16 * G * (C // 2))

        @block.vector
        def _(dve):
            st = Steps(dve, s_dve)
            if zeroed:
                nc.vector.memset(z[:, :], 0.0).then_inc(s_z, 1)
            st.did(nc.vector.memset(onesr[:, :], 1.0))
            st.link(nc.vector.memset(hist[:, :], 0.0))
            dve.wait_ge(s_in, n_pass)
            if digit == 0:
                st.link(nc.vector.tensor_scalar(dig_i[:, :], rows[:, :, 0], R - 1, None, ALU.bitwise_and))
            else:
                st.link(nc.vector.tensor_scalar(dig_i[:, :], rows[:, :, 0], 8, None, ALU.arith_shift_right))
            st.link(nc.vector.tensor_copy(dig[:, :], dig_i[:, :]))
            dve.wait_ge(s_iota, 1)
            n0 = st.n
            with dve.Fori(0, C) as c:
                sl = Steps(dve, s_dve, G, c, n0)
                for g in range(G):
                    sl.link(nc.vector.scalar_tensor_tensor(hist[:, :], digits[:, :], dig[:, ds(c * G + g, 1)],
                                                           hist[:, :], ALU.is_equal, ALU.add))
            n0 += G * C
            st = Steps(dve, s_dve, base=n0)
            st.eng.sem_inc(s_hist, 1)
            dve.wait_ge(s_pre, 1)
            st.link(nc.vector.tensor_copy(total[:, :], psT[:, :]))
            st.link(nc.vector.tensor_tensor_scan(cum[:, :], onesr[:, :], total[:, :], 0.0, ALU.mult, ALU.add))
            st.link(nc.vector.tensor_tensor(cum[:, :], cum[:, :], total[:, :], ALU.subtract))
            st.link(nc.vector.tensor_tensor(hist[:, :], cum[:, :], psB[:, :], ALU.add))
            n0 += st.n
            per = 2 * (2 * G + 2)

            def chunk(c, h, sl):
                for g in range(G):
                    t = c * G + g
                    sl.did(nc.vector.scalar_tensor_tensor(hit[:, g % 2, :], digits[:, :], dig[:, ds(t, 1)], hist[:, :],
                                                          ALU.is_equal, ALU.mult, accum_out=place[:, h, g:g + 1]))
                    sl.link(nc.vector.scalar_tensor_tensor(hist[:, :], digits[:, :], dig[:, ds(t, 1)], hist[:, :],
                                                           ALU.is_equal, ALU.add))
                sl.link(nc.vector.tensor_copy(placei[:, h, :], place[:, h, :]))
                sl.link(nc.vector.tensor_copy(rslot[:, h, :, :], rows[:, ds(c * G, G), :]))
                dve.sem_inc(s_placed, 1)

            for i in turns_from_zero(dve, C // 2):
                sl = Steps(dve, s_dve, per, i, n0)
                for h in range(2):
                    dve.wait_ge(s_sent[h], i * (16 * G))
                    chunk(i * 2 + h, h, sl)


def setup(nc, A, N, E, T, tabD, ident, upper, ones, rows0):
    full = E // T
    rest = E - full * T
    with Stage(nc, "setup") as s:
        onef = s.sb("onef", [P, P])
        key_src = s.sb("key_src", [P, T], I32)
        etype = s.sb("etype", [P, T], I32)
        loads = 16 * 4 * (2 if rest else 1)
        s_one, s_c, s_mem, s_in, s_dve = s.sem("one"), s.sem("c"), s.sem("mem"), s.sem("in"), s.sem("dve")
        block = s.ctx.enter_context(nc.Block())

        @block.vector
        def _(dve):
            st = Steps(dve, s_dve)
            nc.vector.memset(onef[:, :], 1.0).then_inc(s_one, 1)
            st.did(nc.vector.memset(ones[:, :], 1.0))
            for tile, pad in ((tabD["keyi"], PAD_KEY), (tabD["src"], 0), (key_src, PAD_KEY), (etype, 0)):
                nc.vector.memset(tile[:, :], pad).then_inc(s_mem, 1)
            dve.wait_ge(s_in, loads)
            nc.vector.memset(rows0[:, :, 3], 0).then_inc(s_dve, 1)
            for f, tile in enumerate((key_src, tabD["keyi"], etype)):
                nc.vector.tensor_copy(rows0[:, :, f], tile[:, :]).then_inc(s_dve, 1)

        @block.gpsimd
        def _(pool):
            pool.wait_ge(s_one, 1)
            nc.gpsimd.affine_select(out=ident[:, :], in_=onef[:, :], compare_op=ALU.is_equal, fill=0.0, base=0,
                                    pattern=[[-1, P]], channel_multiplier=1).then_inc(s_c, 1)
            nc.gpsimd.affine_select(out=upper[:, :], in_=onef[:, :], compare_op=ALU.is_gt, fill=0.0, base=0,
                                    pattern=[[1, P]], channel_multiplier=-1).then_inc(s_c, 1)

        @block.sync
        def _(sp):
            sp.wait_ge(s_mem, 4)
            for tile, name in ((tabD["keyi"], "dst"), (tabD["src"], "src"), (key_src, "src"),
                               (etype, "edge_type_500")):
                v = A[name]
                sp.dma_start(tile[0:full, :], v[0:full * T].rearrange("(p t) -> p t", t=T)).then_inc(s_in, 16)
                if rest:
                    sp.dma_start(tile[full:full + 1, 0:rest],
                                 v[full * T:E].rearrange("(p t) -> p t", p=1)).then_inc(s_in, 16)



def basis_tables(nc, A, E, T, basisT, ident):
    full, rest = E // T, E - E // T * T
    C = T // G
    with Stage(nc, "basis") as s:
        attr = s.sb("attr", [P, T, 2])
        lowi = s.sb("lowi", [P, T, 2], I32)
        low = s.sb("low", [P, T, 2])
        frac = s.sb("frac", [P, T, 2])
        knot = s.sb("knot", [P, T, 2])
        tmp = s.sb("tmp", [P, T, 2])
        hat = s.sb("hat", [P, 2, T, K])
        prod = s.sb("prod", [P, 2, G, KK])
        parts = s.sb("parts", [P, 2, G, 3 * KK], BF16)
        identb = s.sb("identb", [P, P], BF16)
        psT = [s.ps(f"psT{h}", [3 * KK, G // 2, P], BF16) for h in range(2)]
        s_mem, s_in, s_dve, s_id = s.sem("mem"), s.sem("in"), s.sem("dve"), s.sem("id")
        s_split, s_turned, s_copied = s.sem("split"), s.sem("turned"), s.sem("copied")
        block = s.ctx.enter_context(nc.Block())

        @block.sync
        def _(sp):
            sp.wait_ge(s_mem, 1)
            v = A["edge_attr_2"]
            sp.dma_start(attr[0:full, :, :], v[0:full * T, :].rearrange("(p t) f -> p t f", t=T)).then_inc(s_in, 16)
            if rest:
                sp.dma_start(attr[full:full + 1, 0:rest, :],
                             v[full * T:E, :].rearrange("(p t) f -> p t f", p=1)).then_inc(s_in, 16)

        @block.vector
        def _(dve):
            st = Steps(dve, s_dve)
            nc.vector.memset(attr[:, :, :], 0.0).then_inc(s_mem, 1)
            nc.vector.memset(basisT[:, T * P:], 0.0).then_inc(s_mem, 1)
            nc.vector.tensor_copy(identb[:, :], ident[:, :]).then_inc(s_id, 1)
            dve.wait_ge(s_in, 32 if rest else 16)
            st.link(nc.vector.tensor_scalar(attr[:, :, :], attr[:, :, :], float(K - 1), None, ALU.mult))
            st.link(nc.vector.tensor_copy(lowi[:, :, :], attr[:, :, :]))
            st.link(nc.vector.tensor_copy(low[:, :, :], lowi[:, :, :]))
            st.link(nc.vector.tensor_tensor(tmp[:, :, :], low[:, :, :], attr[:, :, :], ALU.is_gt))
            st.link(nc.vector.tensor_tensor(low[:, :, :], low[:, :, :], tmp[:, :, :], ALU.subtract))
            st.link(nc.vector.tensor_tensor(frac[:, :, :], attr[:, :, :], low[:, :, :], ALU.subtract))
            for upper in range(2):
                st.link(nc.vector.tensor_scalar(knot[:, :, :], low[:, :, :], float(upper), 0.0, ALU.add, ALU.max))
                st.did(nc.vector.tensor_scalar(knot[:, :, :], knot[:, :, :], float(K - 1), None, ALU.min))
                if not upper:
                    st.link(nc.vector.tensor_scalar(tmp[:, :, :], frac[:, :, :], -1.0, 1.0, ALU.mult, ALU.add))
                st.wait()
                part = frac if upper else tmp
                for d in range(2):
                    for a in range(K):
                        if upper:
                            st.link(nc.vector.scalar_tensor_tensor(low[:, :, d], knot[:, :, d], float(a),
                                                                   part[:, :, d], ALU.is_equal, ALU.mult))
                            st.link(nc.vector.tensor_tensor(hat[:, d, :, a], hat[:, d, :, a], low[:, :, d], ALU.add))
                        else:
                            st.did(nc.vector.scalar_tensor_tensor(hat[:, d, :, a], knot[:, :, d], float(a),
                                                                  part[:, :, d], ALU.is_equal, ALU.mult))
                st.wait()
            n0 = st.n
            for i in turns_from_zero(dve, C // 2):
                sl = Steps(dve, s_dve, 2 * (K + 4), i, n0)
                for h in range(2):
                    c = i * 2 + h
                    for b in range(K):
                        sl.did(nc.vector.tensor_tensor(
                            prod[:, h, :, K * b:K * b + K], hat[:, 0, ds(c * G, G), :],
                            hat[:, 1, ds(c * G, G), b:b + 1].broadcast_to([P, G, K]), ALU.mult))
                    sl.wait()
                    dve.wait_ge(s_turned, i * 4 + 2 * h)
                    sl.link(nc.vector.tensor_copy(parts[:, h, :, 0:KK], prod[:, h, :, :]))
                    sl.link(nc.vector.tensor_tensor(prod[:, h, :, :], prod[:, h, :, :], parts[:, h, :, 0:KK], ALU.subtract))
                    sl.link(nc.vector.tensor_copy(parts[:, h, :, KK:2 * KK], prod[:, h, :, :]))
                    sl.link(nc.vector.tensor_tensor(parts[:, h, :, 2 * KK:3 * KK], prod[:, h, :, :],
                                                    parts[:, h, :, KK:2 * KK], ALU.subtract))
                    dve.sem_inc(s_split, 1)

        @block.tensor
        def _(pe):
            pe.wait_ge(s_id, 1)
            pe.sem_inc(s_turned, 2)
            for i in turns_from_zero(pe, C // 2):
                for h in range(2):
                    pe.wait_ge(s_split, i * 2 + (h + 1))
                    for u in range(2):
                        pe.wait_ge(s_copied, i * 4 + (2 * h + u))
                        for g in range(G // 2):
                            ins = nc.tensor.transpose(psT[u][:, g, :], parts[:, h, u * (G // 2) + g, :], identb[:, :])
                        ins.then_inc(s_turned, 1)

        @block.scalar
        def _(act):
            act.sem_inc(s_copied, 1)
            for i in turns_from_zero(act, C // 2):
                for h in range(2):
                    for u in range(2):
                        act.wait_ge(s_turned, i * 4 + (2 * h + u + 3))
                        nc.scalar.activation(basisT[:, ds(((i * 2 + h) * 2 + u) * (G // 2) * P, (G // 2) * P)],
                                             psT[u][:, :, :].rearrange("k g p -> k (g p)"), ACT.Copy).then_inc(s_copied, 1)


def gather_chunks(nc, pool, C, s_turn, jobs, free, n=G, after=None):
    bounds = [pool.to_reg(last) for _, last, *_ in jobs]
    for i in turns_from_zero(pool, C // 2):
        for h in range(2):
            for sem, per in free:
                pool.wait_ge(sem, i * (2 * per) + (h + 1) * per)
                pool.sem_inc(s_turn, 1)
            for (table, _, idx, islot, rslot, s_rows, s_idx), bound in zip(jobs, bounds):
                nc.gpsimd.tensor_copy(islot[:, h, :], idx[:, ds((i * 2 + h) * n, n)]).then_inc(s_idx, 1)
                pool.wait_ge(s_idx, i * 2 + (h + 1))
                pool.sem_inc(s_turn, 1)
                for g in range(n):
                    nc.gpsimd.indirect_dma_start(
                        out=rslot[:, h, g, 0:table.shape[1]], out_offset=None, in_=table[:, :],
                        in_offset=bass.IndirectOffsetOnAxis(ap=islot[:, h, g:g + 1], axis=0),
                        bounds_check=bound, oob_is_err=False).then_inc(s_rows[h], 16)
            if after:
                after(i, h)


def scatter_chunks(nc, pool, C, s_turn, s_ready, table, last, islot, rslot, s_sent):
    bound = pool.to_reg(last)
    for i in turns_from_zero(pool, C // 2):
        for h in range(2):
            pool.wait_ge(s_ready, i * 2 + (h + 1))
            pool.sem_inc(s_turn, 1)
            for g in range(G):
                nc.gpsimd.indirect_dma_start(
                    out=table[:, :], out_offset=bass.IndirectOffsetOnAxis(ap=islot[:, h, g:g + 1], axis=0),
                    in_=rslot[:, h, g, :], in_offset=None, bounds_check=bound,
                    oob_is_err=False).then_inc(s_sent[h], 16)
    for h in range(2):
        pool.wait_ge(s_sent[h], 16 * G * (C // 2))


def spline_messages(nc, name, W, table, width, N, T, tab, basisT, ident, agg, ptr, places=None, relations=None):
    C = T // G
    UN = [range(0, 4), range(4, 8), range(8, 12), range(12, 13)]
    with Stage(nc, name) as s:
        islot = s.sb("islot", [P, 2, G], I32)
        rows = s.sb("rows", [P, 2, G, width])
        rowsT = s.sb("rowsT", [P, 2, G, P])
        scaled = s.sb("scaled", [P, 2, 13, P])
        knots = s.sb("knots", [3 * KK, 26, D], BF16)
        knots0 = s.sb("knots0", [3 * KK, 26, D], BF16)
        Wr = s.sb("Wr", [P, 13, D])
        psX = [s.ps(f"psX{h}", [D, 4, P]) for h in range(2)]
        psB = [s.ps(f"psB{q}", [P, 4, P]) for q in range(4)]
        psM = [s.ps(f"psM{h}", [P, 512]) for h in range(2)]
        BY_EDGE = 256
        msgT = s.sb("msgT", [D, 2, P])
        s_w, s_sel, s_turn, s_idx = s.sem("w"), s.sem("sel"), s.sem("turn"), s.sem("idx")
        s_rows = [s.sem("rows0"), s.sem("rows1")]
        s_xt, s_xcopied, s_basis, s_scaled = s.sem("xt"), s.sem("xcopied"), s.sem("basis"), s.sem("scaled")
        s_main, s_max, s_dve = s.sem("main"), s.sem("max"), s.sem("dve")
        s_kept, s_pturn = s.sem("kept"), s.sem("pturn")
        s_msg, s_back = s.sem("msg"), s.sem("back")
        s_rel_idx, s_rel_kept, s_place, s_byN = (s.sem(k) for k in ("rel_idx", "rel_kept", "place", "byN"))
        s_rel = [s.sem("rel0"), s.sem("rel1")]
        s_sent = [s.sem("sent0"), s.sem("sent1")]
        jobs = [(table, N - 1, tab["src"], islot, rows, s_rows, s_idx)]
        if relations:
            rel_table, rel_type, rel_out = relations
            rel_w = rel_table.shape[1]
            rel_slot = s.sb("rel_slot", [P, 2, G], I32)
            rel_rows = s.sb("rel_rows", [P, 2, G, rel_w])
            jobs.append((rel_table, rel_table.shape[0] - 1, rel_type, rel_slot, rel_rows, s_rel, s_rel_idx))
        if places:
            tabS, place_table, place_byN = places
            end_slot = s.sb("end_slot", [P, 2, G], I32)
            place_slot = s.sb("place_slot", [P, 2, G, 1])
        block = s.ctx.enter_context(nc.Block())

        @block.sync
        def _(sp):
            sp.dma_start(Wr[:, 0:12, :], W[0:24, :, :].rearrange("(c k) i o -> (k i) c o", k=2)).then_inc(s_w, 16)
            sp.dma_start(Wr[0:D, 12, :], W[24, :, :]).then_inc(s_w, 16)

        @block.gpsimd
        def _(pool):
            nc.gpsimd.memset(knots[:, :, :], 0.0).then_inc(s_sel, 1)
            for part in range(3):
                pool.wait_ge(s_sel, part + 1)
                nc.gpsimd.affine_select(out=knots[:, :, :], in_=knots[:, :, :], compare_op=ALU.not_equal, fill=1.0,
                                        base=-KK * part, pattern=[[-1, KK + 1], [0, D]], channel_multiplier=1).then_inc(s_sel, 1)
            bound = pool.to_reg(N - 1)

            def scatter_places(i, h):
                j = i * 2 + h
                pool.wait_ge(s_sent[h], i * (16 * G))
                pool.sem_inc(s_turn, 1)
                nc.gpsimd.tensor_copy(place_slot[:, h, :, 0], tabS["pos1"][:, ds(j * G, G)]).then_inc(s_place, 1)
                nc.gpsimd.tensor_copy(end_slot[:, h, :], tabS["endrow"][:, ds(j * G, G)]).then_inc(s_place, 1)
                pool.wait_ge(s_place, j * 2 + 2)
                pool.sem_inc(s_turn, 1)
                for g in range(G):
                    nc.gpsimd.indirect_dma_start(
                        out=place_table[:, :], out_offset=bass.IndirectOffsetOnAxis(ap=end_slot[:, h, g:g + 1], axis=0),
                        in_=place_slot[:, h, g, :], in_offset=None, bounds_check=bound,
                        oob_is_err=False).then_inc(s_sent[h], 16)

            gather_chunks(nc, pool, C, s_turn, jobs, [(s_xt, 4), (s_kept, 1)] + ([(s_rel_kept, 1)] if relations else []),
                          after=scatter_places if places else None)
            if places:
                for h in range(2):
                    pool.wait_ge(s_sent[h], 16 * G * (C // 2))
                pool.dma_start(place_byN.rearrange("p (c u) -> p c u", u=U),
                               place_table.rearrange("(c p u) w -> p c (u w)", p=P, u=U)).then_inc(s_byN, 16)
                pool.wait_ge(s_byN, 16)

        @block.tensor
        def _(pe):
            pe.wait_ge(s_sel, 4)
            pe.wait_ge(s_w, 32)
            pe.sem_inc(s_xt, 8)

            def spread(m, q):
                for n, c in enumerate(UN[q]):
                    w = P if c < 12 else D
                    ins = nc.tensor.matmul(psB[q][0:w, n, :], knots[:, 2 * c:2 * c + w // D, :],
                                           basisT[:, ds(m * P, P)], start=True, stop=True)
                ins.then_inc(s_basis, 1)

            def turn_back(m, par):
                hold(pe, s_msg, m + 1, s_pturn)
                nc.tensor.transpose(psM[par][:, BY_EDGE:BY_EDGE + D], msgT[:, par, :], ident[0:D, 0:D]).then_inc(s_back, 1)

            pe.sem_inc(s_back, 2)
            for q in range(4):
                spread(0, q)
            for i in turns_from_zero(pe, C // 2):
                for h in range(2):
                    j = i * 2 + h
                    pe.wait_ge(s_rows[h], i * (16 * G) + 16 * G)
                    for q in range(4):
                        hold(pe, s_xcopied, j * 8 + 2 * q, s_pturn)
                        for n, t in enumerate(range(4 * q, min(4 * q + 4, G))):
                            ins = nc.tensor.transpose(psX[q % 2][:, n, :], rows[:, h, t, 0:D], ident[:, :])
                        ins.then_inc(s_xt, 1)
                    for t in range(G):
                        m = j * G + t
                        pe.wait_ge(s_max, m + 1)
                        for q in range(4):
                            if q == 3:
                                hold(pe, s_scaled, m * 4 + (q + 1 + 8 * G), s_pturn)
                            else:
                                pe.wait_ge(s_scaled, m * 4 + (q + 1 + 8 * G))
                            for c in UN[q]:
                                k = P if c < 12 else D
                                ins = nc.tensor.matmul(psM[t % 2][0:D, 0:P], Wr[0:k, c, :], scaled[0:k, t % 2, c, :],
                                                       start=(c == 0), stop=(c == 12))
                            if q == 3:
                                ins.then_inc(s_main, 1)
                            spread(m + 1, q)
                            if q == 1 and t:
                                turn_back(m - 1, (t - 1) % 2)
                    turn_back(j * G + (G - 1), (G - 1) % 2)

        @block.scalar
        def _(act):
            act.sem_inc(s_xcopied, 2)
            for i in turns_from_zero(act, C // 2):
                for h in range(2):
                    j = i * 2 + h
                    act.wait_ge(s_scaled, j * (4 * G) + 4 * G)
                    for q in range(4):
                        n = min(4, G - 4 * q)
                        act.wait_ge(s_xt, j * 4 + (q + 9))
                        for half in (0, D):
                            nc.scalar.activation(rowsT[half:half + D, h, 4 * q:4 * q + n, :], psX[q % 2][:, 0:n, :],
                                                 ACT.Copy).then_inc(s_xcopied, 1)
                    for t in range(G):
                        m = j * G + t
                        act.wait_ge(s_back, m + 1)
                        act.wait_ge(s_main, m + 1)
                        nc.scalar.activation(msgT[:, t % 2, :], psM[t % 2][0:D, 0:P], ACT.Copy).then_inc(s_msg, 1)

        @block.vector
        def _(dve):
            nc.vector.memset(agg[:, 0, :], NEG).then_inc(s_dve, 1)
            dve.wait_ge(s_dve, 1)
            dve.sem_inc(s_max, 2)
            dve.sem_inc(s_scaled, 8 * G)
            dve.sem_inc(s_kept, 2)
            dve.sem_inc(s_rel_kept, 2)

            def running_max(m, par):
                dve.wait_ge(s_back, m + 3)
                dve.wait_ge(s_max, m + 2)
                nc.vector.scalar_tensor_tensor(agg[:, ds(m + 1, 1), :].rearrange("p a d -> p (a d)"),
                                               agg[:, ds(m, 1), :].rearrange("p a d -> p (a d)"),
                                               tab["neg"][:, ds(m, 1)], psM[par][:, BY_EDGE:BY_EDGE + D], ALU.add,
                                               ALU.max).then_inc(s_max, 1)

            for i in turns_from_zero(dve, C // 2):
                for h in range(2):
                    j = i * 2 + h
                    dve.wait_ge(s_rows[h], i * (16 * G) + 16 * G)
                    if ptr is not None:
                        nc.vector.tensor_copy(ptr[:, ds(j * G, G)], rows[:, h, :, D]).then_inc(s_kept, 1)
                    else:
                        dve.sem_inc(s_kept, 1)
                    if relations:
                        dve.wait_ge(s_rel[h], i * (16 * G) + 16 * G)
                        nc.vector.tensor_copy(rel_out[:, ds(j * G, G), :], rel_rows[:, h, :, :]).then_inc(s_rel_kept, 1)
                    for t in range(G):
                        m = j * G + t
                        if t % 4 == 0:
                            dve.wait_ge(s_xcopied, j * 8 + (2 * (t // 4) + 4))
                        for q in range(4):
                            c0, c1 = UN[q][0], UN[q][-1] + 1
                            k = P if c0 < 12 else D
                            dve.wait_ge(s_basis, m * 4 + (q + 1))
                            nc.vector.tensor_tensor(scaled[0:k, t % 2, c0:c1, :], psB[q][0:k, 0:c1 - c0, :],
                                                    bcast(rowsT[0:k, h, t, :], 1, c1 - c0), ALU.mult).then_inc(s_scaled, 1)
                        if t:
                            running_max(m - 1, (t - 1) % 2)
                    running_max(j * G + (G - 1), (G - 1) % 2)


def scatter_ends(nc, name, T, tab, carry, agg, kind, table, N, cols=True):
    C = T // G
    with Stage(nc, name) as s:
        islot = s.sb("islot", [P, 2, G], I32)
        rslot = s.sb("rslot", [P, 2, G, ROW])
        s_turn, s_dve, s_ready = s.sem("turn"), s.sem("dve"), s.sem("ready")
        s_sent = [s.sem("sent0"), s.sem("sent1")]
        block = s.ctx.enter_context(nc.Block())

        @block.gpsimd
        def _(pool):
            scatter_chunks(nc, pool, C, s_turn, s_ready, table, N - 1, islot, rslot, s_sent)

        @block.vector
        def _(dve):
            pre, ops = (tab["negpre"], (ALU.add, ALU.max)) if kind == "max" else (tab["pre"], (ALU.mult, ALU.add))
            for i in turns_from_zero(dve, C // 2):
                for h in range(2):
                    sl = Steps(dve, s_dve, G + 3, i * 2 + h)
                    dve.wait_ge(s_sent[h], i * (16 * G))
                    for g in range(G):
                        t = (i * 2 + h) * G + g
                        sl.did(nc.vector.scalar_tensor_tensor(
                            rslot[:, h, g, 0:D], carry[:, :], pre[:, ds(t, 1)],
                            agg[:, ds(t + 1, 1), :].rearrange("p a d -> p (a d)"), *ops))
                    at = ds((i * 2 + h) * G, G)
                    sl.did(nc.vector.tensor_copy(rslot[:, h, :, D], tab["pos1"][:, at]))
                    sl.did(nc.vector.tensor_copy(rslot[:, h, :, D + 1], tab["count"][:, at]))
                    sl.did(nc.vector.tensor_copy(islot[:, h, :], tab["endrow"][:, at]))
                    sl.wait()
                    dve.sem_inc(s_ready, 1)



def chunk_rows(table, c, last, N):
    v = table.rearrange("(p u) w -> p (u w)", u=U)
    n = (N // U - c * P) if last else P
    return v[ds(c * P, n), :], n


def node_pairs_after(eng, NC):
    loops = (NC - 1) // SLOTS
    pair = lambda i, h: [(i * SLOTS + (h + k), h + k, i, False) for k in range(2)]
    before = None
    if loops:
        yield pair(0, 0), None
        for i in turns_from_zero(eng, loops - 1):
            for h in range(2, SLOTS, 2):
                yield pair(i, h), pair(i, h - 2)
            yield pair(i + 1, 0), pair(i, SLOTS - 2)
        for h in range(2, SLOTS, 2):
            yield pair(loops - 1, h), pair(loops - 1, h - 2)
        before = pair(loops - 1, SLOTS - 2)
    for c in range(loops * SLOTS, NC, 2):
        group = [(k, k % SLOTS, k // SLOTS, k == NC - 1) for k in range(c, min(c + 2, NC))]
        yield group, before
        before = group
    yield None, before


def node_pairs(eng, NC):
    loops = (NC - 1) // SLOTS
    for i in turns_from_zero(eng, loops):
        for h in range(0, SLOTS, 2):
            yield [(i * SLOTS + (h + k), h + k, i, False) for k in range(2)]
    for c in range(loops * SLOTS, NC, 2):
        yield [(k, k % SLOTS, k // SLOTS, k == NC - 1) for k in range(c, min(c + 2, NC))]


def first(group):
    return group[0][0]


def end(group):
    return group[0][0] + len(group)


class Norm:

    def __init__(self, s, name, n, eps_tile):
        self.xc = s.sb(f"{name}_xc", [P, n, D])
        self.sq = s.sb(f"{name}_sq", [P, n, D])
        self.sum = s.sb(f"{name}_sum", [P, n])
        self.mean = s.sb(f"{name}_mean", [P, n])
        self.var = s.sb(f"{name}_var", [P, n])
        self.std = s.sb(f"{name}_std", [P, n])
        self.rstd = s.sb(f"{name}_rstd", [P, n])
        self.n, self.eps = n, eps_tile

    def root(self, nc, s_std):
        nc.scalar.activation(self.std[:, :], self.var[:, :], ACT.Sqrt, bias=self.eps[:, :], scale=1.0 / D).then_inc(s_std, 1)


def spread_rows(eng, tile, vec, sem):
    eng.dma_start(tile, vec.partition_broadcast(P)).then_inc(sem, 16)


class Chunk:

    def __init__(self, nc, s, eps, pos, normed, small):
        self.nc = nc
        if normed:
            self.norm = Norm(s, f"norm{pos}", U, eps)
        self.tmp = s.sb(f"tmp{pos}", [P, U, D])
        if small:
            self.small_in = s.sb(f"small_in{pos}", [P, U])
            self.small_out = s.sb(f"small_out{pos}", [P, U])

    def ask(self, ins):
        ins.then_inc(self.s_asked, 1)

    def answer(self):
        self.nc.vector.wait_ge(self.s_answered, self.base + self.k * self.pair + (self.pos + 1))
        self.k += 1

    def asked(self, ins):
        self.ask(ins)
        yield None
        self.answer()

    def layer_norm(self, x, out):
        nc, n = self.nc, self.norm
        yield nc.vector.tensor_reduce(n.sum[:, :], x, AX.X, ALU.add)
        yield nc.vector.tensor_scalar(n.mean[:, :], n.sum[:, :], 1.0 / D, None, ALU.mult)
        yield nc.vector.tensor_tensor(n.xc[:, :, :], x, bcast(n.mean[:, :], 2, D), ALU.subtract)
        yield nc.vector.tensor_tensor(n.sq[:, :, :], n.xc[:, :, :], n.xc[:, :, :], ALU.mult)
        yield from self.asked(nc.vector.tensor_reduce(n.var[:, :], n.sq[:, :, :], AX.X, ALU.add))
        yield nc.vector.reciprocal(n.rstd[:, :], n.std[:, :])
        yield nc.vector.tensor_tensor(out, n.xc[:, :, :], bcast(n.rstd[:, :], 2, D), ALU.mult)


def node_stage(nc, name, N, NC, ident, loads, stores, consts, product, acts, body, per, tail=None,
               tail_steps=0, eps_value=1e-5, prepare=None):
    turned, weights, bias, result = product or (None, [], None, None)
    early = product is not None and result is None
    late = result is not None
    with Stage(nc, name) as s:
        tiles = {k: s.sb(k, [P, SLOTS, U, w]) for k, (_, w) in {**loads, **stores}.items()}
        vec = {k: s.sb(k, [P, v.shape[0]]) for k, v in consts.items()}
        eps = s.sb("eps", [P, 1])
        work = [Chunk(nc, s, eps, pos, "root" in acts, "exp" in acts or "small root" in acts) for pos in range(2)]
        norms = len(acts)
        short = [k for k, (table, _) in loads.items() if table.shape[0] == N]
        n_mem = 3 + len(short)
        s_dve, s_const, s_mem, s_asked, s_answered, s_weights, s_prepared = (s.sem(k) for k in (
            "dve", "const", "mem", "asked", "answered", "weights", "prepared"))
        s_in = [s.sem(f"in{h}") for h in range(SLOTS)]
        s_out = [s.sem(f"out{h}") for h in range(SLOTS)]
        s_done, s_turned, s_copied, s_product, s_result, s_pool, s_tailed, s_pool_turn, s_sp_turn, s_pturn = (s.sem(k) for k in (
            "done", "turned", "copied", "product", "result", "pool", "tailed", "pool_turn", "sp_turn", "pturn"))
        nw = len(weights)
        if product:
            xT = s.sb("xT", [D + 1, ACC, U * P])
            wb = s.sb("wb", [D + 1, nw, D])
            psX = [s.ps(f"psX{k}", [D, 4 * P]) for k in range(2)]
            psO = [s.ps(f"psO{h}", [P, U, D]) for h in range(ACC)]
        block = s.ctx.enter_context(nc.Block())
        n_const = len(consts) + nw + (1 if bias is not None else 0)

        @block.sync
        def _(sp):
            sp.wait_ge(s_mem, n_mem)
            for k, v in consts.items():
                spread_rows(sp, vec[k][:, :], v, s_const)
            if product:
                for n, w in enumerate(weights):
                    sp.dma_start(wb[0:D, n, :], w).then_inc(s_const, 16)
                if bias is not None:
                    sp.dma_start(wb[D:D + 1, 0, :], bias.rearrange("(a n) -> a n", a=1)).then_inc(s_const, 16)
            for group in node_pairs(sp, NC):
                hold(sp, s_done, end(group), s_sp_turn)
                if tail:
                    hold(sp, s_tailed, end(group), s_sp_turn)
                if early:
                    hold(sp, s_turned, end(group) * 2, s_sp_turn)
                for c, h, i, last in group:
                    for k, (table, w) in loads.items():
                        src, n = chunk_rows(table, c, last and table.shape[0] == N, N)
                        sp.dma_start(tiles[k][0:n, h].rearrange("p u d -> p (u d)"), src).then_inc(s_in[h], 16)

        @block.vector
        def _(dve):
            nc.vector.memset(eps[:, :], eps_value).then_inc(s_mem, 1)
            for k in short:
                nc.vector.memset(tiles[k][:, :, :, :], 0.0).then_inc(s_mem, 1)
            if product:
                nc.vector.memset(xT[D:D + 1, :, :], 1.0).then_inc(s_mem, 1)
                nc.vector.memset(wb[D:D + 1, :, :], 0.0).then_inc(s_mem, 1)
            else:
                dve.sem_inc(s_mem, 2)
            dve.sem_inc(s_done, SLOTS)
            dve.wait_ge(s_const, 16 * n_const)
            if nw == 2:
                nc.vector.tensor_tensor(wb[0:D, 0, :], wb[0:D, 0, :], wb[0:D, 1, :], ALU.add).then_inc(s_weights, 1)
            else:
                dve.sem_inc(s_weights, 1)
            if prepare:
                prepare(Steps(dve, s_prepared), vec)

            for group in node_pairs(dve, NC):
                st = Steps(dve, s_dve, per, first(group))
                bodies = []
                for pos, (c, h, i, last) in enumerate(group):
                    dve.wait_ge(s_in[h], i * (16 * len(loads)) + 16 * len(loads))
                    dve.wait_ge(s_out[h], i * (16 * len(stores)))
                    w = work[pos]
                    w.s_asked, w.s_answered, w.pos, w.pair, w.k = s_asked, s_answered, pos, len(group), 0
                    w.base = first(group) * norms
                    w.product = psO[h % ACC][:, :, :] if early else None
                    t = {n: v[:, h, :, :] for n, v in tiles.items()}
                    bodies.append([body(w, t, vec, c), 0])
                if early:
                    dve.wait_ge(s_product, end(group) + ACC)
                if late:
                    dve.wait_ge(s_turned, end(group) * 2)
                while bodies:
                    for entry in list(bodies):
                        if entry[1]:
                            dve.wait_ge(s_dve, st.start + entry[1])
                        entry[1] = 0
                        try:
                            ins = next(entry[0])
                        except StopIteration:
                            bodies.remove(entry)
                            continue
                        if ins is not None:
                            st.did(ins)
                            entry[1] = st.n
                assert st.n == per * len(group), (st.n, per)
                dve.sem_inc(s_done, len(group))

        @block.tensor
        def _(pe):
            if not product:
                return
            pe.sem_inc(s_product, ACC)
            pe.sem_inc(s_turned, 2 * SLOTS)
            pe.wait_ge(s_mem, n_mem)
            pe.wait_ge(s_weights, 1)
            for group in node_pairs(pe, NC):
                if late:
                    pe.wait_ge(s_done, end(group) + SLOTS)
                for c, h, i, last in group:
                    if early:
                        pe.wait_ge(s_in[h], i * (16 * len(loads)) + 16 * len(loads))
                    for q in range(2):
                        hold(pe, s_copied, c * 2 + (q + 1), s_pturn)
                        for g in range(4):
                            ins = nc.tensor.transpose(psX[q][:, g * P:(g + 1) * P], tiles[turned][:, h, q * 4 + g, 0:D], ident[:, :])
                        ins.then_inc(s_turned, 1)
                if late:
                    hold(pe, s_result, end(group), s_pturn)
                else:
                    hold(pe, s_done, end(group) + SLOTS - ACC, s_pturn)
                for c, h, i, last in group:
                    for g in range(U):
                        if g % 4 == 0:
                            hold(pe, s_copied, c * 2 + (g // 4 + 3), s_pturn)
                        ins = nc.tensor.matmul(psO[h % ACC][:, g, :], xT[:, h % ACC, g * P:(g + 1) * P], wb[:, 0, :], start=True, stop=True)
                    ins.then_inc(s_product, 1)

        @block.scalar
        def _(act):
            act.sem_inc(s_copied, 2)
            act.sem_inc(s_result, ACC)

            def copies(group):
                for c, h, i, last in group:
                    act.wait_ge(s_product, c + 1)
                    for q in range(2):
                        act.wait_ge(s_turned, c * 2 + (q + 1 + 2 * SLOTS))
                        nc.scalar.activation(xT[0:D, h % ACC, q * 4 * P:(q + 1) * 4 * P], psX[q][:, :], ACT.Copy).then_inc(s_copied, 1)

            def answers(group):
                for k in range(norms):
                    for pos in range(len(group)):
                        act.wait_ge(s_asked, first(group) * norms + (k * len(group) + pos + 1))
                        if acts[k] == "root":
                            work[pos].norm.root(nc, s_answered)
                        elif acts[k] == "small root":
                            nc.scalar.activation(work[pos].small_out[:, :], work[pos].small_in[:, :], ACT.Sqrt,
                                                 bias=eps[:, :], scale=1.0).then_inc(s_answered, 1)
                        else:
                            nc.scalar.activation(work[pos].small_out[:, :], work[pos].small_in[:, :], ACT.Exp).then_inc(s_answered, 1)

            act.wait_ge(s_mem, n_mem)
            for group, before in node_pairs_after(act, NC):
                if early and group:
                    copies(group)
                if early and before:
                    answers(before)
                if not early and group:
                    answers(group)
                if late and before:
                    copies(before)
                    for c, h, i, last in before:
                        act.wait_ge(s_product, c + 1 + ACC)
                        act.wait_ge(s_out[h], i * (16 * len(stores)))
                        nc.scalar.activation(tiles[result][:, h, :, :], psO[h % ACC][:, :, :], ACT.Copy).then_inc(s_result, 1)

        @block.gpsimd
        def _(pool):
            pool.sem_inc(s_tailed, SLOTS)
            if tail and n_const:
                pool.wait_ge(s_const, 16 * n_const)
            for group in node_pairs(pool, NC):
                for c, h, i, last in group:
                    pool.wait_ge(s_done, end(group) + SLOTS)
                    pool.sem_inc(s_pool_turn, 1)
                    if tail:
                        sl = Steps(pool, s_pool, tail_steps, c)
                        tail(sl, {n: v[:, h, :, :] for n, v in tiles.items()}, vec, c)
                        assert sl.n == tail_steps
                        sl.wait()
                        pool.sem_inc(s_tailed, 1)
                    if late:
                        pool.wait_ge(s_result, c + 1 + ACC)
                        pool.sem_inc(s_pool_turn, 1)
                    for k, (table, w) in stores.items():
                        dst, n = chunk_rows(table, c, last and table.shape[0] == N, N)
                        pool.dma_start(dst, tiles[k][0:n, h].rearrange("p u d -> p (u d)")).then_inc(s_out[h], 16)
            for h in range(SLOTS):
                if h < NC:
                    pool.wait_ge(s_out[h], 16 * len(stores) * ((NC - h + SLOTS - 1) // SLOTS))


def hidden(nc, A, SD, H, N, NC, ident, countN):
    def body(w, t, v, c):
        yield nc.vector.tensor_tensor(w.tmp[:, :, :], w.product, t["agg"][:, :, 0:D], ALU.add)
        yield nc.vector.tensor_scalar(t["hrow"][:, :, 0:D], w.tmp[:, :, :], 0.0, None, ALU.max)
        yield nc.vector.tensor_copy(t["hrow"][:, :, D:ROW], t["agg"][:, :, D:ROW])
        yield nc.vector.tensor_copy(countN[:, ds(c * U, U)], t["agg"][:, :, D + 1])

    node_stage(nc, "hidden", N, NC, ident, {"x": (A["x"], D), "agg": (SD, ROW)}, {"hrow": (H, ROW)}, {},
               ("x", [A["L0_gnn_root1"]], A["L0_gnn_bias1"], None), [], body, 4)




def relation_scores(nc, A, ones, table):
    R = A["L1_gnn_relation_embed"].shape[0]
    NT = -(-R // P)
    with Stage(nc, "rel") as s:
        emb = s.sb("emb", [P, NT, D])
        ident = s.sb("ident", [P, P])
        embT = s.sb("embT", [D, NT * P])
        w = s.sb("w", [D, 2, P])
        att = s.sb("att", [P, 2, P])
        th = s.sb("th", [P, NT, 2, P])
        prod = s.sb("prod", [P, NT, 2, P])
        res = s.sb("res", [P, NT, 4])
        psX = s.ps("psX", [D, NT * P])
        psS = [s.ps(f"psS{k}", [P, 2, 2, P]) for k in range(NT // 2)]
        s_mem, s_id, s_in, s_xt, s_xc, s_mm, s_th, s_dve, s_res, s_out = (s.sem(k) for k in (
            "mem", "id", "in", "xt", "xc", "mm", "th", "dve", "res", "out"))
        block = s.ctx.enter_context(nc.Block())
        full, rest = R // P, R % P

        @block.sync
        def _(sp):
            sp.wait_ge(s_mem, 1)
            e = A["L1_gnn_relation_embed"]
            for n in range(NT):
                m = min(P, R - n * P)
                sp.dma_start(emb[0:m, n, :], e[n * P:n * P + m, :]).then_inc(s_in, 16)
            for l in range(2):
                sp.dma_start(w[:, l, :], A["L1_gnn_W_r"][l]).then_inc(s_in, 16)
                spread_rows(sp, att[:, l, :], A["L1_gnn_att_r"][l].rearrange("h d -> (h d)"), s_in)
            sp.wait_ge(s_res, 1)
            for n in range(NT):
                m = min(P, R - n * P)
                sp.dma_start(table[n * P:n * P + m, :], res[0:m, n, :]).then_inc(s_out, 16)
            sp.wait_ge(s_out, 16 * NT)

        @block.gpsimd
        def _(pool):
            nc.gpsimd.affine_select(out=ident[:, :], in_=ones[:, :], compare_op=ALU.is_equal, fill=0.0, base=0,
                                    pattern=[[-1, P]], channel_multiplier=1).then_inc(s_id, 1)

        @block.tensor
        def _(pe):
            pe.wait_ge(s_id, 1)
            pe.wait_ge(s_in, 16 * (NT + 4))
            for n in range(NT):
                nc.tensor.transpose(psX[:, n * P:(n + 1) * P], emb[:, n, :], ident[:, :]).then_inc(s_xt, 1)
            pe.wait_ge(s_xc, 1)
            for n in range(NT):
                for l in range(2):
                    nc.tensor.matmul(psS[n // 2][:, n % 2, l, :], embT[:, n * P:(n + 1) * P], w[:, l, :],
                                     start=True, stop=True).then_inc(s_mm, 1)

        @block.scalar
        def _(act):
            act.wait_ge(s_xt, NT)
            nc.scalar.activation(embT[:, :], psX[:, :], ACT.Copy).then_inc(s_xc, 1)
            act.wait_ge(s_mm, 2 * NT)
            for k in range(NT // 2):
                nc.scalar.activation(th[:, 2 * k:2 * k + 2, :, :], psS[k][:, :, :, :], ACT.Tanh).then_inc(s_th, 1)

        @block.vector
        def _(dve):
            st = Steps(dve, s_dve)
            nc.vector.memset(emb[:, :, :], 0.0).then_inc(s_mem, 1)
            dve.wait_ge(s_in, 16 * (NT + 4))
            dve.wait_ge(s_th, NT // 2)
            st.link(nc.vector.tensor_tensor(prod[:, :, :, :], th[:, :, :, :], bcast(att[:, :, :], 1, NT), ALU.mult))
            nc.vector.tensor_reduce(res[:, :, :], prod[:, :, :, :].rearrange("p n l (h d) -> p n (l h) d", h=2),
                                    AX.X, ALU.add).then_inc(s_res, 1)


def sorted_edges(nc, sorted2, T, N, keyS, srcS, dstS, typS):
    with Stage(nc, "byS") as s:
        rows = s.sb("rows", [P, T, 4], I32)
        s_in, s_dve = s.sem("in"), s.sem("dve")
        block = s.ctx.enter_context(nc.Block())

        @block.sync
        def _(sp):
            sp.dma_start(rows[:, :, :], sorted2.rearrange("(p t) f -> p t f", t=T)).then_inc(s_in, 16)

        @block.vector
        def _(dve):
            dve.wait_ge(s_in, 16)
            st = Steps(dve, s_dve)
            st.did(nc.vector.tensor_copy(keyS, rows[:, :, 0]))
            st.did(nc.vector.tensor_copy(typS, rows[:, :, 2]))
            st.did(nc.vector.tensor_scalar(srcS, rows[:, :, 0], float(N - 1), None, ALU.min))
            st.did(nc.vector.tensor_scalar(dstS, rows[:, :, 1], float(N - 1), None, ALU.min))
            st.wait()


def attention_scores(nc, name, A, layer, T, N, HH, srcS, dstS, ident, srel, score, hdst, ptrS):
    C = T // G
    UNITS = G // 2
    with Stage(nc, name) as s:
        islot0 = s.sb("islot0", [P, 2, G], I32)
        islot1 = s.sb("islot1", [P, 2, G], I32)
        rs = s.sb("rs", [P, 2, G, ROW])
        rd = s.sb("rd", [P, 2, G, ROW])
        xT = s.sb("xT", [D, 2, 4 * P])
        w = s.sb("w", [D, 2, P])
        att = s.sb("att", [P, 2, P])
        th = s.sb("th", [P, 2, 2, 2 * P])
        prod = s.sb("prod", [P, 2, 2 * P])
        s4 = s.sb("s4", [P, G, 4])
        s2 = s.sb("s2", [P, G, 2])
        psX = [s.ps(f"psX{k}", [D, 4, P]) for k in range(2)]
        psS = [s.ps(f"psS{k}", [P, 2, 2, P]) for k in range(2)]
        s_w, s_turn, s_pturn, s_idx0, s_idx1, s_kept, s_xt, s_xc, s_mm, s_th, s_prod, s_dve = (s.sem(k) for k in (
            "w", "turn", "pturn", "idx0", "idx1", "kept", "xt", "xc", "mm", "th", "prod", "dve"))
        s_rs = [s.sem("rs0"), s.sem("rs1")]
        s_rd = [s.sem("rd0"), s.sem("rd1")]
        block = s.ctx.enter_context(nc.Block())

        @block.sync
        def _(sp):
            for n, k in enumerate(("h", "t")):
                sp.dma_start(w[:, n, :], A[f"L1_gnn_W_{k}"][layer]).then_inc(s_w, 16)
                spread_rows(sp, att[:, n, :], A[f"L1_gnn_att_{k}"][layer].rearrange("h d -> (h d)"), s_w)

        @block.gpsimd
        def _(pool):
            gather_chunks(nc, pool, C, s_turn, [(HH, N - 1, srcS, islot0, rs, s_rs, s_idx0),
                                                (HH, N - 1, dstS, islot1, rd, s_rd, s_idx1)],
                          [(s_xt, UNITS), (s_kept, 2)])

        @block.tensor
        def _(pe):
            pe.wait_ge(s_w, 64)
            pe.sem_inc(s_xt, 2 * UNITS)
            pe.sem_inc(s_mm, 2)
            for i in turns_from_zero(pe, C // 2):
                def products(v):
                    k = i * (2 * UNITS) + v
                    hold(pe, s_xc, k + 3, s_pturn)
                    hold(pe, s_th, k + 1, s_pturn)
                    for g in range(2):
                        for n in range(2):
                            at = (g * 2 + n) * P
                            ins = nc.tensor.matmul(psS[v % 2][:, g, n, :], xT[:, v % 2, at:at + P], w[:, n, :],
                                                   start=True, stop=True)
                    ins.then_inc(s_mm, 1)

                for v in range(2 * UNITS):
                    h, u = divmod(v, UNITS)
                    if u == 0:
                        hold(pe, s_rs[h], i * (16 * G) + 16 * G, s_pturn)
                        hold(pe, s_rd[h], i * (16 * G) + 16 * G, s_pturn)
                    hold(pe, s_xc, i * (2 * UNITS) + (v + 1), s_pturn)
                    for g in range(2):
                        for n, rows in enumerate((rs, rd)):
                            ins = nc.tensor.transpose(psX[v % 2][:, g * 2 + n, :], rows[:, h, 2 * u + g, 0:D], ident[:, :])
                    ins.then_inc(s_xt, 1)
                    if v:
                        products(v - 1)
                products(2 * UNITS - 1)

        @block.scalar
        def _(act):
            act.sem_inc(s_xc, 2)
            act.sem_inc(s_th, 2)
            for i in turns_from_zero(act, C // 2):
                for v in range(2 * UNITS):
                    k = i * (2 * UNITS) + v
                    act.wait_ge(s_xt, k + (2 * UNITS + 1))
                    act.wait_ge(s_mm, k + 1)
                    nc.scalar.activation(xT[:, v % 2, :], psX[v % 2][:, :, :].rearrange("k n p -> k (n p)"),
                                         ACT.Copy).then_inc(s_xc, 1)
                    act.wait_ge(s_mm, k + 3)
                    act.wait_ge(s_prod, k + 1)
                    nc.scalar.activation(th[:, v % 2, :, :], psS[v % 2][:, :, :, :].rearrange("p g n d -> p g (n d)"),
                                         ACT.Tanh).then_inc(s_th, 1)

        @block.vector
        def _(dve):
            dve.wait_ge(s_w, 64)
            dve.sem_inc(s_kept, 4)
            dve.sem_inc(s_prod, 2)
            for i in turns_from_zero(dve, C // 2):
                for h in range(2):
                    sl = Steps(dve, s_dve, UNITS + 3, i * 2 + h)
                    at = ds((i * 2 + h) * G, G)
                    dve.wait_ge(s_rd[h], i * (16 * G) + 16 * G)
                    nc.vector.tensor_copy(hdst[:, at, :], rd[:, h, :, 0:D]).then_inc(s_kept, 1)
                    nc.vector.tensor_copy(ptrS[:, at], rd[:, h, :, D]).then_inc(s_kept, 1)
                    for u in range(UNITS):
                        v = h * UNITS + u
                        k = i * (2 * UNITS) + v
                        dve.wait_ge(s_th, k + 3)
                        sl.wait()
                        nc.vector.tensor_tensor(prod[:, :, :], th[:, v % 2, :, :],
                                                bcast(att[:, :, :].rearrange("p n d -> p (n d)"), 1, 2),
                                                ALU.mult).then_inc(s_prod, 1)
                        dve.wait_ge(s_prod, k + 3)
                        sl.did(nc.vector.tensor_reduce(
                            s4[:, 2 * u:2 * u + 2, :], prod[:, :, :].rearrange("p g (q d) -> p g q d", d=D), AX.X, ALU.add))
                    sl.wait()
                    sl.link(nc.vector.tensor_tensor(s2[:, :, :], s4[:, :, 0:2], s4[:, :, 2:4], ALU.add))
                    sl.link(nc.vector.tensor_tensor(s2[:, :, :], s2[:, :, :], srel[:, at, 2 * layer:2 * layer + 2], ALU.add))
                    sl.link(nc.vector.scalar_tensor_tensor(score[:, at, :], s2[:, :, :], 0.01, s2[:, :, :],
                                                           ALU.mult, ALU.max))


def segment_softmax(nc, name, T, tab, ident, score, weight, rz, factor, W=2, floor=None):
    with Stage(nc, name) as s:
        top = s.sb("top", [P, T, W])
        end = s.sb("end", [P, W])
        carry = s.sb("carry", [P, W])
        tmp = s.sb("tmp", [P, T, W])

        def vector_block(tag, program):
            with Stage(nc, f"{name}_{tag}") as q:
                s_dve = q.sem("dve")
                block = q.ctx.enter_context(nc.Block())

                @block.vector
                def _(dve):
                    program(dve, Steps(dve, s_dve))

        def forward_max(dve, st):
            for w in range(W):
                st.did(nc.vector.tensor_tensor_scan(top[:, :, w], tab["neg"][:, :], score[:, :, w], NEG, ALU.add, ALU.max))
            st.wait()
            st.link(nc.vector.tensor_copy(end[:, :], top[:, T - 1, :]))

        def backward_max(dve, st):
            for w in range(W):
                st.did(nc.vector.tensor_scalar(tmp[:, :, w], tab["negpre"][:, :], carry[:, w:w + 1], None, ALU.add))
            st.wait()
            st.link(nc.vector.tensor_tensor(tmp[:, :, :], tmp[:, :, :], top[:, :, :], ALU.max))
            for w in range(W):
                st.did(nc.vector.tensor_tensor_scan(top[:, T - 1::-1, w], tab["negback"][:, T - 1::-1],
                                                    tmp[:, T - 1::-1, w], NEG, ALU.add, ALU.max))
            st.wait()
            st.link(nc.vector.tensor_copy(end[:, :], top[:, 0, :]))

        def less_max(dve, st):
            for w in range(W):
                st.did(nc.vector.tensor_scalar(tmp[:, :, w], tab["negpost"][:, :], carry[:, w:w + 1], None, ALU.add))
            st.wait()
            st.link(nc.vector.tensor_tensor(top[:, :, :], tmp[:, :, :], top[:, :, :], ALU.max))
            if floor is not None:
                st.link(nc.vector.tensor_tensor(top[:, :, :], top[:, :, :], floor, ALU.max))
                st.link(nc.vector.tensor_copy(floor, top[:, :, :]))
            st.link(nc.vector.tensor_tensor(tmp[:, :, :], score[:, :, :], top[:, :, :], ALU.subtract))

        def sums(dve, st):
            for w in range(W):
                st.did(nc.vector.tensor_tensor_scan(top[:, :, w], tab["keep"][:, :], weight[:, :, w], 0.0, ALU.mult, ALU.add))
            st.wait()
            st.link(nc.vector.tensor_copy(end[:, :], top[:, T - 1, :]))

        def inverse(dve, st):
            for w in range(W):
                st.did(nc.vector.tensor_scalar(tmp[:, :, w], tab["pre"][:, :], carry[:, w:w + 1], None, ALU.mult))
            st.wait()
            st.link(nc.vector.tensor_tensor(top[:, :, :], tmp[:, :, :], top[:, :, :], ALU.add))
            if factor is None:
                st.link(nc.vector.tensor_copy(rz[:, :, :], top[:, :, :]))
                return
            st.link(nc.vector.tensor_scalar(top[:, :, :], top[:, :, :], 1e-30, None, ALU.max))
            st.link(nc.vector.reciprocal(top[:, :, :], top[:, :, :]))
            st.link(nc.vector.tensor_scalar(rz[:, :, :], top[:, :, :], factor, None, ALU.mult))

        vector_block("fmax", forward_max)
        carry_over(nc, f"{name}_cf", end[:, :], tab["negpre"][:, T - 1:T], ident, W, "max", carry[:, :])
        vector_block("bmax", backward_max)
        carry_over(nc, f"{name}_cb", end[:, :], tab["negpost"][:, 0:1], ident, W, "max", carry[:, :], back=True)
        vector_block("less", less_max)
        with Stage(nc, f"{name}_exp") as q:
            s_e = q.sem("e")
            block = q.ctx.enter_context(nc.Block())

            @block.scalar
            def _(act):
                nc.scalar.activation(weight[:, :, :], tmp[:, :, :], ACT.Exp).then_inc(s_e, 1)
                act.wait_ge(s_e, 1)
        vector_block("sums", sums)
        carry_over(nc, f"{name}_cs", end[:, :], tab["pre"][:, T - 1:T], ident, W, "sum", carry[:, :])
        vector_block("inv", inverse)


def attention_step(nc, name, T, tab, first, EG, ptrS, hdst, weight, state):
    C = T // G
    with Stage(nc, name) as s:
        islot = s.sb("islot", [P, 2, G], I32)
        rows = s.sb("rows", [P, 2, G, 2 * D])
        s_turn, s_idx, s_used, s_dve = s.sem("turn"), s.sem("idx"), s.sem("used"), s.sem("dve")
        s_rows = [s.sem("rows0"), s.sem("rows1")]
        block = s.ctx.enter_context(nc.Block())

        if not first:
            @block.gpsimd
            def _(pool):
                gather_chunks(nc, pool, C, s_turn, [(EG, P * T, ptrS, islot, rows, s_rows, s_idx)], [(s_used, 1)])

        @block.vector
        def _(dve):
            nc.vector.memset(state[:, 0, :], 0.0).then_inc(s_used, 1)
            dve.wait_ge(s_used, 1)
            dve.sem_inc(s_used, 1)
            for i in turns_from_zero(dve, C // 2):
                for h in range(2):
                    sl = Steps(dve, s_dve, (2 if first else 4) + G, i * 2 + h)
                    j = i * 2 + h
                    at = ds(j * G, G)
                    if not first:
                        dve.wait_ge(s_rows[h], i * (16 * G) + 16 * G)
                    r = rows[:, h, :, :].rearrange("p g (h d) -> p g h d", h=2)
                    for hd in range(2):
                        if not first:
                            sl.did(nc.vector.scalar_tensor_tensor(r[:, :, hd, :], hdst[:, at, :], 0.15, r[:, :, hd, :],
                                                                  ALU.mult, ALU.add))
                    if not first:
                        sl.wait()
                    for hd in range(2):
                        z = hdst[:, at, :] if first else r[:, :, hd, :]
                        sl.did(nc.vector.tensor_tensor(r[:, :, hd, :], z, bcast(weight[:, at, hd], 2, D), ALU.mult))
                    sl.wait()
                    sums, keep = state[:, ds(j * G, G + 1), :], tab["keep"][:, at]
                    for g in range(G):
                        sl.link(nc.vector.scalar_tensor_tensor(sums[:, g + 1, :], sums[:, g, :], keep[:, g:g + 1],
                                                               rows[:, h, g, :], ALU.mult, ALU.add))
                    dve.sem_inc(s_used, 1)


def attention_share(nc, name, T, tab, carry, state, rz, EG):
    C = T // G
    with Stage(nc, name) as s:
        rslot = s.sb("rslot", [P, 2, G, 2 * D])
        zero = s.sb("zero", [1, 2 * D])
        s_dve, s_ready, s_z, s_zo = s.sem("dve"), s.sem("ready"), s.sem("z"), s.sem("zo")
        s_out = [s.sem("out0"), s.sem("out1")]
        block = s.ctx.enter_context(nc.Block())
        v = EG[1:P * T + 1, :].rearrange("(p t) d -> p t d", t=T)

        @block.sync
        def _(sp):
            sp.wait_ge(s_z, 1)
            sp.dma_start(EG[0:1, :], zero[:, :]).then_inc(s_zo, 16)
            for i in turns_from_zero(sp, C // 2):
                for h in range(2):
                    sp.wait_ge(s_ready, i * 2 + (h + 1))
                    sp.dma_start(v[:, ds((i * 2 + h) * G, G), :], rslot[:, h, :, :]).then_inc(s_out[h], 16)
            for h in range(2):
                sp.wait_ge(s_out[h], 16 * (C // 2))
            sp.wait_ge(s_zo, 16)

        @block.vector
        def _(dve):
            nc.vector.memset(zero[:, :], 0.0).then_inc(s_z, 1)
            for i in turns_from_zero(dve, C // 2):
                for h in range(2):
                    sl = Steps(dve, s_dve, G + 2, i * 2 + h)
                    dve.wait_ge(s_out[h], i * 16)
                    finish_sums(nc, sl, i * 2 + h, tab, carry, state, rslot[:, h, :, :])
                    for hd in range(2):
                        r = rslot[:, h, :, hd * D:(hd + 1) * D]
                        sl.did(nc.vector.tensor_tensor(r, r, bcast(rz[:, ds((i * 2 + h) * G, G), hd], 2, D), ALU.mult))
                    sl.wait()
                    dve.sem_inc(s_ready, 1)


def finish_sums(nc, sl, j, tab, carry, state, out, n=G):
    sums, pre = state[:, ds(j * n + 1, n), :], tab["pre"][:, ds(j * n, n)]
    for g in range(n):
        sl.did(nc.vector.scalar_tensor_tensor(out[:, g, :], carry[:, :], pre[:, g:g + 1], sums[:, g, :],
                                              ALU.mult, ALU.add))
    sl.wait()


def attention_output(nc, name, A, layer, T, N, tab, carry, state, rz, ident, byS):
    C = T // G
    HG = G // 2
    with Stage(nc, name) as s:
        share = s.sb("share", [P, 2, HG, 2 * D])
        shareT = s.sb("shareT", [P, 2, HG, P])
        rslot = s.sb("rslot", [P, 2, G, D])
        islot = s.sb("islot", [P, 2, G], I32)
        wo = s.sb("wo", [P, D])
        psX = [s.ps(f"psX{k}", [P, 4, P]) for k in range(4)]
        psO = [s.ps(f"psO{k}", [P, HG, D]) for k in range(2)]
        s_w, s_dve, s_share, s_xt, s_xc, s_mm, s_res, s_turn, s_pturn, s_ready = (s.sem(k) for k in (
            "w", "dve", "share", "xt", "xc", "mm", "res", "turn", "pturn", "ready"))
        s_sent = [s.sem("sent0"), s.sem("sent1")]
        block = s.ctx.enter_context(nc.Block())
        CUT = ((0, 4), (4, HG))

        @block.sync
        def _(sp):
            sp.dma_start(wo[:, :], A["L1_gnn_W_o"][layer]).then_inc(s_w, 16)

        @block.gpsimd
        def _(pool):
            scatter_chunks(nc, pool, C, s_turn, s_ready, byS, N - 1, islot, rslot, s_sent)

        @block.tensor
        def _(pe):
            pe.wait_ge(s_w, 16)
            pe.sem_inc(s_xt, 4)
            for i in turns_from_zero(pe, C // 2):
                for h in range(2):
                    j = i * 2 + h
                    for u in range(2):
                        k = j * 2 + u
                        hold(pe, s_share, k + 1, s_pturn)
                        for b, (t0, t1) in enumerate(CUT):
                            hold(pe, s_xc, k * 2 + (b + 1), s_pturn)
                            for t in range(t0, t1):
                                ins = nc.tensor.transpose(psX[2 * u + b][:, t - t0, :], share[:, u, t, :], ident[:, :])
                            ins.then_inc(s_xt, 1)
                        hold(pe, s_xc, k * 2 + 6, s_pturn)
                        hold(pe, s_res, k + 1, s_pturn)
                        for t in range(HG):
                            ins = nc.tensor.matmul(psO[u][:, t, :], shareT[:, u, t, :], wo[:, :], start=True, stop=True)
                        ins.then_inc(s_mm, 1)

        @block.scalar
        def _(act):
            act.sem_inc(s_xc, 4)
            for i in turns_from_zero(act, C // 2):
                for h in range(2):
                    for u in range(2):
                        k = (i * 2 + h) * 2 + u
                        act.wait_ge(s_res, k + 1)
                        for b, (t0, t1) in enumerate(CUT):
                            act.wait_ge(s_xt, k * 2 + (b + 5))
                            nc.scalar.activation(shareT[:, u, t0:t1, :], psX[2 * u + b][:, 0:t1 - t0, :], ACT.Copy).then_inc(s_xc, 1)

        @block.vector
        def _(dve):
            dve.sem_inc(s_res, 2)
            for i in turns_from_zero(dve, C // 2):
                for h in range(2):
                    j = i * 2 + h
                    sl = Steps(dve, s_dve, G + 5, j)
                    for u in range(2):
                        k = j * 2 + u
                        dve.wait_ge(s_xt, k * 2 + 2)
                        finish_sums(nc, sl, k, tab, carry, state, share[:, u, :, :], HG)
                        for hd in range(2):
                            r = share[:, u, :, hd * D:(hd + 1) * D]
                            sl.did(nc.vector.tensor_tensor(r, r, bcast(rz[:, ds(k * HG, HG), hd], 2, D), ALU.mult))
                        sl.wait()
                        dve.sem_inc(s_share, 1)
                    dve.wait_ge(s_sent[h], i * (16 * G))
                    sl.did(nc.vector.tensor_copy(islot[:, h, :], tab["endrow"][:, ds(j * G, G)]))
                    for u in range(2):
                        k = j * 2 + u
                        dve.wait_ge(s_mm, k + 1)
                        nc.vector.tensor_copy(rslot[:, h, u * HG:(u + 1) * HG, :], psO[u][:, :, :]).then_inc(s_res, 1)
                    dve.wait_ge(s_res, j * 2 + 4)
                    sl.wait()
                    dve.sem_inc(s_ready, 1)




def degree_factors(nc, T, NC, countD, countN, rdegD, dD, dN):
    with Stage(nc, "deg") as s:
        mN = s.sb("mN", [P, NC * U])
        s_dve, s_root = s.sem("dve"), s.sem("root")
        block = s.ctx.enter_context(nc.Block())

        @block.vector
        def _(dve):
            st = Steps(dve, s_dve)
            st.link(nc.vector.tensor_scalar(mN[:, :], countN[:, :], 1.0, None, ALU.max))
            st.link(nc.vector.reciprocal(rdegD[:, :], countD[:, :]))
            st.link(nc.vector.reciprocal(mN[:, :], mN[:, :]))

        @block.scalar
        def _(act):
            act.wait_ge(s_dve, 3)
            nc.scalar.activation(dD[:, :], rdegD[:, :], ACT.Sqrt).then_inc(s_root, 1)
            nc.scalar.activation(dN[:, :], mN[:, :], ACT.Sqrt).then_inc(s_root, 1)
            act.wait_ge(s_root, 2)


def running_sums(nc, name, T, tab, table, last, idx, state, weight=None, rows_in=None):
    C = T // G
    with Stage(nc, name) as s:
        islot = s.sb("islot", [P, 2, G], I32)
        rows = s.sb("rows", [P, 2, G, D])
        s_turn, s_idx, s_used, s_dve = s.sem("turn"), s.sem("idx"), s.sem("used"), s.sem("dve")
        s_rows = [s.sem("rows0"), s.sem("rows1")]
        block = s.ctx.enter_context(nc.Block())

        if table is not None:
            @block.gpsimd
            def _(pool):
                gather_chunks(nc, pool, C, s_turn, [(table, last, idx, islot, rows, s_rows, s_idx)], [(s_used, 1)])

        @block.vector
        def _(dve):
            nc.vector.memset(state[:, 0, :], 0.0).then_inc(s_used, 1)
            dve.wait_ge(s_used, 1)
            dve.sem_inc(s_used, 1)
            for i in turns_from_zero(dve, C // 2):
                for h in range(2):
                    j = i * 2 + h
                    sl = Steps(dve, s_dve, G + (1 if weight is not None else 0), j)
                    if table is not None:
                        dve.wait_ge(s_rows[h], i * (16 * G) + 16 * G)
                    if weight is not None:
                        at = ds(j * G, G)
                        sl.link(nc.vector.tensor_tensor(rows[:, h, :, :], rows_in[:, at, :],
                                                        bcast(weight[:, at], 2, D), ALU.mult))
                    sums, keep = state[:, ds(j * G, G + 1), :], tab["keep"][:, ds(j * G, G)]
                    for g in range(G):
                        sl.link(nc.vector.scalar_tensor_tensor(sums[:, g + 1, :], sums[:, g, :], keep[:, g:g + 1],
                                                               rows[:, h, g, :], ALU.mult, ALU.add))
                    dve.sem_inc(s_used, 1)


def degree_share(nc, name, T, tab, carry, state, rdegD, dD, acc, first, EG, byD, N):
    C = T // G
    with Stage(nc, name) as s:
        width = ROW if byD is not None else D
        rslot = s.sb("rslot", [P, 2, G, width])
        tmp = s.sb("tmp", [P, G, D])
        islot = s.sb("islot", [P, 2, G], I32)
        zero = s.sb("zero", [1, D])
        s_dve, s_ready, s_z, s_zo, s_turn = s.sem("dve"), s.sem("ready"), s.sem("z"), s.sem("zo"), s.sem("turn")
        s_out = [s.sem("out0"), s.sem("out1")]
        block = s.ctx.enter_context(nc.Block())

        if byD is None:
            @block.sync
            def _(sp):
                v = EG[1:P * T + 1, :].rearrange("(p t) d -> p t d", t=T)
                sp.wait_ge(s_z, 1)
                sp.dma_start(EG[0:1, :], zero[:, :]).then_inc(s_zo, 16)
                for i in turns_from_zero(sp, C // 2):
                    for h in range(2):
                        sp.wait_ge(s_ready, i * 2 + (h + 1))
                        sp.dma_start(v[:, ds((i * 2 + h) * G, G), :], rslot[:, h, :, :]).then_inc(s_out[h], 16)
                for h in range(2):
                    sp.wait_ge(s_out[h], 16 * (C // 2))
                sp.wait_ge(s_zo, 16)
        else:
            @block.gpsimd
            def _(pool):
                scatter_chunks(nc, pool, C, s_turn, s_ready, byD, N - 1, islot, rslot, s_out)

        @block.vector
        def _(dve):
            nc.vector.memset(zero[:, :], 0.0).then_inc(s_z, 1)
            step = 16 if byD is None else 16 * G
            for i in turns_from_zero(dve, C // 2):
                for h in range(2):
                    j = i * 2 + h
                    at = ds(j * G, G)
                    sl = Steps(dve, s_dve, G + (1 if first else 2) + (1 if byD is None else 3), j)
                    dve.wait_ge(s_out[h], i * step)
                    r = rslot[:, h, :, 0:D]
                    finish_sums(nc, sl, j, tab, carry, state, r)
                    if first:
                        sl.link(nc.vector.tensor_tensor(acc[:, at, :], r, bcast(dD[:, at], 2, D), ALU.mult))
                    else:
                        sl.link(nc.vector.tensor_tensor(tmp[:, :, :], r, bcast(dD[:, at], 2, D), ALU.mult))
                        into = acc[:, at, :] if byD is None else r
                        sl.link(nc.vector.tensor_tensor(into, acc[:, at, :], tmp[:, :, :], ALU.add))
                    if byD is None:
                        sl.link(nc.vector.tensor_tensor(r, r, bcast(rdegD[:, at], 2, D), ALU.mult))
                    else:
                        sl.did(nc.vector.tensor_copy(rslot[:, h, :, D], tab["pos1"][:, at]))
                        sl.did(nc.vector.tensor_copy(rslot[:, h, :, D + 1], tab["count"][:, at]))
                        sl.link(nc.vector.tensor_copy(islot[:, h, :], tab["endrow"][:, at]))
                    dve.sem_inc(s_ready, 1)



EW = D + 2 + 8 + 1


def turns(eng, NU):
    yield 0, 0, None, 0
    pairs = (NU - 1) // 2
    for i in turns_from_zero(eng, pairs):
        for h in (1, 0):
            k = i * 2 + (2 - h)
            yield k, h, k - 1, 1 - h
    if (NU - 1) % 2:
        yield NU - 1, (NU - 1) % 2, NU - 2, (NU - 2) % 2
    yield None, 0, NU - 1, (NU - 1) % 2


def edge_network(nc, name, A, n, NU, N, ident, logits, edges):
    assert NU % 2 == 0
    with Stage(nc, name) as s:
        W1a = s.sb("W1a", [D + 1, D])
        W1b = s.sb("W1b", [EW, D])
        W2 = s.sb("W2", [D + 1, D])
        W2b = s.sb("W2b", [D + 1, D])
        g1 = s.sb("g1", [D, 1])
        be1 = s.sb("be1", [D, 1])
        b2 = s.sb("b2", [1, D])
        b2r = s.sb("b2r", [1, D])
        g2 = s.sb("g2", [P, D])
        be2 = s.sb("be2", [P, D])
        w3 = s.sb("w3", [P, D])
        gw = s.sb("gw", [P, D])
        bw = s.sb("bw", [P, D])
        b3 = s.sb("b3", [P, 1])
        c3 = s.sb("c3", [P, 1])
        eps = s.sb("eps", [P, 1])
        norm1 = Norm(s, "norm1", n, eps)
        norm2 = Norm(s, "norm2", n, eps)
        r1 = s.sb("r1", [P, n, D])
        r2 = s.sb("r2", [P, n, D])
        h1 = s.sb("h1", [P, 2, n, D])
        dot = s.sb("dot", [P, n])
        aT = s.sb("aT", [D + 1, 2, n * P])
        hT = s.sb("hT", [D + 1, 2, n * P])
        BANKS = ((0, 4), (4, n))
        psA = [s.ps(f"psA{k}", [D, 4 * P]) for k in range(2)]
        psH = [s.ps(f"psH{k}", [D, 4 * P]) for k in range(2)]
        ps1 = s.ps("ps1", [P, 8, D])
        ps2 = s.ps("ps2", [P, 8, D])
        rowsQ, src, dst, attr, qs, own = edges
        ra = s.sb("ra", [P, 2, n, ROW])
        rb = s.sb("rb", [P, 2, n, EW])
        bT = s.sb("bT", [EW, 2, n * P])
        islot0 = s.sb("islot0", [P, 2, n], I32)
        islot1 = s.sb("islot1", [P, 2, n], I32)
        psB = [s.ps(f"psB{k}", [EW, 4 * P]) for k in range(2)]
        (s_w, s_mem, s_w2, s_b2, s_dve, s_turn, s_pturn, s_idx0, s_idx1, s_kept, s_at, s_bt, s_ht, s_ac, s_hc,
         s_m1, s_m2, s_r1, s_r2, s_c1, s_c2, s_h1, s_v1, s_v2, s_d1, s_d2, s_log) = (s.sem(k) for k in (
             "w", "mem", "w2", "b2", "dve", "turn", "pturn", "idx0", "idx1", "kept", "at", "bt", "ht", "ac", "hc",
             "m1", "m2", "r1", "r2", "c1", "c2", "h1", "v1", "v2", "d1", "d2", "log"))
        s_ra = [s.sem("ra0"), s.sem("ra1")]
        s_rb = [s.sem("rb0"), s.sem("rb1")]
        block = s.ctx.enter_context(nc.Block())
        got = 16 * n
        n_w = 12
        copies = 4
        row = lambda v: v.rearrange("(a n) -> a n", a=1)

        @block.sync
        def _(sp):
            sp.wait_ge(s_mem, 2)
            w = A["L3_gnn_W1"]
            sp.dma_start(W1a[0:D, :], w[0:D, :]).then_inc(s_w, 16)
            sp.dma_start(W1b[0:D, :], w[D:2 * D, :]).then_inc(s_w, 16)
            sp.dma_start(W1b[D + 2:EW - 1, :], w[2 * D:2 * D + 8, :]).then_inc(s_w, 16)
            sp.dma_start(W1b[EW - 1:EW, :], row(A["L3_gnn_b1"])).then_inc(s_w, 16)
            sp.dma_start(W2[0:D, :], A["L3_gnn_W2"]).then_inc(s_w, 16)
            sp.dma_start(b2[:, :], row(A["L3_gnn_b2"])).then_inc(s_w, 16)
            sp.dma_start(g1[:, :], A["L3_gnn_g1"].rearrange("(n a) -> n a", a=1)).then_inc(s_w, 16)
            sp.dma_start(be1[:, :], A["L3_gnn_be1"].rearrange("(n a) -> n a", a=1)).then_inc(s_w, 16)
            spread_rows(sp, g2[:, :], A["L3_gnn_g2"], s_w)
            spread_rows(sp, be2[:, :], A["L3_gnn_be2"], s_w)
            spread_rows(sp, w3[:, :], A["L3_gnn_W3"].rearrange("n a -> (n a)"), s_w)
            spread_rows(sp, b3[:, :], A["L3_gnn_b3"], s_w)

        @block.gpsimd
        def _(pool):
            gather_chunks(nc, pool, NU, s_turn, [(rowsQ, N - 1, src, islot0, ra, s_ra, s_idx0),
                                                 (rowsQ, N - 1, dst, islot1, rb, s_rb, s_idx1)],
                          [(s_at, 2), (s_bt, 2), (s_kept, 2)], n)

        def rows_value(k, h):
            return (k - h) * (got // 2) + got

        @block.tensor
        def _(pe):
            pe.wait_ge(s_w, 16 * n_w)
            pe.wait_ge(s_mem, 5)
            nc.tensor.matmul(ps2[0:1, 0, :], be1[:, :], W2[0:D, :], start=True, stop=True).then_inc(s_b2, 1)
            pe.wait_ge(s_w2, 1)
            pe.sem_inc(s_at, 4)
            pe.sem_inc(s_bt, 4)
            for k, h, m, g in turns(pe, NU):
                if k is not None:
                    hold(pe, s_ra[h], rows_value(k, h), s_pturn)
                    hold(pe, s_rb[h], rows_value(k, h), s_pturn)
                    hold(pe, s_kept, k * 2 + 6, s_pturn)
                    for b, (t0, t1) in enumerate(BANKS):
                        hold(pe, s_ac, k * copies + (b + 1), s_pturn)
                        for t in range(t0, t1):
                            ins = nc.tensor.transpose(psA[b][:, (t - t0) * P:(t - t0 + 1) * P], ra[:, h, t, 0:D], ident[:, :])
                        ins.then_inc(s_at, 1)
                    for b, (t0, t1) in enumerate(BANKS):
                        hold(pe, s_ac, k * copies + (b + 3), s_pturn)
                        for t in range(t0, t1):
                            ins = nc.tensor.transpose(psB[b][:, (t - t0) * P:(t - t0 + 1) * P], rb[:, h, t, :], ident[:, :])
                        ins.then_inc(s_bt, 1)
                    hold(pe, s_ac, k * copies + 2 * copies, s_pturn)
                    hold(pe, s_r1, k + 1, s_pturn)
                    for t in range(n):
                        at = slice(t * P, (t + 1) * P)
                        nc.tensor.matmul(ps1[:, t, :], aT[0:D, h, at], W1a[0:D, :], start=True, stop=False)
                        ins = nc.tensor.matmul(ps1[:, t, :], bT[:, h, at], W1b[:, :], start=False, stop=True)
                    ins.then_inc(s_m1, 1)
                if m is not None:
                    hold(pe, s_h1, m + 1, s_pturn)
                    for b, (t0, t1) in enumerate(BANKS):
                        hold(pe, s_hc, m * 2 + (b + 1), s_pturn)
                        for t in range(t0, t1):
                            ins = nc.tensor.transpose(psH[b][:, (t - t0) * P:(t - t0 + 1) * P], h1[:, g, t, :], ident[:, :])
                        ins.then_inc(s_ht, 1)
                    hold(pe, s_hc, m * 2 + 4, s_pturn)
                    hold(pe, s_r2, m + 1, s_pturn)
                    for t in range(n):
                        ins = nc.tensor.matmul(ps2[:, t, :], hT[:, g, t * P:(t + 1) * P], W2b[:, :], start=True, stop=True)
                    ins.then_inc(s_m2, 1)

        @block.scalar
        def _(act):
            act.wait_ge(s_mem, 5)
            act.sem_inc(s_ac, copies)
            act.sem_inc(s_hc, 2)
            act.sem_inc(s_r1, 1)
            act.sem_inc(s_r2, 1)
            for k, h, m, g in turns(act, NU):
                if k is not None:
                    if not isinstance(k, int) or k > 1:
                        act.wait_ge(s_m1, k - 1)
                    for b, (t0, t1) in enumerate(BANKS):
                        act.wait_ge(s_at, k * 2 + (b + 5))
                        nc.scalar.activation(aT[0:D, h, t0 * P:t1 * P], psA[b][:, 0:(t1 - t0) * P], ACT.Copy).then_inc(s_ac, 1)
                    for b, (t0, t1) in enumerate(BANKS):
                        act.wait_ge(s_bt, k * 2 + (b + 5))
                        nc.scalar.activation(bT[:, h, t0 * P:t1 * P], psB[b][:, 0:(t1 - t0) * P], ACT.Copy).then_inc(s_ac, 1)
                    act.wait_ge(s_m1, k + 1)
                    act.wait_ge(s_c1, k)
                    nc.scalar.activation(r1[:, :, :], ps1[:, 0:n, :], ACT.Relu).then_inc(s_r1, 1)
                if m is not None:
                    for b, (t0, t1) in enumerate(BANKS):
                        act.wait_ge(s_ht, m * 2 + (b + 1))
                        nc.scalar.activation(hT[0:D, g, t0 * P:t1 * P], psH[b][:, 0:(t1 - t0) * P], ACT.Copy).then_inc(s_hc, 1)
                    act.wait_ge(s_m2, m + 1)
                    act.wait_ge(s_c2, m)
                    nc.scalar.activation(r2[:, :, :], ps2[:, 0:n, :], ACT.Relu).then_inc(s_r2, 1)
                if k is not None:
                    act.wait_ge(s_v1, k + 1)
                    norm1.root(nc, s_d1)
                if m is not None:
                    act.wait_ge(s_v2, m + 1)
                    norm2.root(nc, s_d2)

        @block.vector
        def _(dve):
            st = Steps(dve, s_dve)
            nc.vector.memset(W1b[:, :], 0.0).then_inc(s_mem, 1)
            nc.vector.memset(W1a[:, :], 0.0).then_inc(s_mem, 1)
            nc.vector.memset(eps[:, :], 1e-6).then_inc(s_mem, 1)
            nc.vector.memset(aT[D:D + 1, :, :], 1.0).then_inc(s_mem, 1)
            nc.vector.memset(hT[D:D + 1, :, :], 1.0).then_inc(s_mem, 1)
            dve.sem_inc(s_kept, 4)
            nc.vector.memset(rb[:, :, :, EW - 1], 1.0).then_inc(s_log, 1)
            dve.wait_ge(s_log, 1)
            dve.wait_ge(s_w, 16 * n_w)
            st.did(nc.vector.tensor_scalar(W2b[0:D, :], W2[0:D, :], g1[:, 0:1], None, ALU.mult))
            st.did(nc.vector.tensor_tensor(gw[:, :], g2[:, :], w3[:, :], ALU.mult))
            st.link(nc.vector.tensor_tensor(bw[:, :], be2[:, :], w3[:, :], ALU.mult))
            st.link(nc.vector.tensor_reduce(c3[:, :], bw[:, :], AX.X, ALU.add))
            st.link(nc.vector.tensor_tensor(c3[:, :], c3[:, :], b3[:, :], ALU.add))
            dve.wait_ge(s_b2, 1)
            st.link(nc.vector.tensor_tensor(b2r[:, :], b2[:, :], ps2[0:1, 0, :], ALU.add))
            st.link(nc.vector.tensor_copy(W2b[D:D + 1, :], b2r[:, :]))
            dve.sem_inc(s_w2, 1)
            n0 = st.n

            def keep(k, h):
                at = ds(k * n, n)
                dve.wait_ge(s_ra[h], rows_value(k, h))
                dve.wait_ge(s_rb[h], rows_value(k, h))
                nc.vector.tensor_copy(qs[:, at, :], ra[:, h, :, 0:D]).then_inc(s_kept, 1)
                nc.vector.tensor_copy(own[:, at], rb[:, h, :, D]).then_inc(s_log, 1)
                dve.wait_ge(s_log, k + 2)
                nc.vector.tensor_copy(rb[:, h, :, D + 2:EW - 1], attr[:, at, :]).then_inc(s_kept, 1)

            keep(0, 0)
            A_N, B_N = 5, 7
            for k, h, m, g in turns(dve, NU):
                if k is not None and m is not None:
                    sl = Steps(dve, s_dve, A_N + B_N, m, n0 + A_N)
                elif k is not None:
                    sl = Steps(dve, s_dve, 0, 0, n0)
                else:
                    sl = Steps(dve, s_dve, A_N + B_N, m, n0 + A_N)
                if k is not None:
                    dve.wait_ge(s_r1, k + 2)
                    sl.link(nc.vector.tensor_reduce(norm1.sum[:, :], r1[:, :, :], AX.X, ALU.add))
                    sl.link(nc.vector.tensor_scalar(norm1.mean[:, :], norm1.sum[:, :], 1.0 / D, None, ALU.mult))
                    nc.vector.tensor_tensor(norm1.xc[:, :, :], r1[:, :, :], bcast(norm1.mean[:, :], 2, D), ALU.subtract).then_inc(s_c1, 1)
                    dve.wait_ge(s_c1, k + 1)
                    sl.link(nc.vector.tensor_tensor(norm1.sq[:, :, :], norm1.xc[:, :, :], norm1.xc[:, :, :], ALU.mult))
                    sl.did(nc.vector.tensor_reduce(norm1.var[:, :], norm1.sq[:, :, :], AX.X, ALU.add))
                    sl.wait()
                    dve.sem_inc(s_v1, 1)
                    if not isinstance(k, int) or k + 1 < NU:
                        keep(k + 1, 1 - h)
                if m is not None:
                    dve.wait_ge(s_r2, m + 2)
                    sl.link(nc.vector.tensor_reduce(norm2.sum[:, :], r2[:, :, :], AX.X, ALU.add))
                    sl.link(nc.vector.tensor_scalar(norm2.mean[:, :], norm2.sum[:, :], 1.0 / D, None, ALU.mult))
                    nc.vector.tensor_tensor(norm2.xc[:, :, :], r2[:, :, :], bcast(norm2.mean[:, :], 2, D), ALU.subtract).then_inc(s_c2, 1)
                    dve.wait_ge(s_c2, m + 1)
                    sl.link(nc.vector.tensor_tensor(norm2.sq[:, :, :], norm2.xc[:, :, :], norm2.xc[:, :, :], ALU.mult))
                    nc.vector.tensor_reduce(norm2.var[:, :], norm2.sq[:, :, :], AX.X, ALU.add).then_inc(s_v2, 1)
                if k is not None:
                    dve.wait_ge(s_d1, k + 1)
                    sl.link(nc.vector.reciprocal(norm1.rstd[:, :], norm1.std[:, :]))
                    if not isinstance(k, int) or k > 1:
                        dve.wait_ge(s_ht, k * 2 - 2)
                    nc.vector.tensor_tensor(h1[:, h, :, :], norm1.xc[:, :, :], bcast(norm1.rstd[:, :], 2, D), ALU.mult).then_inc(s_h1, 1)
                if m is not None:
                    dve.wait_ge(s_v2, m + 1)
                    sl.link(nc.vector.tensor_tensor(norm2.sq[:, :, :], norm2.xc[:, :, :], bcast(gw[:, :], 1, n), ALU.mult))
                    sl.did(nc.vector.tensor_reduce(dot[:, :], norm2.sq[:, :, :], AX.X, ALU.add))
                    dve.wait_ge(s_d2, m + 1)
                    sl.link(nc.vector.reciprocal(norm2.rstd[:, :], norm2.std[:, :]))
                    sl.link(nc.vector.tensor_tensor(dot[:, :], dot[:, :], norm2.rstd[:, :], ALU.mult))
                    nc.vector.tensor_scalar(logits[:, ds(m * n, n)], dot[:, :], c3[:, 0:1], 0.0, ALU.add, ALU.max).then_inc(s_turn, 1)


def last_norm(nc, name, A, logits):
    n = logits.shape[1]
    with Stage(nc, name) as s:
        g3 = s.sb("g3", [P, 1])
        be3 = s.sb("be3", [P, 1])
        mean = s.sb("mean", [P, n])
        xc = s.sb("xc", [P, n])
        var = s.sb("var", [P, n])
        eps = s.sb("eps", [P, 1])
        s_w, s_dve, s_std = s.sem("w"), s.sem("dve"), s.sem("std")
        block = s.ctx.enter_context(nc.Block())

        @block.sync
        def _(sp):
            spread_rows(sp, g3[:, :], A["L3_gnn_g3"], s_w)
            spread_rows(sp, be3[:, :], A["L3_gnn_be3"], s_w)

        @block.scalar
        def _(act):
            act.wait_ge(s_dve, 4)
            nc.scalar.activation(var[:, :], var[:, :], ACT.Sqrt, bias=eps[:, :], scale=1.0).then_inc(s_std, 1)

        @block.vector
        def _(dve):
            st = Steps(dve, s_dve)
            st.did(nc.vector.memset(eps[:, :], 1e-6))
            st.link(nc.vector.tensor_scalar(mean[:, :], logits, 1.0, None, ALU.mult))
            st.link(nc.vector.tensor_tensor(xc[:, :], logits, mean[:, :], ALU.subtract))
            st.link(nc.vector.tensor_tensor(var[:, :], xc[:, :], xc[:, :], ALU.mult))
            dve.wait_ge(s_std, 1)
            dve.wait_ge(s_w, 32)
            st.link(nc.vector.reciprocal(var[:, :], var[:, :]))
            st.link(nc.vector.tensor_tensor(xc[:, :], xc[:, :], var[:, :], ALU.mult))
            st.link(nc.vector.tensor_scalar(logits, xc[:, :], g3[:, 0:1], be3[:, 0:1], ALU.mult, ALU.add))


def scatter_attention(nc, T, N, tab, carry, state, zsum, top, byD):
    C = T // G
    with Stage(nc, "scatt") as s:
        rslot = s.sb("rslot", [P, 2, G, ROW])
        islot = s.sb("islot", [P, 2, G], I32)
        s_dve, s_ready, s_turn = s.sem("dve"), s.sem("ready"), s.sem("turn")
        s_out = [s.sem("out0"), s.sem("out1")]
        block = s.ctx.enter_context(nc.Block())

        @block.gpsimd
        def _(pool):
            scatter_chunks(nc, pool, C, s_turn, s_ready, byD, N - 1, islot, rslot, s_out)

        @block.vector
        def _(dve):
            for i in turns_from_zero(dve, C // 2):
                for h in range(2):
                    j = i * 2 + h
                    at = ds(j * G, G)
                    sl = Steps(dve, s_dve, G + 3, j)
                    dve.wait_ge(s_out[h], i * (16 * G))
                    finish_sums(nc, sl, j, tab, carry, state, rslot[:, h, :, 0:D])
                    sl.did(nc.vector.tensor_copy(rslot[:, h, :, D], zsum[:, at]))
                    sl.did(nc.vector.tensor_copy(rslot[:, h, :, D + 1], top[:, at]))
                    sl.link(nc.vector.tensor_copy(islot[:, h, :], tab["endrow"][:, at]))
                    dve.sem_inc(s_ready, 1)


def load_attributes(nc, A, E, T, attr):
    full, rest = E // T, E - E // T * T
    with Stage(nc, "attr") as s:
        s_mem, s_in = s.sem("mem"), s.sem("in")
        block = s.ctx.enter_context(nc.Block())

        @block.vector
        def _(dve):
            nc.vector.memset(attr[:, :, :], 0.0).then_inc(s_mem, 1)

        @block.sync
        def _(sp):
            sp.wait_ge(s_mem, 1)
            v = A["edge_attr_8"]
            sp.dma_start(attr[0:full, :, :], v[0:full * T, :].rearrange("(p t) f -> p t f", t=T)).then_inc(s_in, 16)
            if rest:
                sp.dma_start(attr[full:full + 1, 0:rest, :],
                             v[full * T:E, :].rearrange("(p t) f -> p t f", p=1)).then_inc(s_in, 16)
            sp.wait_ge(s_in, 32 if rest else 16)


TAB = ("keep", "keepback", "neg", "negback", "pre", "post", "negpre", "negpost", "count", "pos1")


def tables(nc, ctx, name, T):
    tab = {k: ctx.enter_context(nc.sbuf_tensor(f"{name}_{k}", [P, T], F32)) for k in TAB}
    for k in ("keyi", "src", "endrow"):
        tab[k] = ctx.enter_context(nc.sbuf_tensor(f"{name}_{k}", [P, T], I32))
    tab["ccount"] = ctx.enter_context(nc.sbuf_tensor(f"{name}_ccount", [P, 1], F32))
    return tab


def build(nc, A, out, N, E, T):
    RETIRED.clear()
    NC = -(-N // (P * U))
    NP = NC * P * U
    dram = lambda name, shape, dt=F32: nc.dram_tensor(name, shape, dt).ap()
    sorted1 = dram("sorted1", (P * T, 4), I32)
    sorted2 = dram("sorted2", (P * T, 4), I32)
    byD = dram("byD", (NP, ROW))
    byS = dram("byS", (NP, D))
    places = dram("places", (NP, 1))
    H = dram("H", (NP, ROW))
    with ExitStack() as ctx:
        sb = lambda name, shape, dt=F32: ctx.enter_context(nc.sbuf_tensor(name, shape, dt))
        ident = sb("ident", [P, P])
        upper = sb("upper", [P, P])
        ones = sb("ones", [P, P])
        rows0 = sb("rows0", [P, T, 4], I32)
        countN = sb("countN", [P, NC * U])
        tabD = tables(nc, ctx, "tabD", T)
        ptrD = sb("ptrD", [P, T], I32)
        setup(nc, A, N, E, T, tabD, ident, upper, ones, rows0)
        segment_tables(nc, "segD", tabD["keyi"][:, :], T, ident, tabD)
        sort_pass(nc, "sort0", lambda sp, rows, sem: sp.dma_start(rows[:, :, :], rows0[:, :, :]).then_inc(sem, 16), 0, sorted1, T, ones, upper, 16, [byD, byS, places])
        sort_pass(nc, "sort1", lambda sp, rows, sem: sp.dma_start(rows[:, :, :], sorted1.rearrange("(p t) f -> p t f", t=T)).then_inc(sem, 16), 1, sorted2, T, ones, upper, 16)
        relations = dram("relations", (A["L1_gnn_relation_embed"].shape[0], 4))
        tabS = tables(nc, ctx, "tabS", T)
        dstS = sb("dstS", [P, T], I32)
        typS = sb("typS", [P, T], I32)
        ptrS = sb("ptrS", [P, T], I32)
        ptrN = sb("ptrN", [P, NC * U])
        srel = sb("srel", [P, T, 4])
        sorted_edges(nc, sorted2, T, N, tabS["keyi"][:, :], tabS["src"][:, :], dstS[:, :], typS[:, :])
        segment_tables(nc, "segS", tabS["keyi"][:, :], T, ident, tabS)
        relation_scores(nc, A, ones, relations)
        with ExitStack() as c0:
            basisT = c0.enter_context(nc.sbuf_tensor("basisT", [3 * KK, (T + 1) * P], BF16))
            agg = c0.enter_context(nc.sbuf_tensor("aggmax", [P, T + 1, D], F32))
            carry = c0.enter_context(nc.sbuf_tensor("carry", [P, D], F32))
            basis_tables(nc, A, E, T, basisT, ident)
            for layer in range(2):
                table, width = ((A["x"], D), (H, ROW))[layer]
                spline_messages(nc, f"spline{layer}", A[f"L0_gnn_W{layer + 1}"], table, width, N, T, tabD,
                                basisT, ident, agg, ptrD if layer else None,
                                **({"relations": (relations, typS, srel)} if layer else {"places": (tabS, places, ptrN[:, :])}))
                carry_over(nc, f"scarry{layer}", agg[:, T, :], tabD["negpre"][:, T - 1:T], ident, D, "max", carry[:, :])
                scatter_ends(nc, f"sends{layer}", T, tabD, carry, agg, "max", byD, N)
                if layer == 0:
                    hidden(nc, A, byD, H, N, NC, ident, countN)
        x1 = dram("x1", (NP, D))
        HH = dram("HH", (NP, ROW))
        ent = dram("ent", (NP, D))
        HH1 = dram("HH1", (NP, ROW))
        x2 = dram("x2", (NP, D))
        x2d = dram("x2d", (NP, D))
        EG = dram("EG", (P * T + 1, 2 * D))

        def hidden_tail(st, t, v, c):
            out = t["hh"]
            st.link(nc.gpsimd.tensor_tensor(out[:, :, 0:D], out[:, :, 0:D], bcast(v["g"][:, :], 1, U), ALU.mult))
            st.link(nc.gpsimd.tensor_tensor(out[:, :, 0:D], out[:, :, 0:D], bcast(v["b"][:, :], 1, U), ALU.add))
            st.did(nc.gpsimd.tensor_copy(out[:, :, D], ptrN[:, ds(c * U, U)]))
            st.did(nc.gpsimd.tensor_copy(out[:, :, D + 1], ptrN[:, ds(c * U, U)]))

        def first_body(w, t, v, c):
            tmp = w.tmp[:, :, :]
            yield nc.vector.tensor_tensor(tmp, w.product, t["agg"][:, :, 0:D], ALU.add)
            yield nc.vector.tensor_tensor(tmp, tmp, t["x"], ALU.add)
            yield from w.layer_norm(tmp, t["x1"])
            yield from w.layer_norm(t["x1"], t["hh"][:, :, 0:D])

        node_stage(nc, "nfirst", N, NC, ident, {"x": (A["x"], D), "agg": (byD, ROW), "h": (H, ROW)},
                   {"x1": (x1, D), "hh": (HH, ROW)},
                   {"g": A["L1_gnn_ln_gamma"][0], "b": A["L1_gnn_ln_beta"][0]},
                   ("h", [A["L0_gnn_root2"]], A["L0_gnn_bias2"], None), ["root", "root"], first_body, 14, hidden_tail, 4)
        for layer in range(2):
            table = (HH, HH1)[layer]
            with ExitStack() as c1:
                sb1 = lambda name, shape, dt=F32: c1.enter_context(nc.sbuf_tensor(f"{name}_{layer}", shape, dt))
                score = sb1("score", [P, T, 2])
                rz = sb1("rz", [P, T, 2])
                carry = sb1("carry1", [P, 2 * D])
                hdst = sb1("hdst", [P, T, D])
                attention_scores(nc, f"att{layer}", A, layer, T, N, table, tabS["src"], dstS, ident, srel, score, hdst, ptrS)
                segment_softmax(nc, f"soft{layer}", T, tabS, ident, score, score, rz, 0.85)
                with ExitStack() as c2:
                    state = c2.enter_context(nc.sbuf_tensor(f"state_{layer}", [P, T + 1, 2 * D], F32))
                    for step in range(3):
                        attention_step(nc, f"step{layer}{step}", T, tabS, step == 0, EG, ptrS, hdst, score, state)
                        carry_over(nc, f"stepc{layer}{step}", state[:, T, :], tabS["pre"][:, T - 1:T], ident, 2 * D, "sum", carry[:, :])
                        if step < 2:
                            attention_share(nc, f"share{layer}{step}", T, tabS, carry, state, rz, EG)
                        else:
                            attention_output(nc, f"wo{layer}", A, layer, T, N, tabS, carry, state, rz, ident, byS)

            def ent_body(w, t, v, c):
                tmp = w.tmp[:, :, :]
                yield nc.vector.scalar_tensor_tensor(tmp, w.product, 0.15, t["agg"], ALU.mult, ALU.add)
                yield nc.vector.tensor_tensor(t["ent"], tmp, t["x"], ALU.add)
                yield from w.layer_norm(t["ent"], t["hh"][:, :, 0:D])

            def last_body(w, t, v, c):
                tmp = w.tmp[:, :, :]
                yield nc.vector.scalar_tensor_tensor(tmp, w.product, 0.15, t["agg"], ALU.mult, ALU.add)
                yield nc.vector.tensor_tensor(tmp, tmp, t["x"], ALU.add)
                yield nc.vector.tensor_tensor(tmp, tmp, t["x1"], ALU.add)
                yield from w.layer_norm(tmp, t["x2"])

            def last_tail(st, t, v, c):
                st.did(nc.gpsimd.tensor_tensor(t["x2d"], t["x2"], bcast(dN[:, ds(c * U, U)], 2, D), ALU.mult))

            W_o = A["L1_gnn_W_o"][layer]
            halves = ("h", [W_o[0:D, :], W_o[D:2 * D, :]], None, None)
            if layer == 0:
                node_stage(nc, "nent", N, NC, ident, {"x": (x1, D), "agg": (byS, D), "h": (HH, ROW)},
                           {"ent": (ent, D), "hh": (HH1, ROW)},
                           {"g": A["L1_gnn_ln_gamma"][1], "b": A["L1_gnn_ln_beta"][1]},
                           halves, ["root"], ent_body, 8, hidden_tail, 4)
            else:
                dN = sb("dN", [P, NC * U])
                rdegD = sb("rdegD", [P, T])
                dD = sb("dD", [P, T])
                degree_factors(nc, T, NC, tabD["count"], countN, rdegD, dD, dN)
                node_stage(nc, "nlast", N, NC, ident,
                           {"x": (ent, D), "agg": (byS, D), "h": (HH1, ROW), "x1": (x1, D)},
                           {"x2": (x2, D), "x2d": (x2d, D)}, {}, halves, ["root"], last_body, 9, last_tail, 1)
        EG2 = dram("EG2", (P * T + 1, D))
        x3 = dram("x3", (NP, D))
        q0 = dram("q0", (NP, D))
        h1 = dram("h1", (NP, D))
        Q = dram("Q", (NP, ROW))
        with ExitStack() as c3:
            sb3 = lambda name, shape, dt=F32: c3.enter_context(nc.sbuf_tensor(name, shape, dt))
            state = sb3("stateD", [P, T + 1, D])
            acc = sb3("accD", [P, T, D])
            carry = sb3("carryD", [P, D])
            for step in range(3):
                if step == 0:
                    running_sums(nc, "deg0", T, tabD, x2d, N - 1, tabD["src"], state)
                else:
                    running_sums(nc, f"deg{step}", T, tabD, EG2, P * T, ptrD, state)
                carry_over(nc, f"degc{step}", state[:, T, :], tabD["pre"][:, T - 1:T], ident, D, "sum", carry[:, :])
                degree_share(nc, f"degs{step}", T, tabD, carry, state, rdegD, dD, acc, step == 0, EG2,
                             byD if step == 2 else None, N)

        def q_body(w, t, v, c):
            tmp = w.tmp[:, :, :]
            yield nc.vector.tensor_tensor(tmp, t["x"], t["agg"][:, :, 0:D], ALU.add)
            yield nc.vector.scalar_tensor_tensor(tmp, tmp, 0.25, t["x"], ALU.mult, ALU.add)
            yield from w.layer_norm(tmp, t["x3"])

        node_stage(nc, "nq", N, NC, ident, {"x": (x2, D), "agg": (byD, ROW)}, {"x3": (x3, D), "q": (q0, D)}, {},
                   ("x3", [A["L3_gnn_W_q"]], A["L3_gnn_b_q"], "q"), ["root"], q_body, 8)
        lN = sb("lN", [P, NC * U])
        c3 = sb("c3", [P, 1])

        def net1_body(w, t, v, c):
            yield nc.vector.tensor_scalar(w.tmp[:, :, :], w.product, 0.0, None, ALU.max)
            yield from w.layer_norm(w.tmp[:, :, :], t["h1"])

        def net1_tail(st, t, v, c):
            st.link(nc.gpsimd.tensor_tensor(t["h1"], t["h1"], bcast(v["g"][:, :], 1, U), ALU.mult))
            st.link(nc.gpsimd.tensor_tensor(t["h1"], t["h1"], bcast(v["b"][:, :], 1, U), ALU.add))

        def net2_prepare(st, v):
            st.link(nc.vector.tensor_tensor(v["g"][:, :], v["g"][:, :], v["w3"][:, :], ALU.mult))
            st.link(nc.vector.tensor_tensor(v["b"][:, :], v["b"][:, :], v["w3"][:, :], ALU.mult))
            st.link(nc.vector.tensor_reduce(c3[:, :], v["b"][:, :], AX.X, ALU.add))
            st.link(nc.vector.tensor_tensor(c3[:, :], c3[:, :], v["b3"][:, :], ALU.add))

        def net2_body(w, t, v, c):
            tmp, n, own = w.tmp[:, :, :], w.norm, lN[:, ds(c * U, U)]
            yield nc.vector.tensor_scalar(tmp, w.product, 0.0, None, ALU.max)
            yield nc.vector.tensor_reduce(n.sum[:, :], tmp, AX.X, ALU.add)
            yield nc.vector.tensor_scalar(n.mean[:, :], n.sum[:, :], 1.0 / D, None, ALU.mult)
            yield nc.vector.tensor_tensor(n.xc[:, :, :], tmp, bcast(n.mean[:, :], 2, D), ALU.subtract)
            yield nc.vector.tensor_tensor(n.sq[:, :, :], n.xc[:, :, :], n.xc[:, :, :], ALU.mult)
            w.ask(nc.vector.tensor_reduce(n.var[:, :], n.sq[:, :, :], AX.X, ALU.add))
            yield nc.vector.tensor_tensor(tmp, n.xc[:, :, :], bcast(v["g"][:, :], 1, U), ALU.mult)
            yield nc.vector.tensor_reduce(n.sum[:, :], tmp, AX.X, ALU.add)
            w.answer()
            yield nc.vector.reciprocal(n.rstd[:, :], n.std[:, :])
            yield nc.vector.tensor_tensor(n.sum[:, :], n.sum[:, :], n.rstd[:, :], ALU.mult)
            yield nc.vector.tensor_scalar(n.sum[:, :], n.sum[:, :], c3[:, 0:1], 0.0, ALU.add, ALU.max)
            yield nc.vector.tensor_scalar(n.mean[:, :], n.sum[:, :], 1.0, None, ALU.mult)
            yield nc.vector.tensor_tensor(n.sum[:, :], n.sum[:, :], n.mean[:, :], ALU.subtract)
            yield from w.asked(nc.vector.tensor_tensor(w.small_in[:, :], n.sum[:, :], n.sum[:, :], ALU.mult))
            yield nc.vector.reciprocal(n.rstd[:, :], w.small_out[:, :])
            yield nc.vector.tensor_tensor(n.sum[:, :], n.sum[:, :], n.rstd[:, :], ALU.mult)
            yield nc.vector.tensor_scalar(own, n.sum[:, :], v["g3"][:, 0:1], v["be3"][:, 0:1], ALU.mult, ALU.add)

        def net2_tail(st, t, v, c):
            st.did(nc.gpsimd.tensor_copy(t["row"][:, :, 0:D], t["q"]))
            st.did(nc.gpsimd.tensor_copy(t["row"][:, :, D], lN[:, ds(c * U, U)]))
            st.did(nc.gpsimd.tensor_copy(t["row"][:, :, D + 1], lN[:, ds(c * U, U)]))

        W1 = A["L3_gnn_W1"]
        node_stage(nc, "net1", N, NC, ident, {"q": (q0, D)}, {"h1": (h1, D)}, {"g": A["L3_gnn_g1"], "b": A["L3_gnn_be1"]},
                   ("q", [W1[0:D, :], W1[D:2 * D, :]], A["L3_gnn_b1"], None), ["root"], net1_body, 7, net1_tail, 2, 1e-6)
        node_stage(nc, "net2", N, NC, ident, {"h1": (h1, D), "q": (q0, D)}, {"row": (Q, ROW)},
                   {"g": A["L3_gnn_g2"], "b": A["L3_gnn_be2"], "w3": A["L3_gnn_W3"].rearrange("n a -> (n a)"),
                    "b3": A["L3_gnn_b3"], "g3": A["L3_gnn_g3"], "be3": A["L3_gnn_be3"]},
                   ("h1", [A["L3_gnn_W2"]], A["L3_gnn_b2"], None), ["root", "small root"], net2_body, 15,
                   net2_tail, 3, 1e-6, net2_prepare)
        with ExitStack() as c4:
            sb4 = lambda name, shape, dt=F32: c4.enter_context(nc.sbuf_tensor(name, shape, dt))
            attr = sb4("attr8", [P, T, 8])
            qs = sb4("qs", [P, T, D])
            own = sb4("own", [P, T])
            lE = sb4("lE", [P, T])
            dstD = sb4("dstD", [P, T], I32)
            zsum = sb4("zsum", [P, T])
            carry = sb4("carryQ", [P, D])
            load_attributes(nc, A, E, T, attr)
            with Stage(nc, "dstD") as s:
                s_dve = s.sem("dve")
                block = s.ctx.enter_context(nc.Block())

                @block.vector
                def _(dve):
                    nc.vector.tensor_scalar(dstD[:, :], tabD["keyi"][:, :], float(N - 1), None, ALU.min).then_inc(s_dve, 1)
            edge_network(nc, "nete", A, G // 2, 2 * (T // G), N, ident, lE,
                         (Q, tabD["src"], dstD, attr, qs, own))
            last_norm(nc, "lne", A, lE[:, :])
            one = lambda x: x[:, :].rearrange("p (t a) -> p t a", a=1)
            segment_softmax(nc, "softQ", T, tabD, ident, one(lE), one(lE), one(zsum), None, 1, one(own))
            state = sb4("stateQ", [P, T + 1, D])
            running_sums(nc, "sumQ", T, tabD, None, None, None, state, lE, qs)
            carry_over(nc, "carQ", state[:, T, :], tabD["pre"][:, T - 1:T], ident, D, "sum", carry[:, :])
            scatter_attention(nc, T, N, tabD, carry, state, zsum, own, byD)

        def out_body(w, t, v, c):
            z, top = t["agg"][:, :, D], t["agg"][:, :, D + 1]
            own = lN[:, ds(c * U, U)]
            tmp, less, more = w.tmp[:, :, :], w.small_in[:, :], w.small_out[:, :]
            yield nc.vector.tensor_scalar(more, countN[:, ds(c * U, U)], 0.0, None, ALU.is_gt)
            yield nc.vector.tensor_tensor(less, own, top, ALU.subtract)
            yield from w.asked(nc.vector.tensor_tensor(less, less, more, ALU.mult))
            yield nc.vector.tensor_tensor(less, more, z, ALU.add)
            yield nc.vector.reciprocal(less, less)
            yield nc.vector.tensor_tensor(tmp, t["q"], bcast(more, 2, D), ALU.mult)
            yield nc.vector.tensor_tensor(tmp, tmp, t["agg"][:, :, 0:D], ALU.add)
            yield nc.vector.tensor_tensor(tmp, tmp, bcast(less, 2, D), ALU.mult)
            yield nc.vector.scalar_tensor_tensor(tmp, tmp, 0.01, tmp, ALU.mult, ALU.max)
            yield nc.vector.tensor_tensor(tmp, tmp, t["x3"], ALU.add)
            yield from w.layer_norm(tmp, t["out"])

        node_stage(nc, "nout", N, NC, ident, {"x3": (x3, D), "q": (q0, D), "agg": (byD, ROW)}, {"out": (out, D)}, {},
                   None, ["exp", "root"], out_body, 15)


_OUTS = [((50000, 64), "float32")]


def kernel(**inputs):
    import numpy as np
    import concourse.bacc as bacc
    from concourse.bass_utils import run_bass_kernel_spmd

    nc = bacc.Bacc("TRN2", target_bir_lowering=False, num_devices=1)
    arrays, A = {}, {}
    for name, value in inputs.items():
        a = np.ascontiguousarray(value)
        arrays[f"in_{name}"] = a
        A[name] = nc.dram_tensor(f"in_{name}", a.shape, mybir.dt.from_np(a.dtype), kind="ExternalInput").ap()
    N, E = A["x"].shape[0], A["src"].shape[0]
    tiles = -(-E // P)
    T = -(-tiles // (2 * G)) * 2 * G
    out = nc.dram_tensor("out_0", (N, D), F32, kind="ExternalOutput").ap()
    build(nc, A, out, N, E, T)
    r = run_bass_kernel_spmd(nc, [arrays], core_ids=[0])
    return r.results[0]["out_0"]
```
